# Optimizing a Trainium2 kernel written in Bass

```python
import numpy as np
import jax
import jax.numpy as jnp

def _softmax(x, axis=-1):
    return jax.nn.softmax(x, axis=axis)

def _gelu(x):
    return jax.nn.gelu(x, approximate=True)

def _silu(x):
    return jax.nn.silu(x)

def _sigmoid(x):
    return jax.nn.sigmoid(x)

def _layernorm(x, axis=-1, eps=1e-05):
    m = jnp.mean(x, axis=axis, keepdims=True)
    v = jnp.var(x, axis=axis, keepdims=True)
    return (x - m) / jnp.sqrt(v + eps)

def _scatter_add(tgt, idx, src, axis=0):
    return tgt.at[idx].add(src)

def _segment_sum(src, seg, n):
    return jax.ops.segment_sum(src, seg, n)
kernel_name = 'mk_macaron_d1_jaxref_r8_39ad1c'

def setup_inputs(seed: int=0):
    np.random.seed(seed)
    _w = jnp.asarray

    def _L0_attn_setup():
        import jax, jax.numpy as jnp
        import numpy as np
        from jax.scipy.linalg import solve_triangular
        B, L, HID, NH = (2, 128, 128, 4)
        DK = DV = 32
        CONV_K, CHUNK, FIR_S_K, FIR_L_K = (4, 32, 3, 31)
        GATE_IN = HID + 3 * DV * 4 + DV * 4
        GATE_H = 2 * DV

        def _l2norm(x):
            return x * jax.lax.rsqrt(jnp.sum(x * x, -1, keepdims=True) + 1e-06)

        def _short_conv(x, w):
            c, k = w.shape
            y = jax.lax.conv_general_dilated(x.transpose(0, 2, 1), w[:, None, :], (1,), [(k - 1, 0)], feature_group_count=c)
            return jax.nn.silu(y.transpose(0, 2, 1))

        def _fir(x, f):
            b, l, h, d = x.shape
            k = f.shape[-1]
            xf = x.transpose(0, 2, 3, 1).reshape(b, h * d, l)
            y = jax.lax.conv_general_dilated(xf, f.reshape(h * d, 1, k), (1,), [(k - 1, 0)], feature_group_count=h * d)
            return y.reshape(b, h, d, l).transpose(0, 3, 1, 2)

        def _delta_rule(q, k, v, beta, chunk=CHUNK):
            b, h, l, dk = q.shape
            dv = v.shape[-1]
            n = l // chunk
            q = _l2norm(q)
            k = _l2norm(k)
            v = v * beta[..., None]
            kb = k * beta[..., None]
            rs = lambda t: t.reshape(b, h, n, chunk, -1)
            q, k, v, kb = map(rs, (q, k, v, kb))
            A = -jnp.tril(jnp.einsum('bhncd,bhned->bhnce', kb, k), -1)
            eye = jnp.eye(chunk, dtype=q.dtype)
            T = solve_triangular(eye - A, jnp.broadcast_to(eye, A.shape), lower=True)
            u = T @ v
            w = T @ kb
            mov = lambda t: jnp.moveaxis(t, 2, 0)

            def step(S, inp):
                qi, ki, ui, wi = inp
                attn = jnp.tril(qi @ ki.transpose(0, 1, 3, 2))
                u_i = ui - wi @ S
                o_i = qi @ S + attn @ u_i
                return (S + ki.transpose(0, 1, 3, 2) @ u_i, o_i)
            S0 = jnp.zeros((b, h, dk, dv), dtype=q.dtype)
            S, o = jax.lax.scan(step, S0, (mov(q), mov(k), mov(u), mov(w)))
            o = jnp.moveaxis(o, 0, 2).reshape(b, h, l, dv)
            return (o, S)

        def _gate(hidden, branches, W1, b1, W2, b2, temp, eps_floor):

            def stats(p):
                m = p.mean(-1, keepdims=True)
                r = jnp.sqrt(jnp.clip((p * p).mean(-1, keepdims=True), 1e-08))
                mx = p.max(-1, keepdims=True)
                return jnp.concatenate([jnp.broadcast_to(m, p.shape), jnp.broadcast_to(r, p.shape), jnp.broadcast_to(mx, p.shape)], -1)
            b, l, h, d = branches[0].shape
            hb = jnp.broadcast_to(hidden[:, :, None, :], (b, l, h, hidden.shape[-1]))
            head_in = jnp.concatenate([hb] + [stats(p) for p in branches] + list(branches), -1)
            hmid = jax.nn.gelu(head_in @ W1 + b1, approximate=False)
            logits = hmid @ W2 + b2
            t = jnp.clip(temp, 0.2, 10.0)[None, None, :, None]
            w = jax.nn.softmax(logits / t, -1)
            floor = jnp.clip(eps_floor, 1e-07, 0.1)[None, None]
            w = jnp.maximum(w, floor)
            return w / w.sum(-1, keepdims=True)
        key = jax.random.key(seed)
        ks = jax.random.split(key, 16)
        s = 0.02
        inp = {'x': jax.random.normal(ks[0], (B, L, HID), jnp.float32), 'Wq': jax.random.normal(ks[1], (HID, NH * DK), jnp.float32) * s, 'Wk': jax.random.normal(ks[2], (HID, NH * DK), jnp.float32) * s, 'Wv': jax.random.normal(ks[3], (HID, NH * DV), jnp.float32) * s, 'Wb': jax.random.normal(ks[4], (HID, NH), jnp.float32) * s, 'qc_w': jax.random.normal(ks[5], (NH * DK, CONV_K), jnp.float32) * 0.5, 'kc_w': jax.random.normal(ks[6], (NH * DK, CONV_K), jnp.float32) * 0.5, 'vc_w': jax.random.normal(ks[7], (NH * DV, CONV_K), jnp.float32) * 0.5, 'gW1': jax.random.normal(ks[10], (GATE_IN, GATE_H), jnp.float32) * s, 'gb1': jnp.zeros((GATE_H,), jnp.float32), 'gW2': jax.random.normal(ks[11], (GATE_H, 4), jnp.float32) * s, 'gb2': jnp.zeros((4,), jnp.float32), 'temp': jnp.ones((NH,), jnp.float32), 'eps_floor': jnp.full((NH, 4), 0.01, jnp.float32), 'onorm_w': jnp.ones((DV,), jnp.float32), 'Wo': jax.random.normal(ks[12], (NH * DV, HID), jnp.float32) * s}
        fs = jnp.zeros((NH, DV, FIR_S_K)).at[..., -1].set(1.0)
        fl = jnp.zeros((NH, DV, FIR_L_K)).at[..., -1].set(1.0)
        inp['fir_s'] = fs + s * jax.random.normal(ks[8], fs.shape, jnp.float32)
        inp['fir_l'] = fl + s * jax.random.normal(ks[9], fl.shape, jnp.float32)
        return inp
    _L0_attn_in = _L0_attn_setup()

    def _L0_ffn_setup():
        import jax, jax.numpy as jnp
        import numpy as np
        D = 128
        N_EXP = 8
        TOP_K = 1
        key = jax.random.key(seed)
        ks = jax.random.split(key, 7)
        s = 0.02
        return {'x': jax.random.normal(ks[0], (4, 256, D), jnp.float32), 'gate_w': jax.random.normal(ks[1], (D, N_EXP), jnp.float32) * s, 'gate_b': jnp.zeros((N_EXP,), jnp.float32), 'w1': jax.random.normal(ks[2], (N_EXP, D, 4 * D), jnp.float32) * s, 'b1': jnp.zeros((N_EXP, 4 * D), jnp.float32), 'w2': jax.random.normal(ks[3], (N_EXP, 4 * D, D), jnp.float32) * s, 'b2': jnp.zeros((N_EXP, D), jnp.float32)}
    _L0_ffn_in = _L0_ffn_setup()
    _d = {'L0_attn_x': _L0_attn_in['x'], 'L0_attn_Wq': _L0_attn_in['Wq'], 'L0_attn_Wk': _L0_attn_in['Wk'], 'L0_attn_Wv': _L0_attn_in['Wv'], 'L0_attn_Wb': _L0_attn_in['Wb'], 'L0_attn_qc_w': _L0_attn_in['qc_w'], 'L0_attn_kc_w': _L0_attn_in['kc_w'], 'L0_attn_vc_w': _L0_attn_in['vc_w'], 'L0_attn_fir_s': _L0_attn_in['fir_s'], 'L0_attn_fir_l': _L0_attn_in['fir_l'], 'L0_attn_gW1': _L0_attn_in['gW1'], 'L0_attn_gb1': _L0_attn_in['gb1'], 'L0_attn_gW2': _L0_attn_in['gW2'], 'L0_attn_gb2': _L0_attn_in['gb2'], 'L0_attn_temp': _L0_attn_in['temp'], 'L0_attn_eps_floor': _L0_attn_in['eps_floor'], 'L0_attn_onorm_w': _L0_attn_in['onorm_w'], 'L0_attn_Wo': _L0_attn_in['Wo'], 'L0_ffn_gate_w': _L0_ffn_in['gate_w'], 'L0_ffn_gate_b': _L0_ffn_in['gate_b'], 'L0_ffn_w1': _L0_ffn_in['w1'], 'L0_ffn_b1': _L0_ffn_in['b1'], 'L0_ffn_w2': _L0_ffn_in['w2'], 'L0_ffn_b2': _L0_ffn_in['b2']}
    _x0 = _d['L0_attn_x']
    _d['L0_attn_x'] = jax.random.normal(jax.random.fold_in(jax.random.key(seed), 1), (2, 1024, 128), dtype=_x0.dtype)
    del _x0
    return _d

def reference(L0_attn_x, L0_attn_Wq, L0_attn_Wk, L0_attn_Wv, L0_attn_Wb, L0_attn_qc_w, L0_attn_kc_w, L0_attn_vc_w, L0_attn_fir_s, L0_attn_fir_l, L0_attn_gW1, L0_attn_gb1, L0_attn_gW2, L0_attn_gb2, L0_attn_temp, L0_attn_eps_floor, L0_attn_onorm_w, L0_attn_Wo, L0_ffn_gate_w, L0_ffn_gate_b, L0_ffn_w1, L0_ffn_b1, L0_ffn_w2, L0_ffn_b2):

    def _L0_attn_ref(x, Wq, Wk, Wv, Wb, qc_w, kc_w, vc_w, fir_s, fir_l, gW1, gb1, gW2, gb2, temp, eps_floor, onorm_w, Wo):
        import jax, jax.numpy as jnp
        import numpy as np
        from jax.scipy.linalg import solve_triangular
        B, L, HID, NH = (2, 128, 128, 4)
        DK = DV = 32
        CONV_K, CHUNK, FIR_S_K, FIR_L_K = (4, 32, 3, 31)
        GATE_IN = HID + 3 * DV * 4 + DV * 4
        GATE_H = 2 * DV

        def _l2norm(x):
            return x * jax.lax.rsqrt(jnp.sum(x * x, -1, keepdims=True) + 1e-06)

        def _short_conv(x, w):
            c, k = w.shape
            y = jax.lax.conv_general_dilated(x.transpose(0, 2, 1), w[:, None, :], (1,), [(k - 1, 0)], feature_group_count=c)
            return jax.nn.silu(y.transpose(0, 2, 1))

        def _fir(x, f):
            b, l, h, d = x.shape
            k = f.shape[-1]
            xf = x.transpose(0, 2, 3, 1).reshape(b, h * d, l)
            y = jax.lax.conv_general_dilated(xf, f.reshape(h * d, 1, k), (1,), [(k - 1, 0)], feature_group_count=h * d)
            return y.reshape(b, h, d, l).transpose(0, 3, 1, 2)

        def _delta_rule(q, k, v, beta, chunk=CHUNK):
            b, h, l, dk = q.shape
            dv = v.shape[-1]
            n = l // chunk
            q = _l2norm(q)
            k = _l2norm(k)
            v = v * beta[..., None]
            kb = k * beta[..., None]
            rs = lambda t: t.reshape(b, h, n, chunk, -1)
            q, k, v, kb = map(rs, (q, k, v, kb))
            A = -jnp.tril(jnp.einsum('bhncd,bhned->bhnce', kb, k), -1)
            eye = jnp.eye(chunk, dtype=q.dtype)
            T = solve_triangular(eye - A, jnp.broadcast_to(eye, A.shape), lower=True)
            u = T @ v
            w = T @ kb
            mov = lambda t: jnp.moveaxis(t, 2, 0)

            def step(S, inp):
                qi, ki, ui, wi = inp
                attn = jnp.tril(qi @ ki.transpose(0, 1, 3, 2))
                u_i = ui - wi @ S
                o_i = qi @ S + attn @ u_i
                return (S + ki.transpose(0, 1, 3, 2) @ u_i, o_i)
            S0 = jnp.zeros((b, h, dk, dv), dtype=q.dtype)
            S, o = jax.lax.scan(step, S0, (mov(q), mov(k), mov(u), mov(w)))
            o = jnp.moveaxis(o, 0, 2).reshape(b, h, l, dv)
            return (o, S)

        def _gate(hidden, branches, W1, b1, W2, b2, temp, eps_floor):

            def stats(p):
                m = p.mean(-1, keepdims=True)
                r = jnp.sqrt(jnp.clip((p * p).mean(-1, keepdims=True), 1e-08))
                mx = p.max(-1, keepdims=True)
                return jnp.concatenate([jnp.broadcast_to(m, p.shape), jnp.broadcast_to(r, p.shape), jnp.broadcast_to(mx, p.shape)], -1)
            b, l, h, d = branches[0].shape
            hb = jnp.broadcast_to(hidden[:, :, None, :], (b, l, h, hidden.shape[-1]))
            head_in = jnp.concatenate([hb] + [stats(p) for p in branches] + list(branches), -1)
            hmid = jax.nn.gelu(head_in @ W1 + b1, approximate=False)
            logits = hmid @ W2 + b2
            t = jnp.clip(temp, 0.2, 10.0)[None, None, :, None]
            w = jax.nn.softmax(logits / t, -1)
            floor = jnp.clip(eps_floor, 1e-07, 0.1)[None, None]
            w = jnp.maximum(w, floor)
            return w / w.sum(-1, keepdims=True)
        b, l, _ = x.shape
        q = _short_conv(x @ Wq, qc_w).reshape(b, l, NH, DK)
        k = _short_conv(x @ Wk, kc_w).reshape(b, l, NH, DK)
        v = _short_conv(x @ Wv, vc_w).reshape(b, l, NH, DV)
        beta = jax.nn.sigmoid(x @ Wb)
        tr = lambda t: t.transpose(0, 2, 1, 3)
        delta_o, _ = _delta_rule(tr(q), tr(k), tr(v), beta.transpose(0, 2, 1))
        delta_o = tr(delta_o)
        branches = [_fir(v, fir_s), _fir(v, fir_l), delta_o, v]
        w = _gate(x, branches, gW1, gb1, gW2, gb2, temp, eps_floor)
        o = sum((w[..., i:i + 1] * branches[i] for i in range(4)))
        o = o * jax.lax.rsqrt((o * o).mean(-1, keepdims=True) + 1e-05) * onorm_w
        return o.reshape(b, l, NH * DV) @ Wo

    def _L0_ffn_ref(x, gate_w, gate_b, w1, b1, w2, b2):
        import jax, jax.numpy as jnp
        import numpy as np
        D = 128
        N_EXP = 8
        TOP_K = 1
        b, s, d = x.shape
        xf = x.reshape(-1, d)
        logits = xf @ gate_w + gate_b
        pb = jax.nn.softmax(logits, axis=-1)
        _, idx = jax.lax.top_k(pb, TOP_K)
        sel = jnp.any(idx[:, :, None] == jnp.arange(N_EXP)[None, None, :], axis=1)
        weights = pb * sel

        def expert_step(acc, params):
            w1e, b1e, w2e, b2e, wgt = params
            h = jax.nn.gelu(xf @ w1e + b1e, approximate=False)
            y = h @ w2e + b2e
            return (acc + wgt[:, None] * y, None)
        out0 = jnp.zeros_like(xf)
        out, _ = jax.lax.scan(expert_step, out0, (w1, b1, w2, b2, weights.T))
        return out.reshape(b, s, d)
    x = L0_attn_x
    x = x + 0.5 * _L0_ffn_ref(_layernorm(x, axis=-1), L0_ffn_gate_w, L0_ffn_gate_b, L0_ffn_w1, L0_ffn_b1, L0_ffn_w2, L0_ffn_b2)
    x = x + _L0_attn_ref(_layernorm(x, axis=-1), L0_attn_Wq, L0_attn_Wk, L0_attn_Wv, L0_attn_Wb, L0_attn_qc_w, L0_attn_kc_w, L0_attn_vc_w, L0_attn_fir_s, L0_attn_fir_l, L0_attn_gW1, L0_attn_gb1, L0_attn_gW2, L0_attn_gb2, L0_attn_temp, L0_attn_eps_floor, L0_attn_onorm_w, L0_attn_Wo)
    x = x + 0.5 * _L0_ffn_ref(_layernorm(x, axis=-1), L0_ffn_gate_w, L0_ffn_gate_b, L0_ffn_w1, L0_ffn_b1, L0_ffn_w2, L0_ffn_b2)
    return x

_drawn_inputs = setup_inputs


def setup_inputs(seed=0):
    import zlib

    import numpy as np

    out = dict(_drawn_inputs(seed))
    spreads = {'L0_attn_gb1': (0.0, 0.8),
     'L0_attn_gb2': (0.0, 0.8),
     'L0_attn_temp': (1.0, 0.6),
     'L0_attn_eps_floor': (0.009999999776482582, 0.6),
     'L0_attn_onorm_w': (1.0, 0.2),
     'L0_ffn_gate_b': (0.0, 0.549),
     'L0_ffn_b1': (0.0, 0.8),
     'L0_ffn_b2': (0.0, 0.493)}
    factors = {'L0_attn_Wb': 8.0,
     'L0_attn_fir_s': 24.648,
     'L0_attn_gW1': 8.0,
     'L0_attn_gW2': 8.0,
     'L0_ffn_gate_w': 3.214,
     'L0_ffn_w1': 6.261,
     'L0_ffn_w2': 5.692}
    for name, (base, spread) in spreads.items():
        noise = np.random.default_rng([zlib.crc32(name.encode()), seed]).standard_normal(out[name].shape)
        drawn = base * np.exp(spread * noise) if base else spread * noise
        out[name] = jnp.asarray(drawn.astype(out[name].dtype))
    for name, factor in factors.items():
        out[name] = (out[name] * factor).astype(out[name].dtype)
    return out
```

```python
from contextlib import ExitStack

import concourse.bass as bass
from concourse import mybir

F32 = mybir.dt.float32
I32 = mybir.dt.int32
ALU = mybir.AluOpType
ACT = mybir.ActivationFunctionType
AX = mybir.AxisListType

P = 128
BANK = 512
LN_EPS = 1e-5


class Chain:

    def __init__(self, eng, sem):
        self.eng, self.sem, self.n = eng, sem, 0

    def link(self, ins):
        self.n += 1
        ins.then_inc(self.sem, 1)
        return ins

    def wait(self):
        self.eng.wait_ge(self.sem, self.n)

    def step(self, ins):
        self.link(ins)
        self.wait()


def moe_ffn(nc, rep, cst, mem, banks, NT, NE, F):
    D = P
    FC = F // P
    MAXT = NT + NE - 1
    groups = [(g, min(4, MAXT - g)) for g in range(0, MAXT, 4)]
    X, b1T, a = mem["X"], mem["b1T"], mem["a"]
    XN, XNT = mem["XN"], mem["XNT"]
    xsort, ysort = mem["xsort"], mem["ysort"]
    ident, before, ones, gw, gb = cst["ident"], cst["before"], cst["ones"], cst["gw"], cst["gb"]
    with ExitStack() as ctx:
        def sb(name, shape, dt=F32):
            return ctx.enter_context(nc.sbuf_tensor(f"{name}_{rep}", shape, dt))

        def sem(name):
            return ctx.enter_context(nc.semaphore(f"{name}_{rep}"))

        W1 = sb("W1", [P, NE, F])
        W2 = sb("W2", [P, NE, FC, D])
        b2bc = sb("b2bc", [P, NE, D])
        weights_in = sem("weights_in")
        stats = sb("stats", [P, NT, 6])
        mv = sb("mv", [P, NT, 2])
        vare = sb("vare", [P, NT])
        rstd = sb("rstd", [P, NT])
        lg = sb("lg", [P, NT, NE])
        ex = sb("ex", [P, NT, NE])
        pb = sb("pb", [P, NT, NE])
        onehot = sb("onehot", [P, NT, NE])
        mx = sb("mx", [P, NT])
        den = sb("den", [P, NT])
        rden = sb("rden", [P, NT])
        pmax = sb("pmax", [P, NT])
        first = sb("first", [P, NT])
        wtok = sb("wtok", [P, NT])
        tot = sb("tot", [P, NE, NT])
        cum = sb("cum", [P, 1 + NE * NT])
        zero = sb("zero", [P, NE * NT])
        base = sb("base", [P, NE, NT])
        cnt = sb("cnt", [P, NE])
        over = sb("over", [P, NE, NT])
        ntile = sb("ntile", [P, NE])
        tend = sb("tend", [P, 1 + NE])
        goff = sb("goff", [P, NE])
        slot = sb("slot", [P, NT, NE])
        posf = sb("posf", [P, NT])
        pos = sb("pos", [P, NT], I32)
        past = sb("past", [P, MAXT, NE])
        eoff = sb("eoff", [P, MAXT])
        etile = sb("etile", [P, MAXT], I32)
        xs = sb("xs", [P, MAXT, D])
        xT = sb("xT", [P, MAXT, P])
        w1s = sb("w1s", [P, 2, F])
        b1s = sb("b1s", [P, 2, FC])
        hT = sb("hT", [P, 2, FC, P])
        Y = sb("Y", [P, MAXT, D])
        G = sb("G", [P, NT, D])

        dve_step = sem("dve_step")
        var_ready = sem("var_ready")
        rstd_ready = sem("rstd_ready")
        xn_ready = sem("xn_ready")
        xnT_psum = sem("xnT_psum")
        xnT_ready = sem("xnT_ready")
        gate_done = sem("gate_done")
        shifted = sem("shifted")
        exp_done = sem("exp_done")
        onehot_ready = sem("onehot_ready")
        ranks_done = sem("ranks_done")
        pos_ready = sem("pos_ready")
        etile_ready = sem("etile_ready")
        scattered = sem("scattered")
        x_loaded = [sem(f"x_loaded{c}") for c in range(len(groups))]
        xT_psum = sem("xT_psum")
        xT_ready = sem("xT_ready")
        w1_staged = sem("w1_staged")
        h_psum = sem("h_psum")
        h_ready = sem("h_ready")
        y_psum = sem("y_psum")
        y_ready = sem("y_ready")
        y_stored = sem("y_stored")
        gathered = [sem(f"gathered{c}") for c in range(NT // 4)]

        pT, pR, pRank, pTot = banks[0:2], banks[2], banks[3], banks[4]
        pX, pH, pY = banks[0:2], banks[2:4], banks[4:6]
        NC = NT // 4

        with nc.Block() as block:

            @block.sync
            def _(sp):
                sp.dma_start(W1[:], a["L0_ffn_w1"].rearrange("e d f -> d e f")).then_inc(weights_in, 16)
                sp.dma_start(W2[:], a["L0_ffn_w2"].rearrange("e (j f) d -> f e j d", f=P)).then_inc(weights_in, 16)
                sp.dma_start(b2bc[:], a["L0_ffn_b2"].partition_broadcast(P)).then_inc(weights_in, 16)
                sp.wait_ge(scattered, 16 * NT)
                for c, (g, n) in enumerate(groups):
                    sp.dma_start(xs[:, g:g + n, :], xsort[g * P:(g + n) * P, :].rearrange("(t p) d -> p t d", p=P))\
                      .then_inc(x_loaded[c], 16)
                with sp.Fori(0, MAXT) as t:
                    sp.wait_ge(y_ready, t + 1)
                    sp.dma_start(ysort[bass.ds(t * P, P), :], Y[:, bass.ds(t, 1), :]).then_inc(y_stored, 16)

            @block.gpsimd
            def _(gp):
                gp.wait_ge(var_ready, 1)
                gp.tensor_tensor(rstd[:], vare[:], cst["neghalf"][:, 0:1].to_broadcast([P, NT]), ALU.pow).then_inc(rstd_ready, 1)
                gp.wait_ge(pos_ready, 1)
                for t in range(NT):
                    gp.indirect_dma_start(xsort, bass.IndirectOffsetOnAxis(pos[:, t:t + 1], 0),
                                          XN[:, t, :], None).then_inc(scattered, 16)

                gp.wait_ge(y_stored, 16 * MAXT)
                for t in range(NT):
                    gp.indirect_dma_start(G[:, t, :], None, ysort,
                                          bass.IndirectOffsetOnAxis(pos[:, t:t + 1], 0)).then_inc(gathered[t // 4], 16)

            @block.tensor
            def _(pe):
                for t in range(NT):
                    pe.wait_ge(xn_ready, t + 1)
                    if t % 4 == 0 and t >= 8:
                        pe.wait_ge(xnT_ready, t // 4 - 1)
                    tr = pe.transpose(pT[t // 4 % 2][:, t % 4 * P:(t % 4 + 1) * P], XN[:, t, :], ident[:])
                    if t % 4 == 3:
                        tr.then_inc(xnT_psum, 1)
                for t in range(NT):
                    if t % 4 == 0:
                        pe.wait_ge(xnT_ready, t // 4 + 1)
                    mm = pe.matmul(pR[:, t * NE:(t + 1) * NE], XNT[:, t * P:(t + 1) * P], gw[:], start=True, stop=True)
                mm.then_inc(gate_done, 1)
                pe.wait_ge(onehot_ready, 1)
                pe.matmul(pRank[:, 0:NT * NE], before[:], onehot[:], start=True, stop=True)
                pe.matmul(pTot[:, 0:NT * NE], ones[:], onehot[:], start=True, stop=True).then_inc(ranks_done, 1)
                pe.wait_ge(etile_ready, 1)
                pe.wait_ge(weights_in, 48)

                for c, (g, n) in enumerate(groups):
                    pe.wait_ge(x_loaded[c], 16)
                    if c >= 2:
                        pe.wait_ge(xT_ready, c - 1)
                    for t in range(n):
                        tr = pe.transpose(pX[c % 2][:, t * P:(t + 1) * P], xs[:, g + t, :], ident[:])
                    tr.then_inc(xT_psum, 1)
                pe.wait_ge(xT_ready, len(groups))

                def up(t, s, reuse):
                    pe.wait_ge(w1_staged, t + 1)
                    if reuse:
                        pe.wait_ge(h_ready, FC * t - FC)
                    for j in range(FC):
                        mm = pe.matmul(pH[s][:, j * P:(j + 1) * P], w1s[:, s, j * P:(j + 1) * P],
                                       xT[:, bass.ds(t, 1), :], start=True, stop=True)
                    mm.then_inc(h_psum, 1)

                def down(t, s, reuse):
                    pe.wait_ge(h_ready, FC * t + FC)
                    if reuse:
                        pe.wait_ge(y_ready, t - 1)
                    e = pe.value_load(etile[0:1, bass.ds(t, 1)], min_val=0, max_val=NE - 1)
                    for j in range(FC):
                        mm = pe.matmul(pY[s][:, 0:D], hT[:, s, j, :], W2[:, bass.ds(e, 1), j, :],
                                       start=(j == 0), stop=(j == FC - 1))
                    mm.then_inc(y_psum, 1)

                up(0, 0, False)
                up(1, 1, False)
                down(0, 0, False)
                up(2, 0, True)
                down(1, 1, False)
                with pe.Fori(3, MAXT - 1, 2) as i:
                    for s in (1, 0):
                        up(i + 1 - s, s, True)
                        down(i - s, 1 - s, True)
                down(MAXT - 1, 0, True)

            @block.scalar
            def _(act):
                for c in range(NC):
                    act.wait_ge(xnT_psum, c + 1)
                    act.activation(XNT[:, c * BANK:(c + 1) * BANK], pT[c % 2][:], ACT.Copy).then_inc(xnT_ready, 1)
                act.wait_ge(shifted, 1)
                act.activation(ex[:], lg[:], ACT.Exp).then_inc(exp_done, 1)

                def gelu(t, s, reuse):
                    act.wait_ge(h_psum, t + 1)
                    if reuse:
                        act.wait_ge(y_psum, t - 1)
                    for j in range(FC):
                        act.activation(hT[:, s, j, :], pH[s][:, j * P:(j + 1) * P], ACT.Gelu,
                                       bias=b1s[:, s, j:j + 1]).then_inc(h_ready, 1)

                gelu(0, 0, False)
                gelu(1, 1, False)
                with act.Fori(2, MAXT - 1, 2) as i:
                    for s in range(2):
                        gelu(i + s, s, True)
                gelu(MAXT - 1, 0, True)

            @block.vector
            def _(ve):
                ch = Chain(ve, dve_step)
                for t in range(NT):
                    bs = ve.bn_stats(stats[:, t, :], X[:, t, :])
                ch.step(bs)
                for t in range(NT):
                    ag = ve.bn_aggr(mv[:, t, :], stats[:, t, :])
                ch.step(ag)
                ve.tensor_scalar(vare[:], mv[:, :, 1], LN_EPS, None, ALU.add).then_inc(var_ready, 1)
                ve.wait_ge(rstd_ready, 1)
                for t in range(NT):
                    ve.tensor_scalar(XN[:, t, :], X[:, t, :], mv[:, t, 0:1], rstd[:, t:t + 1],
                                     ALU.subtract, ALU.mult).then_inc(xn_ready, 1)

                def ebc(ap):
                    return ap.unsqueeze(2).to_broadcast([P, NT, NE])

                ch.step(ve.memset(zero[:], 0.0))
                ve.wait_ge(gate_done, 1)
                ch.step(ve.tensor_tensor(lg[:], pR[:, 0:NT * NE].rearrange("p (t e) -> p t e", e=NE),
                                         gb[:].unsqueeze(1).to_broadcast([P, NT, NE]), ALU.add))
                ch.step(ve.tensor_reduce(mx[:], lg[:], AX.X, ALU.max))
                ve.tensor_tensor(lg[:], lg[:], ebc(mx[:]), ALU.subtract).then_inc(shifted, 1)
                ve.wait_ge(exp_done, 1)
                ch.step(ve.tensor_reduce(den[:], ex[:], AX.X, ALU.add))
                ch.step(ve.reciprocal(rden[:], den[:]))
                ch.step(ve.tensor_tensor(pb[:], ex[:], ebc(rden[:]), ALU.mult))
                ch.step(ve.tensor_reduce(pmax[:], pb[:], AX.X, ALU.max))
                ve.tensor_scalar(wtok[:], pmax[:], 0.5, None, ALU.mult)
                ch.step(ve.tensor_tensor(pb[:], pb[:], ebc(pmax[:]), ALU.is_ge))
                ch.step(ve.tensor_tensor(pb[:], pb[:], cst["falling"][:].unsqueeze(1).to_broadcast([P, NT, NE]), ALU.mult))
                ch.step(ve.tensor_reduce(first[:], pb[:], AX.X, ALU.max))
                ve.tensor_tensor(onehot[:], pb[:], ebc(first[:]), ALU.is_equal).then_inc(onehot_ready, 1)
                ve.wait_ge(ranks_done, 1)
                ch.step(ve.tensor_copy(tot[:].rearrange("p e t -> p t e"), pTot[:, 0:NT * NE].rearrange("p (t e) -> p t e", e=NE)))
                ch.step(ve.memset(cum[:, 0:1], 0.0))
                ch.step(ve.tensor_tensor_scan(cum[:, 1:1 + NE * NT], tot[:].rearrange("p e t -> p (e t)"), zero[:], 0.0, ALU.add, ALU.add))
                C = cum[:, 1:1 + NE * NT].rearrange("p (e t) -> p e t", t=NT)
                ends, starts = C[:, :, NT - 1], cum[:, 0:NE * NT].rearrange("p (e t) -> p e t", t=NT)[:, :, 0]
                ch.step(ve.tensor_tensor(cnt[:], ends, starts, ALU.subtract))
                ch.step(ve.tensor_tensor(over[:], cnt[:].unsqueeze(2).to_broadcast([P, NE, NT]),
                                         cst["tilestart"][:].unsqueeze(1).to_broadcast([P, NE, NT]), ALU.is_gt))
                ch.step(ve.tensor_reduce(ntile[:], over[:], AX.X, ALU.add))
                ch.step(ve.memset(tend[:, 0:1], 0.0))
                ch.step(ve.tensor_tensor_scan(tend[:, 1:1 + NE], ntile[:], zero[:, 0:NE], 0.0, ALU.add, ALU.add))
                ch.step(ve.scalar_tensor_tensor(goff[:], tend[:, 0:NE], float(P), starts, ALU.mult, ALU.subtract))
                ch.step(ve.tensor_tensor(base[:], C, tot[:], ALU.subtract))
                ch.step(ve.tensor_tensor(base[:], base[:], goff[:].unsqueeze(2).to_broadcast([P, NE, NT]), ALU.add))
                ch.step(ve.tensor_tensor(slot[:], pRank[:, 0:NT * NE].rearrange("p (t e) -> p t e", e=NE),
                                         base[:].rearrange("p e t -> p t e"), ALU.add))
                ch.step(ve.tensor_tensor(slot[:], slot[:], onehot[:], ALU.mult))
                ch.step(ve.tensor_reduce(posf[:], slot[:], AX.X, ALU.add))
                ve.tensor_copy(pos[:], posf[:]).then_inc(pos_ready, 1)
                ch.step(ve.tensor_tensor(past[:], cst["tileno"][:].unsqueeze(2).to_broadcast([P, MAXT, NE]),
                                         tend[:, 1:1 + NE].unsqueeze(1).to_broadcast([P, MAXT, NE]), ALU.is_ge))
                ch.step(ve.tensor_reduce(eoff[:], past[:], AX.X, ALU.add))
                ch.step(ve.tensor_scalar(eoff[:], eoff[:], float(NE - 1), None, ALU.min))
                ve.tensor_copy(etile[:], eoff[:]).then_inc(etile_ready, 1)

                def stage(t, s, reuse):
                    if reuse:
                        ve.wait_ge(h_psum, t - 1)
                        ve.wait_ge(h_ready, FC * t - FC)
                    e = ve.value_load(etile[0:1, bass.ds(t, 1)], min_val=0, max_val=NE - 1)
                    ve.tensor_copy(b1s[:, s, :], b1T[:, bass.ds(e, 1), :])
                    ve.tensor_copy(w1s[:, s, :], W1[:, bass.ds(e, 1), :]).then_inc(w1_staged, 1)

                def take_y(t, s):
                    ve.wait_ge(y_psum, t + 1)
                    e = ve.value_load(etile[0:1, bass.ds(t, 1)], min_val=0, max_val=NE - 1)
                    ve.tensor_tensor(Y[:, bass.ds(t, 1), :], pY[s][:, 0:D], b2bc[:, bass.ds(e, 1), :], ALU.add).then_inc(y_ready, 1)

                ve.wait_ge(etile_ready, 1)
                ve.wait_ge(weights_in, 48)
                stage(0, 0, False)
                stage(1, 1, False)
                for c, (g, n) in enumerate(groups):
                    ve.wait_ge(xT_psum, c + 1)
                    ve.tensor_copy(xT[:, g:g + n, :], pX[c % 2][:, 0:n * P].rearrange("p (t q) -> p t q", q=P)).then_inc(xT_ready, 1)
                stage(2, 0, True)
                take_y(0, 0)
                with ve.Fori(3, MAXT - 1, 2) as i:
                    for s in (1, 0):
                        stage(i + 1 - s, s, True)
                        take_y(i - 1 - s, s)
                take_y(MAXT - 2, 1)
                take_y(MAXT - 1, 0)
                for t in range(NT):
                    if t % 4 == 0:
                        ve.wait_ge(gathered[t // 4], 64)
                    ve.scalar_tensor_tensor(X[:, t, :], G[:, t, :], wtok[:, t:t + 1], X[:, t, :], ALU.mult, ALU.add)


def layernorm(ve, gp, X, XN, t, ch, var_ready, rstd_ready, xn_ready, neghalf, NT):
    if ve is not None:
        for n in range(NT):
            bs = ve.bn_stats(t["stats"][:, n, :], X[:, n, :])
        ch.step(bs)
        for n in range(NT):
            ag = ve.bn_aggr(t["mv"][:, n, :], t["stats"][:, n, :])
        ch.step(ag)
        ve.tensor_scalar(t["vare"][:], t["mv"][:, :, 1], LN_EPS, None, ALU.add).then_inc(var_ready, 1)
        ve.wait_ge(rstd_ready, 1)
        for n in range(NT):
            ve.tensor_scalar(XN[:, n, :], X[:, n, :], t["mv"][:, n, 0:1], t["rstd"][:, n:n + 1],
                             ALU.subtract, ALU.mult).then_inc(xn_ready, 1)
    if gp is not None:
        gp.wait_ge(var_ready, 1)
        gp.tensor_tensor(t["rstd"][:], t["vare"][:], neghalf[:, 0:1].to_broadcast([P, NT]), ALU.pow)\
          .then_inc(rstd_ready, 1)


def attn_project(nc, cst, mem, banks, B, L, NH):
    NT, NG, TB = B * L // P, B * L // BANK, 4
    DK = P // NH
    X, XN, XNT = mem["X"], mem["XN"], mem["XNT"]
    QT, KT, KBT, K, KB, V, VB, VP = (mem[n] for n in ("QT", "KT", "KBT", "K", "KB", "V", "VB", "VP"))
    ident = cst["ident"]
    TAPS, PAD = cst["convw"].shape[2], VP.shape[2] - L
    with ExitStack() as ctx:
        def sb(name, shape, dt=F32):
            return ctx.enter_context(nc.sbuf_tensor(f"a_{name}", shape, dt))

        def sem(name):
            return ctx.enter_context(nc.semaphore(f"a_{name}"))

        ln = {"stats": sb("stats", [P, NT, 6]), "mv": sb("mv", [P, NT, 2]), "vare": sb("vare", [P, NT]), "rstd": sb("rstd", [P, NT])}
        PRE = [sb(f"PRE{w}", [P, B, TAPS - 1 + L]) for w in range(3)]
        CV = [sb(f"CV{w}", [P, B, L]) for w in range(3)]
        Q = sb("Q", [P, NT, P])
        SQ = [sb("SQ0", [P, NT, P]), XN]
        eb = sb("eb", [P, NT, NH])
        beta = sb("beta", [P, NT, NH])
        ss = sb("ss", [P, 2, NT, NH])
        rn = sb("rn", [P, 2, NT, NH])
        dve_step, var_ready, rstd_ready, xn_ready = sem("dve_step"), sem("var_ready"), sem("rstd_ready"), sem("xn_ready")
        xnT_psum, xnT_ready = sem("xnT_psum"), sem("xnT_ready")
        beta_psum, beta_exp, beta_ready = sem("beta_psum"), sem("beta_exp"), sem("beta_ready")
        proj_psum = sem("proj_psum")
        proj_taken = sem("proj_taken")
        padded = sem("padded")
        conv_ready = sem("conv_ready")
        silu_ready = sem("silu_ready")
        raw_psum, raw_taken = sem("raw_psum"), sem("raw_taken")
        sq_ready = sem("sq_ready")
        ss_ready, rn_ready = sem("ss_ready"), sem("rn_ready")
        norm_ready = sem("norm_ready")
        vb_ready = sem("vb_ready")
        nT_psum, nT_taken = sem("nT_psum"), sem("nT_taken")
        raw_dst = [Q, K, V]
        raw_src = [QT[:], KT[:], None]
        ring = banks[2:6]

        with nc.Block() as block:

            @block.tensor
            def _(pe):
                for t in range(NT):
                    pe.wait_ge(xn_ready, t + 1)
                    if t % TB == 0 and t >= 2 * TB:
                        pe.wait_ge(xnT_ready, t // TB - 1)
                    tr = pe.transpose(banks[t // TB % 2][:, t % TB * P:(t % TB + 1) * P], XN[:, t, :], ident[:])
                    if t % TB == TB - 1:
                        tr.then_inc(xnT_psum, 1)
                for w in range(3):
                    for c in range(NG):
                        i = w * NG + c
                        if w == 0:
                            pe.wait_ge(xnT_ready, c + 1)
                        if i >= 4:
                            pe.wait_ge(proj_taken, i - 3)
                        pe.matmul(ring[i % 4][:], cst["wqkv"][:, w, :], XNT[:, c * BANK:(c + 1) * BANK],
                                  start=True, stop=True).then_inc(proj_psum, 1)
                for t in range(NT):
                    mm = pe.matmul(banks[7][:, t * NH:(t + 1) * NH], XNT[:, t * P:(t + 1) * P], cst["wb"][:], start=True, stop=True)
                mm.then_inc(beta_psum, 1)
                pe.wait_ge(proj_taken, 3 * NG)
                for w in range(3):
                    for g in range(NG):
                        i = w * NG + g
                        pe.wait_ge(silu_ready, w * B + g * BANK // L + 1)
                        if i >= 4:
                            pe.wait_ge(raw_taken, i - 3)
                        for t in range(TB):
                            n = g * TB + t
                            if w < 2:
                                src = raw_src[w][:, n * P:(n + 1) * P]
                            else:
                                b, o = n * P // L, n * P % L
                                src = VP[:, b, PAD + o:PAD + o + P]
                            tr = pe.transpose(ring[i % 4][:, t * P:(t + 1) * P], src, ident[:])
                        tr.then_inc(raw_psum, 1)
                pe.wait_ge(raw_taken, 3 * NG)
                for w, src in enumerate((Q, K, KB)):
                    pe.wait_ge(norm_ready, w + 1)
                    for g in range(NG):
                        i = w * NG + g
                        if i >= 4:
                            pe.wait_ge(nT_taken, i - 3)
                        for t in range(TB):
                            tr = pe.transpose(ring[i % 4][:, t * P:(t + 1) * P], src[:, g * TB + t, :], ident[:])
                        tr.then_inc(nT_psum, 1)

            @block.scalar
            def _(act):
                for c in range(NG):
                    act.wait_ge(xnT_psum, c + 1)
                    act.activation(XNT[:, c * BANK:(c + 1) * BANK], banks[c % 2][:], ACT.Copy).then_inc(xnT_ready, 1)
                for w in range(3):
                    for c in range(NG):
                        i = w * NG + c
                        act.wait_ge(proj_psum, i + 1)
                        b, o = c * BANK // L, c * BANK % L
                        act.activation(PRE[w][:, b, TAPS - 1 + o:TAPS - 1 + o + BANK], ring[i % 4][:], ACT.Copy).then_inc(proj_taken, 1)
                act.wait_ge(beta_psum, 1)
                act.activation(eb[:].rearrange("p t h -> p (t h)"), banks[7][:, 0:NT * NH], ACT.Exp, scale=-1.0).then_inc(beta_exp, 1)
                for w, dst in enumerate((QT[:].rearrange("p (b l) -> p b l", b=B), KT[:].rearrange("p (b l) -> p b l", b=B), VP[:, :, PAD:PAD + L])):
                    for b in range(B):
                        act.wait_ge(conv_ready, w * B + b + 1)
                        act.activation(dst[:, b, :], CV[w][:, b, :], ACT.Silu).then_inc(silu_ready, 1)
                for w in range(3):
                    for g in range(NG):
                        i = w * NG + g
                        act.wait_ge(raw_psum, i + 1)
                        psum = ring[i % 4][:].rearrange("p (t c) -> p t c", c=P)
                        if w < 2:
                            if w == 1 and g == 0:
                                act.wait_ge(xnT_psum, NG)
                            act.activation(SQ[w][:, g * TB:(g + 1) * TB, :], psum, ACT.Square).then_inc(sq_ready, 1)
                        act.activation(raw_dst[w][:, g * TB:(g + 1) * TB, :], psum, ACT.Copy).then_inc(raw_taken, 1)
                for w, dst in enumerate((QT, KT, KBT)):
                    for g in range(NG):
                        act.wait_ge(nT_psum, w * NG + g + 1)
                        act.activation(dst[:, g * BANK:(g + 1) * BANK], ring[(w * NG + g) % 4][:], ACT.Copy).then_inc(nT_taken, 1)

            @block.gpsimd
            def _(gp):
                layernorm(None, gp, X, XN, ln, None, var_ready, rstd_ready, xn_ready, cst["neghalf"], NT)
                gp.wait_ge(ss_ready, 2)
                gp.tensor_tensor(rn[:], ss[:], cst["neghalf"][:, 0:1].to_broadcast([P, 2 * NT * NH]).rearrange("p (a t h) -> p a t h", a=2, h=NH), ALU.pow).then_inc(rn_ready, 1)
                gp.wait_ge(beta_ready, 1)
                gp.wait_ge(raw_taken, 3 * NG)
                gp.tensor_tensor(VB[:].rearrange("p t (h d) -> p (t h) d", h=NH), V[:].rearrange("p t (h d) -> p (t h) d", h=NH),
                                 beta[:].rearrange("p t h -> p (t h)").unsqueeze(2).to_broadcast([P, NT * NH, DK]), ALU.mult).then_inc(vb_ready, 1)

            @block.vector
            def _(ve):
                ch = Chain(ve, dve_step)
                for w in range(3):
                    ve.memset(PRE[w][:, :, 0:TAPS - 1], 0.0)
                ve.memset(VP[:, :, 0:PAD], 0.0)
                layernorm(ve, None, X, XN, ln, ch, var_ready, rstd_ready, xn_ready, None, NT)
                for w in range(3):
                    ve.wait_ge(proj_taken, (w + 1) * NG)
                    for k in range(TAPS):
                        for b in range(B):
                            src, cw = PRE[w][:, b, k:k + L], cst["convw"][:, w, k:k + 1]
                            if k == 0:
                                ins = ve.tensor_scalar(CV[w][:, b, :], src, cw, None, ALU.mult)
                            else:
                                ve.wait_ge(dve_step, ch.n - B + 1)
                                ins = ve.scalar_tensor_tensor(CV[w][:, b, :], src, cw, CV[w][:, b, :], ALU.mult, ALU.add)
                            if k == TAPS - 1:
                                ins.then_inc(conv_ready, 1)
                                ch.n += 0
                            else:
                                ch.link(ins)
                        if k == TAPS - 2:
                            ch.wait()
                ve.wait_ge(beta_exp, 1)
                ch.step(ve.tensor_scalar(eb[:], eb[:], 1.0, None, ALU.add))
                ve.reciprocal(beta[:], eb[:]).then_inc(beta_ready, 1)
                for w in range(2):
                    ve.wait_ge(sq_ready, NG * (w + 1))
                    ch.step(ve.tensor_reduce(ss[:, w, :, :], SQ[w][:].rearrange("p t (h d) -> p t h d", h=NH), AX.X, ALU.add))
                    ve.tensor_scalar(ss[:, w, :, :], ss[:, w, :, :], 1e-6, None, ALU.add).then_inc(ss_ready, 1)
                ve.wait_ge(rn_ready, 1)
                ve.wait_ge(raw_taken, 2 * NG)
                ve.wait_ge(beta_ready, 1)

                def bc(ap):
                    return ap.rearrange("p t h -> p (t h)").unsqueeze(2).to_broadcast([P, NT * NH, DK])

                def heads(ap):
                    return ap.rearrange("p t (h d) -> p (t h) d", h=NH)
                ve.tensor_tensor(heads(Q[:]), heads(Q[:]), bc(rn[:, 0, :, :]), ALU.mult).then_inc(norm_ready, 1)
                ve.tensor_tensor(heads(K[:]), heads(K[:]), bc(rn[:, 1, :, :]), ALU.mult).then_inc(norm_ready, 1)
                ve.wait_ge(norm_ready, 2)
                ve.tensor_tensor(heads(KB[:]), heads(K[:]), bc(beta[:]), ALU.mult).then_inc(norm_ready, 1)


def attn_delta(nc, cst, mem, banks, B, L, NH):
    C = 32
    NT, TB, DK = B * L // P, 4, P // NH
    CT = P // C
    TH = NT // B
    S = TH * NH
    SG = BANK // C
    NGS = S // SG
    QT, KT, KBT, K, KB, VB, VP = (mem[n] for n in ("QT", "KT", "KBT", "K", "KB", "VB", "VP"))
    FS, FL, DEL, XN = (mem[n] for n in ("FS", "FL", "DEL", "XN"))
    PAD = VP.shape[2] - L
    NL = 3
    with ExitStack() as ctx:
        def sb(name, shape, dt=F32):
            return ctx.enter_context(nc.sbuf_tensor(f"d_{name}", shape, dt))

        def sem(name):
            return ctx.enter_context(nc.semaphore(f"d_{name}"))

        AT = sb("AT", [P, S, P])
        DT = sb("DT", [P, S, P])
        D = sb("D", [P, S, C])
        Z = sb("Z", [P, S, C])
        WT = sb("WT", [P, NT * P])
        U = sb("U", [P, NT, P])
        SB = sb("SB", [P, B, P])
        dve_step = sem("dve_step")
        zeroed = sem("zeroed")
        at_psum, at_ready = sem("at_psum"), sem("at_ready")
        prod_psum = sem("prod_psum")
        z_ready = sem("z_ready")
        d_ready = sem("d_ready")
        dt_ready = sem("dt_ready")
        u0_psum, u0_ready = sem("u0_psum"), sem("u0_ready")
        wt_psum, wt_ready = sem("wt_psum"), sem("wt_ready")
        ws_psum = sem("ws_psum")
        u_ready = sem("u_ready")
        s_psum, s_ready = sem("s_psum"), sem("s_ready")
        qs_psum, qs_taken = sem("qs_psum"), sem("qs_taken")
        m_psum, m_ready = sem("m_psum"), sem("m_ready")
        o_psum = sem("o_psum")
        fir_step = sem("fir_step")

        def stacked(ap, g):
            return ap[:, g * SG:(g + 1) * SG, :]

        def bank3(bank):
            return bank[:].rearrange("p (s c) -> p s c", c=C)

        STAGES = 3 + 2 * NL
        RS = TH // TB
        at_banks = [banks[i] for i in (0, 1, 6, 7)]

        def head_of(m, r, h):
            r %= RS
            return m[:, r * TB * NH:(r + 1) * TB * NH, :].rearrange("p (t h) c -> p t h c", h=NH)[:, :, h, :]

        with nc.Block() as block:

            @block.tensor
            def _(pe):
                for b in range(B):
                    for r in range(b * RS, (b + 1) * RS):
                        for h in range(NH):
                            rows = slice(h * DK, (h + 1) * DK)
                            if r >= 1:
                                pe.wait_ge(at_ready, (r - 1) * NH + h + 1)
                            for t in range(TB):
                                cols = slice((r * TB + t) * P, (r * TB + t + 1) * P)
                                mm = pe.matmul(at_banks[h][:, t * P:(t + 1) * P], KT[rows, cols], KBT[rows, cols], start=True, stop=True)
                            mm.then_inc(at_psum, 1)
                    pe.wait_ge(at_ready, (b + 1) * RS * NH)
                    for st in range(STAGES):
                        for g in range(NGS):
                            base = b * (3 + NL) * NGS
                            lvl = (st - 3) // 2
                            if st == 0:
                                lhs, rhs = AT, None
                                if b > 0:
                                    pe.wait_ge(d_ready, base)
                            elif st < 3 or st % 2 == 1:
                                lhs, rhs = AT, D
                                before = st if st < 3 else 3 + lvl
                                pe.wait_ge(d_ready, base + (before - 1) * NGS + g + 1)
                            else:
                                lhs, rhs = DT, Z
                                pe.wait_ge(z_ready, b * STAGES * NGS - b * NL * NGS + (3 + lvl) * NGS + g + 1)
                                pe.wait_ge(dt_ready, b * (1 + NL) * NGS + lvl * NGS + g + 1)
                            for s in range(SG):
                                r = cst["istack"][:] if rhs is None else rhs[:, g * SG + s, :]
                                mm = pe.matmul(banks[2 + g][:, s * C:(s + 1) * C], lhs[:, g * SG + s, :], r, start=True, stop=True)
                            mm.then_inc(prod_psum, 1)
                    pe.wait_ge(dt_ready, (b + 1) * (1 + NL) * NGS)
                    for g in range(TH // TB):
                        n = b * TH // TB + g
                        if n >= 1:
                            pe.wait_ge(u0_ready, n)
                            pe.wait_ge(wt_ready, n)
                        for t in range(TB):
                            tile, s0 = b * TH + g * TB + t, (g * TB + t) * NH
                            for h in range(NH):
                                mm = pe.matmul(banks[4][:, t * P + h * DK:t * P + (h + 1) * DK], DT[:, s0 + h, :],
                                               VB[:, tile, h * DK:(h + 1) * DK], start=True, stop=True)
                        mm.then_inc(u0_psum, 1)
                        for t in range(TB):
                            tile, s0 = b * TH + g * TB + t, (g * TB + t) * NH
                            for h in range(NH):
                                mm = pe.matmul(banks[5][h * DK:(h + 1) * DK, t * P:(t + 1) * P], KB[:, tile, h * DK:(h + 1) * DK],
                                               DT[:, s0 + h, :], start=True, stop=True)
                        mm.then_inc(wt_psum, 1)
                pe.wait_ge(u0_ready, NT // TB)
                pe.wait_ge(wt_ready, NT // TB)
                for n in range(L // C):
                    c, t = n % CT, n // CT
                    rows = slice(c * C, (c + 1) * C)
                    for b in range(B):
                        tile = b * TH + t
                        cols = slice(tile * P + c * C, tile * P + (c + 1) * C)
                        i = n * B + b
                        if n > 0:
                            pe.wait_ge(s_ready, i - B + 1)
                        pe.matmul(banks[b][rows, 0:P], WT[:, cols], SB[:, b, :], start=True, stop=True).then_inc(ws_psum, 1)
                        if c == 0 and t >= 2:
                            pe.wait_ge(qs_taken, (t - 2) * B + b + 1)
                        mm = pe.matmul(banks[4 + 2 * b + t % 2][rows, 0:P], QT[:, cols], SB[:, b, :], start=True, stop=True)
                        if c == CT - 1:
                            mm.then_inc(qs_psum, 1)
                    for b in range(B):
                        tile, i = b * TH + t, n * B + b
                        pe.wait_ge(u_ready, i + 1)
                        pe.matmul(banks[2 + b][:, 0:P], K[rows, tile, :], U[rows, tile, :], start=(n == 0),
                                  stop=(n == L // C - 1), skip_group_check=True).then_inc(s_psum, 1)
                pe.wait_ge(qs_taken, NT)
                pe.wait_ge(s_ready, B * (L // C))
                def scores(r):
                    for h in range(NH):
                        rows = slice(h * DK, (h + 1) * DK)
                        if r >= 1:
                            pe.wait_ge(m_ready, (r - 1) * NH + h + 1)
                        for t in range(TB):
                            cols = slice((r * TB + t) * P, (r * TB + t + 1) * P)
                            mm = pe.matmul(banks[h][:, t * P:(t + 1) * P], KT[rows, cols], QT[rows, cols], start=True, stop=True)
                        mm.then_inc(m_psum, 1)
                scores(0)
                for r in range(NT // TB):
                    if r + 1 < NT // TB:
                        scores(r + 1)
                    pe.wait_ge(m_ready, (r + 1) * NH)
                    for h in range(NH):
                        for t in range(TB):
                            tile = r * TB + t
                            mm = pe.matmul(banks[4 + r][:, t * P + h * DK:t * P + (h + 1) * DK],
                                           AT[:, tile % TH * NH + h, :], U[:, tile, h * DK:(h + 1) * DK], start=True, stop=True)
                    mm.then_inc(o_psum, 1)

            @block.scalar
            def _(act):
                for n in range(NT // TB):
                    act.wait_ge(u0_psum, n + 1)
                    act.activation(U[:, n * TB:(n + 1) * TB, :], banks[4][:].rearrange("p (t c) -> p t c", c=P), ACT.Copy).then_inc(u0_ready, 1)
                    act.wait_ge(wt_psum, n + 1)
                    act.activation(WT[:, n * BANK:(n + 1) * BANK], banks[5][:], ACT.Copy).then_inc(wt_ready, 1)
                for t in range(TH):
                    for b in range(B):
                        act.wait_ge(qs_psum, t * B + b + 1)
                        act.activation(DEL[:, b * TH + t, :], banks[4 + 2 * b + t % 2][:, 0:P], ACT.Copy).then_inc(qs_taken, 1)

            @block.gpsimd
            def _(gp):
                gp.memset(DT[:].rearrange("p s c -> p (s c)"), 0.0).then_inc(zeroed, 1)
                gp.memset(SB[:], 0.0).then_inc(zeroed, 1)

            @block.vector
            def _(ve):
                taps = [(FS, cst["firs"], k) for k in range(cst["firs"].shape[1])] + \
                       [(FL, cst["firl"], k) for k in range(cst["firl"].shape[1])]
                done = [0]

                def fir(count):
                    for dst, f, k in taps[done[0]:done[0] + count]:
                        K_ = f.shape[1]
                        for b in range(B):
                            src = VP[:, b, PAD - (K_ - 1) + k:PAD - (K_ - 1) + k + L]
                            if k == 0:
                                ve.tensor_scalar(dst[:, b, :], src, f[:, k:k + 1], None, ALU.mult).then_inc(fir_step, 1)
                            else:
                                ve.wait_ge(fir_step, B * done[0] + b - B + 1)
                                ve.scalar_tensor_tensor(dst[:, b, :], src, f[:, k:k + 1], dst[:, b, :], ALU.mult, ALU.add).then_inc(fir_step, 1)
                        done[0] += 1

                def mask(i):
                    return cst["lmask"][:, i, :].unsqueeze(1).to_broadcast([P, SG, C])

                ve.wait_ge(zeroed, 2)
                for b in range(B):
                    if b > 0:
                        ve.wait_ge(u0_psum, b * TH // TB)
                        ve.wait_ge(wt_psum, b * TH // TB)
                    for r in range(b * RS, (b + 1) * RS):
                        for h in range(NH):
                            ve.wait_ge(at_psum, r * NH + h + 1)
                            ve.tensor_tensor(head_of(AT, r, h), at_banks[h][:].rearrange("p (t c) -> p t c", c=P),
                                             cst["atmask"][:].unsqueeze(1).to_broadcast([P, TB, P]), ALU.mult).then_inc(at_ready, 1)
                    zn, dn = b * (3 + NL) * NGS, b * (3 + NL) * NGS

                    def transposed(g):
                        ve.wait_ge(d_ready, dn)
                        for q in range(CT):
                            rows = slice(q * C, (q + 1) * C)
                            tr = ve.transpose(DT[rows, g * SG:(g + 1) * SG, rows], D[rows, g * SG:(g + 1) * SG, :])
                        tr.then_inc(dt_ready, 1)

                    for st in range(STAGES):
                        for g in range(NGS):
                            ve.wait_ge(prod_psum, (b * STAGES + st) * NGS + g + 1)
                            zg, dg, psum = stacked(Z, g), stacked(D, g), bank3(banks[2 + g])
                            if st < 3:
                                ve.tensor_tensor(zg, psum, mask(0), ALU.mult).then_inc(z_ready, 1)
                                zn += 1
                                ve.wait_ge(z_ready, zn)
                                ve.tensor_tensor(dg, zg, cst["istack"][:].unsqueeze(1).to_broadcast([P, SG, C]), ALU.add).then_inc(d_ready, 1)
                                dn += 1
                                if st == 2:
                                    transposed(g)
                            elif st % 2 == 1:
                                ve.tensor_tensor(zg, psum, mask(1 + (st - 3) // 2), ALU.mult).then_inc(z_ready, 1)
                                zn += 1
                            else:
                                ve.tensor_tensor(dg, psum, dg, ALU.add).then_inc(d_ready, 1)
                                dn += 1
                                transposed(g)
                for n in range(L // C):
                    c, t = n % CT, n // CT
                    rows = slice(c * C, (c + 1) * C)
                    for b in range(B):
                        tile, i = b * TH + t, n * B + b
                        ve.wait_ge(ws_psum, i + 1)
                        if n == 0:
                            ve.wait_ge(u0_ready, NT // TB)
                        ve.tensor_tensor(U[rows, tile, :], U[rows, tile, :], banks[b][rows, 0:P], ALU.subtract).then_inc(u_ready, 1)
                    for b in range(B):
                        i = n * B + b
                        ve.wait_ge(s_psum, i + 1)
                        ve.tensor_tensor(SB[:, b, :], banks[2 + b][:, 0:P], cst["blk"][:], ALU.mult).then_inc(s_ready, 1)
                    fir(1)
                fir(len(taps) - done[0])
                ve.wait_ge(qs_taken, NT)
                for r in range(NT // TB + 1):
                    for h in range(NH if r < NT // TB else 0):
                        ve.wait_ge(m_psum, r * NH + h + 1)
                        if r >= RS:
                            ve.wait_ge(o_psum, r - RS + 1)
                        ve.tensor_tensor(head_of(AT, r, h), banks[h][:].rearrange("p (t c) -> p t c", c=P),
                                         cst["mmask"][:].unsqueeze(1).to_broadcast([P, TB, P]), ALU.mult).then_inc(m_ready, 1)
                    if r > 0:
                        ve.wait_ge(o_psum, r)
                        ve.tensor_tensor(DEL[:, (r - 1) * TB:r * TB, :], DEL[:, (r - 1) * TB:r * TB, :],
                                         banks[3 + r][:].rearrange("p (t c) -> p t c", c=P), ALU.add)


def attn_mix(nc, cst, mem, banks, B, L, NH):
    NT, NG, TB, DK = B * L // P, B * L // BANK, 4, P // NH
    NB, NP = 4, NH // 2
    X, XNT, V, VP, FS, FL, DEL = (mem[n] for n in ("X", "XNT", "V", "VP", "FS", "FL", "DEL"))
    PAD = VP.shape[2] - L
    ident = cst["ident"]
    with ExitStack() as ctx:
        def sb(name, shape, dt=F32):
            return ctx.enter_context(nc.sbuf_tensor(f"m_{name}", shape, dt))

        def sem(name):
            return ctx.enter_context(nc.semaphore(f"m_{name}"))

        FSt, FLt = sb("FSt", [P, NT, P]), sb("FLt", [P, NT, P])
        DELT = sb("DELT", [P, NT * P])
        SQ = sb("SQ", [P, 2, NT, P])
        ms = sb("ms", [P, NT, NB, NH])
        ST = sb("ST", [P, NT, 2, NB, NH])
        STT = sb("STT", [2 * NB * NH, NT * P])
        G = sb("G", [P, NP, NT * P])
        lg = sb("lg", [P, NT, NH, NB])
        mx = sb("mx", [P, NT, NH])
        ex = sb("ex", [P, NT, NH, NB])
        MIX = sb("MIX", [P, NT, P])
        TMP = sb("TMP", [P, 2, NT, P])
        os_ = sb("os", [P, NT, NH])
        ro = sb("ro", [P, NT, NH])
        OT = sb("OT", [P, NT * P])
        dve_step = sem("dve_step")
        tr_psum, tr_taken = sem("tr_psum"), sem("tr_taken")
        sq_ready, sq_read = sem("sq_ready"), sem("sq_read")
        ms_ready, rms_ready, max_ready = sem("ms_ready"), sem("rms_ready"), sem("max_ready")
        st_psum, st_taken = sem("st_psum"), sem("st_taken")
        gate_psum, gelu_ready = sem("gate_psum"), sem("gelu_ready")
        logit_psum, shifted, exp_done = sem("logit_psum"), sem("shifted"), sem("exp_done")
        mix_ready, mixsq_ready, os_ready, ro_ready = sem("mix_ready"), sem("mixsq_ready"), sem("os_ready"), sem("ro_ready")
        o_ready = sem("o_ready")
        oT_psum, oT_taken = sem("oT_psum"), sem("oT_taken")
        out_psum = sem("out_psum")

        tok = [FSt, FLt, DEL, V]

        def by_chan(br, c):
            b, o = c * BANK // L, c * BANK % L
            if br == 2:
                return DELT[:, c * BANK:(c + 1) * BANK]
            if br == 3:
                return VP[:, b, PAD + o:PAD + o + BANK]
            return (FS, FL)[br][:, b, o:o + BANK]

        with nc.Block() as block:

            @block.tensor
            def _(pe):
                for i in range(3 * NG):
                    br, g = i // NG, i % NG
                    if i >= 4:
                        pe.wait_ge(tr_taken, i - 3)
                    for t in range(TB):
                        n = g * TB + t
                        src = DEL[:, n, :] if br == 2 else (FS, FL)[br][:, n * P // L, n * P % L:n * P % L + P]
                        tr = pe.transpose(banks[i % 4][:, t * P:(t + 1) * P], src, ident[:])
                    tr.then_inc(tr_psum, 1)
                pe.wait_ge(rms_ready, 1)
                pe.wait_ge(max_ready, NB)
                pe.wait_ge(tr_taken, 3 * NG)
                R = 2 * NB * NH
                for g in range(NG):
                    for t in range(TB):
                        tr = pe.transpose(banks[g % 4][0:R, t * P:(t + 1) * P],
                                          ST[:, g * TB + t, :, :, :].rearrange("p k b h -> p (k b h)"), ident[:])
                    tr.then_inc(st_psum, 1)
                for c in range(NG):
                    for hp in range(NP):
                        i = c * NP + hp
                        bank = banks[4 + i % 4]
                        cols = slice(c * BANK, (c + 1) * BANK)
                        if i >= 4:
                            pe.wait_ge(gelu_ready, i - 3)
                        pe.matmul(bank[:], cst["w1x"][:], XNT[:, cols], start=True, stop=False)
                        for br in range(NB):
                            pe.matmul(bank[:], cst["wbr"][:, br, hp, :], by_chan(br, c), start=False, stop=False)
                        pe.wait_ge(st_taken, c + 1)
                        pe.matmul(bank[:], cst["wst"][:, hp, :], STT[:, cols], start=False, stop=True).then_inc(gate_psum, 1)
                for t in range(NT):
                    for hp in range(NP):
                        pe.wait_ge(gelu_ready, t // TB * NP + NP)
                        o = t * NH * NB + hp * 2 * NB
                        mm = pe.matmul(banks[0][:, o:o + 2 * NB], G[:, hp, t * P:(t + 1) * P], cst["w2bd"][:], start=True, stop=True)
                mm.then_inc(logit_psum, 1)
                pe.wait_ge(o_ready, 1)
                for g in range(NG):
                    if g >= 2:
                        pe.wait_ge(oT_taken, g - 1)
                    for t in range(TB):
                        tr = pe.transpose(banks[1 + g % 2][:, t * P:(t + 1) * P], MIX[:, g * TB + t, :], ident[:])
                    tr.then_inc(oT_psum, 1)
                    pe.wait_ge(oT_taken, g + 1)
                    for t in range(TB):
                        n = g * TB + t
                        mm = pe.matmul(banks[4 + g][:, t * P:(t + 1) * P], OT[:, n * P:(n + 1) * P], cst["wo"][:], start=True, stop=True)
                    mm.then_inc(out_psum, 1)

            @block.scalar
            def _(act):
                dst = [FSt[:].rearrange("p t c -> p (t c)"), FLt[:].rearrange("p t c -> p (t c)"), DELT[:]]
                for k, br in enumerate((2, 3)):
                    act.activation(SQ[:, k, :, :], tok[br][:], ACT.Square).then_inc(sq_ready, 1)
                for i in range(3 * NG):
                    act.wait_ge(tr_psum, i + 1)
                    act.activation(dst[i // NG][:, i % NG * BANK:(i % NG + 1) * BANK], banks[i % 4][:], ACT.Copy).then_inc(tr_taken, 1)
                    if i in (NG, 2 * NG):
                        br = i // NG - 1
                        act.wait_ge(tr_taken, NG * (br + 1))
                        act.wait_ge(sq_read, br + 1)
                        act.activation(SQ[:, br, :, :], tok[br][:], ACT.Square).then_inc(sq_ready, 1)
                for g in range(NG):
                    act.wait_ge(st_psum, g + 1)
                    act.activation(STT[:, g * BANK:(g + 1) * BANK], banks[g % 4][0:2 * NB * NH, :], ACT.Copy).then_inc(st_taken, 1)
                for i in range(NG * NP):
                    act.wait_ge(gate_psum, i + 1)
                    c, hp = i // NP, i % NP
                    act.activation(G[:, hp, c * BANK:(c + 1) * BANK], banks[4 + i % 4][:], ACT.Gelu, bias=cst["gb1"][:, 0:1]).then_inc(gelu_ready, 1)
                act.wait_ge(shifted, 1)
                act.activation(ex[:], lg[:], ACT.Exp).then_inc(exp_done, 1)
                act.wait_ge(mix_ready, 1)
                act.activation(SQ[:, 0, :, :], MIX[:], ACT.Square).then_inc(mixsq_ready, 1)
                for g in range(NG):
                    act.wait_ge(oT_psum, g + 1)
                    act.activation(OT[:, g * BANK:(g + 1) * BANK], banks[1 + g % 2][:], ACT.Copy).then_inc(oT_taken, 1)

            @block.gpsimd
            def _(gp):
                gp.wait_ge(ms_ready, 1)
                gp.tensor_tensor(ST[:, :, 0, :, :].rearrange("p t b h -> p t (b h)"), ms[:].rearrange("p t b h -> p t (b h)"),
                                 cst["half"][:, 0:1].to_broadcast([P, NT * NB * NH]).rearrange("p (t r) -> p t r", t=NT), ALU.pow).then_inc(rms_ready, 1)
                gp.wait_ge(os_ready, 1)
                gp.tensor_tensor(ro[:], os_[:], cst["neghalf"][:, 0:1].to_broadcast([P, NT * NH]).rearrange("p (t h) -> p t h", t=NT), ALU.pow).then_inc(ro_ready, 1)

            @block.vector
            def _(ve):
                ch = Chain(ve, dve_step)

                def heads(ap):
                    return ap.rearrange("p t (h d) -> p t h d", h=NH)

                for k, br in enumerate((2, 3, 0, 1)):
                    if br < 2:
                        ve.wait_ge(tr_taken, NG * (br + 1))
                    ve.tensor_reduce(ST[:, :, 1, br, :], heads(tok[br][:]), AX.X, ALU.max).then_inc(max_ready, 1)
                    ve.wait_ge(sq_ready, k + 1)
                    ve.tensor_reduce(ms[:, :, br, :], heads(SQ[:, k % 2, :, :]), AX.X, ALU.add).then_inc(sq_read, 1)
                ve.wait_ge(sq_read, NB)
                ch.step(ve.tensor_scalar(ms[:], ms[:], 1.0 / DK, None, ALU.mult))
                ve.tensor_scalar(ms[:], ms[:], 1e-8, None, ALU.max).then_inc(ms_ready, 1)

                def ebc(ap):
                    return ap.unsqueeze(3).to_broadcast([P, NT, NH, NB])
                flat = [P, NT * NH, NB]

                def f3(ap):
                    return ap.rearrange("p t h b -> p (t h) b")

                def e3(ap):
                    return ap.rearrange("p t h -> p (t h)").unsqueeze(2).to_broadcast(flat)
                ve.wait_ge(logit_psum, 1)
                ch.step(ve.tensor_tensor(f3(lg[:]), banks[0][:, 0:NT * NH * NB].rearrange("p (r b) -> p r b", b=NB),
                                         cst["gb2"][:].unsqueeze(1).to_broadcast(flat), ALU.add))
                ch.step(ve.tensor_tensor(lg[:], lg[:], cst["rtemp"][:].unsqueeze(1).unsqueeze(3).to_broadcast([P, NT, NH, NB]), ALU.mult))
                ch.step(ve.tensor_reduce(mx[:], lg[:], AX.X, ALU.max))
                ve.tensor_tensor(f3(lg[:]), f3(lg[:]), e3(mx[:]), ALU.subtract).then_inc(shifted, 1)
                ve.wait_ge(exp_done, 1)
                ch.step(ve.tensor_reduce(mx[:], ex[:], AX.X, ALU.add))
                ch.step(ve.reciprocal(mx[:], mx[:]))
                ch.step(ve.tensor_tensor(f3(ex[:]), f3(ex[:]), e3(mx[:]), ALU.mult))
                ch.step(ve.tensor_tensor(ex[:].rearrange("p t h b -> p t (h b)"), ex[:].rearrange("p t h b -> p t (h b)"),
                                         cst["floor"][:].rearrange("p h b -> p (h b)").unsqueeze(1).to_broadcast([P, NT, NH * NB]), ALU.max))
                ch.step(ve.tensor_reduce(mx[:], ex[:], AX.X, ALU.add))
                ch.step(ve.reciprocal(mx[:], mx[:]))
                ch.step(ve.tensor_tensor(f3(ex[:]), f3(ex[:]), e3(mx[:]), ALU.mult))

                def h3(ap):
                    return ap.rearrange("p t (h d) -> p (t h) d", h=NH)

                def weight(br):
                    return ex[:].rearrange("p t h b -> p (t h) b")[:, :, br:br + 1].to_broadcast([P, NT * NH, DK])

                ch.link(ve.tensor_tensor(h3(MIX[:]), h3(tok[0][:]), weight(0), ALU.mult))
                for br in range(1, NB):
                    ch.step(ve.tensor_tensor(h3(TMP[:, br % 2, :, :]), h3(tok[br][:]), weight(br), ALU.mult))
                    ins = ve.tensor_tensor(MIX[:], MIX[:], TMP[:, br % 2, :, :], ALU.add)
                    if br < NB - 1:
                        ch.link(ins)
                    else:
                        ins.then_inc(mix_ready, 1)
                ve.wait_ge(mixsq_ready, 1)
                ch.step(ve.tensor_reduce(os_[:], heads(SQ[:, 0, :, :]), AX.X, ALU.add))
                ve.tensor_scalar(os_[:], os_[:], 1.0 / DK, 1e-5, ALU.mult, ALU.add).then_inc(os_ready, 1)
                ve.wait_ge(ro_ready, 1)
                ve.tensor_tensor(h3(MIX[:]), h3(MIX[:]), ro[:].rearrange("p t h -> p (t h)").unsqueeze(2).to_broadcast([P, NT * NH, DK]), ALU.mult).then_inc(o_ready, 1)
                for g in range(NG):
                    ve.wait_ge(out_psum, g + 1)
                    ve.tensor_tensor(X[:, g * TB:(g + 1) * TB, :], X[:, g * TB:(g + 1) * TB, :], banks[4 + g][:].rearrange("p (t c) -> p t c", c=P), ALU.add)


def attn_consts(nc, cst, a, banks, NH):
    C, DK, NB, NP = 32, P // NH, 4, NH // 2
    HID = P
    U_ = a["L0_attn_gW1"].shape[1]
    with ExitStack() as ctx:
        def sb(name, shape, dt=F32):
            return ctx.enter_context(nc.sbuf_tensor(f"c_{name}", shape, dt))

        def sem(name):
            return ctx.enter_context(nc.semaphore(f"c_{name}"))
        wm, wr, wx = (sb(n, [P, NB, NP, P]) for n in ("wm", "wr", "wx"))
        sel = sb("sel", [P, 8, 8, NH])
        onrep = sb("onrep", [P, 1])
        full = sb("full", [P, 5, P])
        zeroed, loaded, step, masks, dstep, ps = sem("zeroed"), sem("loaded"), sem("step"), sem("masks"), sem("dstep"), sem("ps")
        wbr = cst["wbr"]
        NLOAD = [0]
        with nc.Block() as block:
            @block.sync
            def _(sp):
                def ld(dst, src):
                    sp.dma_start(dst, src).then_inc(loaded, 16)
                    NLOAD[0] += 16
                for w, n in enumerate(("q", "k", "v")):
                    ld(cst["wqkv"][:, w, :], a[f"L0_attn_W{n}"])
                    ld(cst["convw"][:, w, :], a[f"L0_attn_{n}c_w"])
                ld(cst["wb"][:], a["L0_attn_Wb"])
                ld(cst["firs"][:], a["L0_attn_fir_s"].rearrange("h d k -> (h d) k"))
                ld(cst["firl"][:], a["L0_attn_fir_l"].rearrange("h d k -> (h d) k"))
                gw1 = a["L0_attn_gW1"]
                for i in range(2):
                    ld(cst["w1x"][:, i * U_:(i + 1) * U_], gw1[0:HID, :])
                    ld(cst["gb1"][i * U_:(i + 1) * U_, :], a["L0_attn_gb1"].rearrange("(u o) -> u o", o=1))
                ld(cst["gb2"][:], a["L0_attn_gb2"].partition_broadcast(P))
                ld(cst["rtemp"][:], a["L0_attn_temp"].partition_broadcast(P))
                ld(cst["floor"][:].rearrange("p h b -> p (h b)"), a["L0_attn_eps_floor"].rearrange("h b -> (h b)").partition_broadcast(P))
                ld(cst["wo"][:], a["L0_attn_Wo"])
                for h in range(NH):
                    ld(onrep[h * DK:(h + 1) * DK, :], a["L0_attn_onorm_w"].rearrange("(d o) -> d o", o=1))
                sp.wait_ge(zeroed, 5)
                for i in range(2):
                    ld(cst["w2bd"][i * U_:(i + 1) * U_, i * NB:(i + 1) * NB], a["L0_attn_gW2"])
                stat = gw1[HID:HID + 3 * NB * DK, :].rearrange("(b k d) u -> k d b u", b=NB, k=3)
                for h in range(NH):
                    rows, cols = slice(h * DK, (h + 1) * DK), slice(h % 2 * U_, (h % 2 + 1) * U_)
                    for k, dst in enumerate((wm, wr, wx)):
                        ld(dst[rows, :, h // 2, cols], stat[k])
                    ld(wbr[rows, :, h // 2, cols], gw1[HID + 3 * NB * DK:, :].rearrange("(b d) u -> d b u", b=NB))

            @block.gpsimd
            def _(gp):
                n = [0]

                def sel_(dst, src, op, base, pattern, cm, last=False):
                    gp.wait_ge(step, n[0])
                    gp.affine_select(out=dst, in_=src, compare_op=op, fill=0.0, base=base, pattern=pattern,
                                     channel_multiplier=cm).then_inc(step, 1)
                    n[0] += 1
                gp.memset(cst["half"][:], 0.5)
                gp.memset(cst["blk"][:], 1.0)
                gp.memset(full[:, 1:4, :], 0.0)
                gp.memset(full[:, 4, :], 0.0)
                gp.memset(full[:, 0, :], 1.0)
                gp.memset(sel[:], 0.0).then_inc(step, 1)
                n[0] += 1
                gp.wait_ge(step, 1)
                for i in range(8):
                    gp.memset(sel[:, i, i, :], 1.0)
                for i in range(3):
                    s = 8 << i
                    ms_ = gp.memset(full[:, 1 + i, :].rearrange("p (b s) -> p b s", s=s)[:, :, 0:s // 2], 1.0)
                ms_.then_inc(step, 1)
                n[0] += 1
                v = sel[:].rearrange("p a b h -> p (a b) h")
                sel_(v, v, ALU.is_ge, 0, [[0, 64], [-DK, NH]], 1)
                sel_(v, v, ALU.is_ge, DK - 1, [[0, 64], [DK, NH]], -1)
                v = cst["blk"][:].rearrange("p (b c) -> p b c", c=C)
                sel_(v, v, ALU.is_ge, 0, [[-C, 4], [0, C]], 1)
                sel_(v, v, ALU.is_ge, C - 1, [[C, 4], [0, C]], -1)
                sel_(cst["mmask"][:], cst["blk"][:], ALU.is_ge, 0, [[1, P]], -1)
                sel_(cst["atmask"][:], cst["blk"][:], ALU.is_gt, 0, [[1, P]], -1)
                v = full[:, 0, :].rearrange("p (b c) -> p b c", c=4)
                sel_(v, v, ALU.is_ge, 3, [[4, P // 4], [0, 4]], -1)
                sel_(v, v, ALU.is_gt, 0, [[-4, P // 4], [-1, 4]], 1)
                for i in range(3):
                    s = 8 << i
                    v = full[:, 1 + i, :].rearrange("p (b s) -> p b s", s=s)[:, :, 0:s // 2]
                    sel_(v, v, ALU.is_ge, -s // 2, [[-s, P // s], [0, s // 2]], 1)
                    sel_(v, v, ALU.is_ge, s - 1, [[s, P // s], [0, s // 2]], -1)
                gp.wait_ge(step, n[0])
                gp.tensor_copy(full[:, 4, :], cst["ident"][:]).then_inc(masks, 1)

            @block.vector
            def _(ve):
                ch = Chain(ve, dstep)
                for z in (wm, wr, wx, wbr):
                    ve.memset(z[:], 0.0).then_inc(zeroed, 1)
                ve.memset(cst["w2bd"][:], 0.0).then_inc(zeroed, 1)
                ve.wait_ge(masks, 1)
                for i in range(5):
                    dst = cst["lmask"][:, i, :] if i < 4 else cst["istack"][:]
                    ve.tensor_reduce(dst, full[:, i, :].rearrange("p (b c) -> p c b", c=C), AX.X, ALU.add)
                ve.tensor_scalar(cst["atmask"][:], cst["atmask"][:], -1.0, None, ALU.mult)
                ve.wait_ge(loaded, NLOAD[0])
                ch.step(ve.tensor_scalar(cst["rtemp"][:], cst["rtemp"][:], 0.2, 10.0, ALU.max, ALU.min))
                ve.reciprocal(cst["rtemp"][:], cst["rtemp"][:])
                ve.tensor_scalar(cst["floor"][:], cst["floor"][:], 1e-7, 0.1, ALU.max, ALU.min)
                ve.tensor_scalar(cst["wo"][:], cst["wo"][:], onrep[:, 0:1], None, ALU.mult)
                ve.wait_ge(ps, 1)
                for i in range(2):
                    w = wbr[:].rearrange("p b n u -> p (b n u)")[:, i * BANK:(i + 1) * BANK]
                    ve.scalar_tensor_tensor(w, banks[i][:], 1.0 / DK, w, ALU.mult, ALU.add)
                ve.tensor_copy(cst["wst"][:].rearrange("p n u -> p (n u)"), banks[2][0:8 * NH, 0:NP * P])

            @block.tensor
            def _(pe):
                pe.wait_ge(masks, 1)
                pe.wait_ge(loaded, NLOAD[0])
                for i in range(2):
                    pe.matmul(banks[i][:], cst["blk"][:], wm[:].rearrange("p b n u -> p (b n u)")[:, i * BANK:(i + 1) * BANK], start=True, stop=True)
                for i in range(8):
                    w = (wr, wx)[i // NB]
                    mm = pe.matmul(banks[2][0:8 * NH, 0:NP * P], sel[:, i, :, :].rearrange("p b h -> p (b h)"),
                                   w[:, i % NB, :, :].rearrange("p n u -> p (n u)"), start=(i == 0), stop=(i == 7))
                mm.then_inc(ps, 1)


def program(nc, a):
    x, out = a["L0_attn_x"], a["out"]
    B, L, D = x.shape
    NT = B * L // P
    NE, _, F = a["L0_ffn_w1"].shape
    FC = F // P
    MAXT = NT + NE - 1
    NH = a["L0_attn_Wb"].shape[1]
    with ExitStack() as ctx:
        def sb(name, shape, dt=F32):
            return ctx.enter_context(nc.sbuf_tensor(name, shape, dt))

        def sem(name):
            return ctx.enter_context(nc.semaphore(name))

        banks = [ctx.enter_context(nc.psum_tensor(f"bank{i}", [P, BANK], F32)) for i in range(8)]
        X = sb("X", [P, NT, D])
        XN = sb("XN", [P, NT, D])
        XNT = sb("XNT", [P, NT * P])
        b1rows = sb("b1rows", [NE * FC, P])
        b1T = sb("b1T", [P, NE, FC])
        cst = {
            "ident": sb("ident", [P, P]), "before": sb("before", [P, P]), "ones": sb("ones", [P, P]),
            "gw": sb("gw", [P, NE]), "gb": sb("gb", [P, NE]), "neghalf": sb("neghalf", [P, 1]),
            "falling": sb("falling", [P, NE]), "tilestart": sb("tilestart", [P, NT]), "tileno": sb("tileno", [P, MAXT]),
            "half": sb("half", [P, 1]), "blk": sb("blk", [P, P]), "mmask": sb("mmask", [P, P]), "atmask": sb("atmask", [P, P]),
            "lmask": sb("lmask", [P, 4, 32]), "istack": sb("istack", [P, 32]),
            "wqkv": sb("wqkv", [P, 3, P]), "convw": sb("convw", [P, 3, 4]), "wb": sb("wb", [P, NH]),
            "firs": sb("firs", [P, a["L0_attn_fir_s"].shape[2]]), "firl": sb("firl", [P, a["L0_attn_fir_l"].shape[2]]),
            "w1x": sb("w1x", [P, P]), "gb1": sb("gb1", [P, 1]), "gb2": sb("gb2", [P, 4]), "rtemp": sb("rtemp", [P, NH]),
            "floor": sb("floor", [P, NH, 4]), "wo": sb("wo", [P, P]), "w2bd": sb("w2bd", [P, 8]),
            "wbr": sb("wbr", [P, 4, 2, P]), "wst": sb("wst", [32, 2, P]),
        }
        zrow = sb("zrow", [P, D])
        xsort = nc.dram_tensor("xsort", (MAXT * P, D), F32, kind="Internal").ap()
        ysort = nc.dram_tensor("ysort", (MAXT * P, D), F32, kind="Internal").ap()
        mem = {"X": X, "XN": XN, "XNT": XNT, "b1T": b1T, "a": a, "xsort": xsort, "ysort": ysort}
        x_in, small_in, pad_zero, pool_step, consts, b1_psum, stored = (sem(n) for n in (
            "x_in", "small_in", "pad_zero", "pool_step", "consts", "b1_psum", "stored"))

        with nc.Block() as block:
            @block.sync
            def _(sp):
                sp.dma_start(X[:], x.rearrange("b (n p) d -> p (b n) d", p=P)).then_inc(x_in, 16)
                sp.wait_ge(x_in, 16)
                sp.wait_ge(pad_zero, 16)

            @block.scalar
            def _(act):
                act.dma_start(b1rows[:], a["L0_ffn_b1"].rearrange("e (j f) -> (e j) f", f=P)).then_inc(small_in, 16)
                act.dma_start(cst["gw"][:], a["L0_ffn_gate_w"]).then_inc(small_in, 16)
                act.dma_start(cst["gb"][:], a["L0_ffn_gate_b"].partition_broadcast(P)).then_inc(small_in, 16)
                act.wait_ge(pool_step, 2)
                act.dma_start(xsort.rearrange("(t p) d -> p t d", p=P),
                              zrow[:].unsqueeze(1).to_broadcast([P, MAXT, D])).then_inc(pad_zero, 16)
                act.wait_ge(b1_psum, 1)
                act.activation(b1T[:].rearrange("p e j -> p (e j)"), banks[7][:, 0:NE * FC], ACT.Copy)

            @block.gpsimd
            def _(gp):
                gp.memset(cst["ident"][:], 0.0).then_inc(pool_step, 1)
                gp.memset(zrow[:], 0.0).then_inc(pool_step, 1)
                gp.memset(cst["ones"][:], 1.0).then_inc(pool_step, 1)
                gp.memset(cst["neghalf"][:], -0.5)
                gp.iota(cst["falling"][:], [[-1, NE]], base=NE, channel_multiplier=0, allow_small_or_imprecise_dtypes=True)
                gp.iota(cst["tilestart"][:], [[P, NT]], base=0, channel_multiplier=0, allow_small_or_imprecise_dtypes=True)
                gp.iota(cst["tileno"][:], [[1, MAXT]], base=0, channel_multiplier=0, allow_small_or_imprecise_dtypes=True)
                gp.wait_ge(pool_step, 3)
                gp.affine_select(out=cst["ident"][:], in_=cst["ident"][:], compare_op=ALU.not_equal, fill=1.0,
                                 base=0, pattern=[[-1, P]], channel_multiplier=1).then_inc(consts, 1)
                gp.affine_select(out=cst["before"][:], in_=cst["ones"][:], compare_op=ALU.is_gt, fill=0.0,
                                 base=0, pattern=[[1, P]], channel_multiplier=-1).then_inc(consts, 1)

            @block.tensor
            def _(pe):
                pe.wait_ge(small_in, 48)
                pe.wait_ge(consts, 2)
                pe.transpose(banks[7][:, 0:NE * FC], b1rows[:], cst["ident"][0:NE * FC, 0:NE * FC]).then_inc(b1_psum, 1)

        attn_consts(nc, cst, a, banks, NH)
        moe_ffn(nc, 0, cst, mem, banks, NT, NE, F)
        with ExitStack() as attn:
            PAD = a["L0_attn_fir_l"].shape[2] - 1

            def ab(name, shape):
                mem[name] = attn.enter_context(nc.sbuf_tensor(name, shape, F32))
            ab("VP", [P, B, PAD + L])
            for name in ("FS", "FL"):
                ab(name, [P, B, L])
            for name in ("V", "DEL"):
                ab(name, [P, NT, P])
            with ExitStack() as delta:
                def db(name, shape):
                    mem[name] = delta.enter_context(nc.sbuf_tensor(name, shape, F32))
                for name in ("QT", "KT", "KBT"):
                    db(name, [P, NT * P])
                for name in ("K", "KB", "VB"):
                    db(name, [P, NT, P])
                attn_project(nc, cst, mem, banks, B, L, NH)
                attn_delta(nc, cst, mem, banks, B, L, NH)
            attn_mix(nc, cst, mem, banks, B, L, NH)
        moe_ffn(nc, 1, cst, mem, banks, NT, NE, F)

        with nc.Block() as block:
            @block.sync
            def _(sp):
                sp.dma_start(out.rearrange("b (n p) d -> p (b n) d", p=P), X[:]).then_inc(stored, 16)
                sp.wait_ge(stored, 16)


_INS = ['L0_attn_x', 'L0_attn_Wq', 'L0_attn_Wk', 'L0_attn_Wv', 'L0_attn_Wb', 'L0_attn_qc_w', 'L0_attn_kc_w',
        'L0_attn_vc_w', 'L0_attn_fir_s', 'L0_attn_fir_l', 'L0_attn_gW1', 'L0_attn_gb1', 'L0_attn_gW2', 'L0_attn_gb2',
        'L0_attn_temp', 'L0_attn_eps_floor', 'L0_attn_onorm_w', 'L0_attn_Wo', 'L0_ffn_gate_w', 'L0_ffn_gate_b',
        'L0_ffn_w1', 'L0_ffn_b1', 'L0_ffn_w2', 'L0_ffn_b2']


def kernel(**inputs):
    import numpy as np
    import concourse.bacc as bacc
    from concourse.bass_utils import run_bass_kernel_spmd as run

    nc = bacc.Bacc("TRN2", target_bir_lowering=False, num_devices=1)
    arrays, aps = {}, {}
    for name in _INS:
        v = np.ascontiguousarray(inputs[name])
        arrays["in_" + name] = v
        aps[name] = nc.dram_tensor("in_" + name, v.shape, mybir.dt.from_np(v.dtype), kind="ExternalInput").ap()
    aps["out"] = nc.dram_tensor("out_0", inputs['L0_attn_x'].shape, F32, kind="ExternalOutput").ap()
    program(nc, aps)
    r = run(nc, [arrays], core_ids=[0])
    return r.results[0]["out_0"]
```

```python
from contextlib import ExitStack

import concourse.bass as bass
from concourse import mybir

F32 = mybir.dt.float32
I32 = mybir.dt.int32
ALU = mybir.AluOpType
ACT = mybir.ActivationFunctionType
AX = mybir.AxisListType

P = 128
BANK = 512
LN_EPS = 1e-5


class Chain:

    def __init__(self, eng, sem):
        self.eng, self.sem, self.n = eng, sem, 0

    def link(self, ins):
        self.n += 1
        ins.then_inc(self.sem, 1)
        return ins

    def wait(self):
        self.eng.wait_ge(self.sem, self.n)

    def step(self, ins):
        self.link(ins)
        self.wait()


def moe_ffn(nc, rep, cst, mem, banks, NT, NE, F):
    D = P
    FC = F // P
    MAXT = NT + NE - 1
    groups = [(g, min(4, MAXT - g)) for g in range(0, MAXT, 4)]
    X, b1T, a = mem["X"], mem["b1T"], mem["a"]
    XN, XNT = mem["XN"], mem["XNT"]
    xsort, ysort = mem["xsort"], mem["ysort"]
    ident, before, ones, gw, gb = cst["ident"], cst["before"], cst["ones"], cst["gw"], cst["gb"]
    with ExitStack() as ctx:
        def sb(name, shape, dt=F32):
            return ctx.enter_context(nc.sbuf_tensor(f"{name}_{rep}", shape, dt))

        def sem(name):
            return ctx.enter_context(nc.semaphore(f"{name}_{rep}"))

        W1 = sb("W1", [P, NE, F])
        W2 = sb("W2", [P, NE, FC, D])
        b2bc = sb("b2bc", [P, NE, D])
        weights_in = sem("weights_in")
        stats = sb("stats", [P, NT, 6])
        mv = sb("mv", [P, NT, 2])
        vare = sb("vare", [P, NT])
        rstd = sb("rstd", [P, NT])
        lg = sb("lg", [P, NT, NE])
        ex = sb("ex", [P, NT, NE])
        pb = sb("pb", [P, NT, NE])
        onehot = sb("onehot", [P, NT, NE])
        mx = sb("mx", [P, NT])
        den = sb("den", [P, NT])
        rden = sb("rden", [P, NT])
        pmax = sb("pmax", [P, NT])
        first = sb("first", [P, NT])
        wtok = sb("wtok", [P, NT])
        tot = sb("tot", [P, NE, NT])
        cum = sb("cum", [P, 1 + NE * NT])
        zero = sb("zero", [P, NE * NT])
        base = sb("base", [P, NE, NT])
        cnt = sb("cnt", [P, NE])
        over = sb("over", [P, NE, NT])
        ntile = sb("ntile", [P, NE])
        tend = sb("tend", [P, 1 + NE])
        goff = sb("goff", [P, NE])
        slot = sb("slot", [P, NT, NE])
        posf = sb("posf", [P, NT])
        pos = sb("pos", [P, NT], I32)
        past = sb("past", [P, MAXT, NE])
        eoff = sb("eoff", [P, MAXT])
        etile = sb("etile", [P, MAXT], I32)
        xs = sb("xs", [P, MAXT, D])
        xT = sb("xT", [P, MAXT, P])
        w1s = sb("w1s", [P, 2, F])
        b1s = sb("b1s", [P, 2, FC])
        hT = sb("hT", [P, 2, FC, P])
        Y = sb("Y", [P, MAXT, D])
        G = sb("G", [P, NT, D])

        dve_step = sem("dve_step")
        var_ready = sem("var_ready")
        rstd_ready = sem("rstd_ready")
        xn_ready = sem("xn_ready")
        xnT_psum = sem("xnT_psum")
        xnT_ready = sem("xnT_ready")
        gate_done = sem("gate_done")
        shifted = sem("shifted")
        exp_done = sem("exp_done")
        onehot_ready = sem("onehot_ready")
        ranks_done = sem("ranks_done")
        pos_ready = sem("pos_ready")
        etile_ready = sem("etile_ready")
        scattered = sem("scattered")
        x_loaded = [sem(f"x_loaded{c}") for c in range(len(groups))]
        xT_psum = sem("xT_psum")
        xT_ready = sem("xT_ready")
        w1_staged = sem("w1_staged")
        h_psum = sem("h_psum")
        h_ready = sem("h_ready")
        y_psum = sem("y_psum")
        y_ready = sem("y_ready")
        y_stored = sem("y_stored")
        gathered = [sem(f"gathered{c}") for c in range(NT // 4)]

        pT, pR, pRank, pTot = banks[0:2], banks[2], banks[3], banks[4]
        pX, pH, pY = banks[0:2], banks[2:4], banks[4:6]
        NC = NT // 4

        with nc.Block() as block:

            @block.sync
            def _(sp):
                sp.dma_start(W1[:], a["L0_ffn_w1"].rearrange("e d f -> d e f")).then_inc(weights_in, 16)
                sp.dma_start(W2[:], a["L0_ffn_w2"].rearrange("e (j f) d -> f e j d", f=P)).then_inc(weights_in, 16)
                sp.dma_start(b2bc[:], a["L0_ffn_b2"].partition_broadcast(P)).then_inc(weights_in, 16)
                sp.wait_ge(scattered, 16 * NT)
                for c, (g, n) in enumerate(groups):
                    sp.dma_start(xs[:, g:g + n, :], xsort[g * P:(g + n) * P, :].rearrange("(t p) d -> p t d", p=P))\
                      .then_inc(x_loaded[c], 16)
                with sp.Fori(0, MAXT) as t:
                    sp.wait_ge(y_ready, t + 1)
                    sp.dma_start(ysort[bass.ds(t * P, P), :], Y[:, bass.ds(t, 1), :]).then_inc(y_stored, 16)

            @block.gpsimd
            def _(gp):
                gp.wait_ge(var_ready, 1)
                gp.tensor_tensor(rstd[:], vare[:], cst["neghalf"][:, 0:1].to_broadcast([P, NT]), ALU.pow).then_inc(rstd_ready, 1)
                gp.wait_ge(pos_ready, 1)
                for t in range(NT):
                    gp.indirect_dma_start(xsort, bass.IndirectOffsetOnAxis(pos[:, t:t + 1], 0),
                                          XN[:, t, :], None).then_inc(scattered, 16)

                gp.wait_ge(y_stored, 16 * MAXT)
                for t in range(NT):
                    gp.indirect_dma_start(G[:, t, :], None, ysort,
                                          bass.IndirectOffsetOnAxis(pos[:, t:t + 1], 0)).then_inc(gathered[t // 4], 16)

            @block.tensor
            def _(pe):
                for t in range(NT):
                    pe.wait_ge(xn_ready, t + 1)
                    if t % 4 == 0 and t >= 8:
                        pe.wait_ge(xnT_ready, t // 4 - 1)
                    tr = pe.transpose(pT[t // 4 % 2][:, t % 4 * P:(t % 4 + 1) * P], XN[:, t, :], ident[:])
                    if t % 4 == 3:
                        tr.then_inc(xnT_psum, 1)
                for t in range(NT):
                    if t % 4 == 0:
                        pe.wait_ge(xnT_ready, t // 4 + 1)
                    mm = pe.matmul(pR[:, t * NE:(t + 1) * NE], XNT[:, t * P:(t + 1) * P], gw[:], start=True, stop=True)
                mm.then_inc(gate_done, 1)
                pe.wait_ge(onehot_ready, 1)
                pe.matmul(pRank[:, 0:NT * NE], before[:], onehot[:], start=True, stop=True)
                pe.matmul(pTot[:, 0:NT * NE], ones[:], onehot[:], start=True, stop=True).then_inc(ranks_done, 1)
                pe.wait_ge(etile_ready, 1)
                pe.wait_ge(weights_in, 48)

                for c, (g, n) in enumerate(groups):
                    pe.wait_ge(x_loaded[c], 16)
                    if c >= 2:
                        pe.wait_ge(xT_ready, c - 1)
                    for t in range(n):
                        tr = pe.transpose(pX[c % 2][:, t * P:(t + 1) * P], xs[:, g + t, :], ident[:])
                    tr.then_inc(xT_psum, 1)
                pe.wait_ge(xT_ready, len(groups))

                def up(t, s, reuse):
                    pe.wait_ge(w1_staged, t + 1)
                    if reuse:
                        pe.wait_ge(h_ready, FC * t - FC)
                    for j in range(FC):
                        mm = pe.matmul(pH[s][:, j * P:(j + 1) * P], w1s[:, s, j * P:(j + 1) * P],
                                       xT[:, bass.ds(t, 1), :], start=True, stop=True)
                    mm.then_inc(h_psum, 1)

                def down(t, s, reuse):
                    pe.wait_ge(h_ready, FC * t + FC)
                    if reuse:
                        pe.wait_ge(y_ready, t - 1)
                    e = pe.value_load(etile[0:1, bass.ds(t, 1)], min_val=0, max_val=NE - 1)
                    for j in range(FC):
                        mm = pe.matmul(pY[s][:, 0:D], hT[:, s, j, :], W2[:, bass.ds(e, 1), j, :],
                                       start=(j == 0), stop=(j == FC - 1))
                    mm.then_inc(y_psum, 1)

                up(0, 0, False)
                up(1, 1, False)
                down(0, 0, False)
                up(2, 0, True)
                down(1, 1, False)
                with pe.Fori(3, MAXT - 1, 2) as i:
                    for s in (1, 0):
                        up(i + 1 - s, s, True)
                        down(i - s, 1 - s, True)
                down(MAXT - 1, 0, True)

            @block.scalar
            def _(act):
                for c in range(NC):
                    act.wait_ge(xnT_psum, c + 1)
                    act.activation(XNT[:, c * BANK:(c + 1) * BANK], pT[c % 2][:], ACT.Copy).then_inc(xnT_ready, 1)
                act.wait_ge(shifted, 1)
                act.activation(ex[:], lg[:], ACT.Exp).then_inc(exp_done, 1)

                def gelu(t, s, reuse):
                    act.wait_ge(h_psum, t + 1)
                    if reuse:
                        act.wait_ge(y_psum, t - 1)
                    for j in range(FC):
                        act.activation(hT[:, s, j, :], pH[s][:, j * P:(j + 1) * P], ACT.Gelu,
                                       bias=b1s[:, s, j:j + 1]).then_inc(h_ready, 1)

                gelu(0, 0, False)
                gelu(1, 1, False)
                with act.Fori(2, MAXT - 1, 2) as i:
                    for s in range(2):
                        gelu(i + s, s, True)
                gelu(MAXT - 1, 0, True)

            @block.vector
            def _(ve):
                ch = Chain(ve, dve_step)
                for t in range(NT):
                    bs = ve.bn_stats(stats[:, t, :], X[:, t, :])
                ch.step(bs)
                for t in range(NT):
                    ag = ve.bn_aggr(mv[:, t, :], stats[:, t, :])
                ch.step(ag)
                ve.tensor_scalar(vare[:], mv[:, :, 1], LN_EPS, None, ALU.add).then_inc(var_ready, 1)
                ve.wait_ge(rstd_ready, 1)
                for t in range(NT):
                    ve.tensor_scalar(XN[:, t, :], X[:, t, :], mv[:, t, 0:1], rstd[:, t:t + 1],
                                     ALU.subtract, ALU.mult).then_inc(xn_ready, 1)

                def ebc(ap):
                    return ap.unsqueeze(2).to_broadcast([P, NT, NE])

                ch.step(ve.memset(zero[:], 0.0))
                ve.wait_ge(gate_done, 1)
                ch.step(ve.tensor_tensor(lg[:], pR[:, 0:NT * NE].rearrange("p (t e) -> p t e", e=NE),
                                         gb[:].unsqueeze(1).to_broadcast([P, NT, NE]), ALU.add))
                ch.step(ve.tensor_reduce(mx[:], lg[:], AX.X, ALU.max))
                ve.tensor_tensor(lg[:], lg[:], ebc(mx[:]), ALU.subtract).then_inc(shifted, 1)
                ve.wait_ge(exp_done, 1)
                ch.step(ve.tensor_reduce(den[:], ex[:], AX.X, ALU.add))
                ch.step(ve.reciprocal(rden[:], den[:]))
                ch.step(ve.tensor_tensor(pb[:], ex[:], ebc(rden[:]), ALU.mult))
                ch.step(ve.tensor_reduce(pmax[:], pb[:], AX.X, ALU.max))
                ve.tensor_scalar(wtok[:], pmax[:], 0.5, None, ALU.mult)
                ch.step(ve.tensor_tensor(pb[:], pb[:], ebc(pmax[:]), ALU.is_ge))
                ch.step(ve.tensor_tensor(pb[:], pb[:], cst["falling"][:].unsqueeze(1).to_broadcast([P, NT, NE]), ALU.mult))
                ch.step(ve.tensor_reduce(first[:], pb[:], AX.X, ALU.max))
                ve.tensor_tensor(onehot[:], pb[:], ebc(first[:]), ALU.is_equal).then_inc(onehot_ready, 1)
                ve.wait_ge(ranks_done, 1)
                ch.step(ve.tensor_copy(tot[:].rearrange("p e t -> p t e"), pTot[:, 0:NT * NE].rearrange("p (t e) -> p t e", e=NE)))
                ch.step(ve.memset(cum[:, 0:1], 0.0))
                ch.step(ve.tensor_tensor_scan(cum[:, 1:1 + NE * NT], tot[:].rearrange("p e t -> p (e t)"), zero[:], 0.0, ALU.add, ALU.add))
                C = cum[:, 1:1 + NE * NT].rearrange("p (e t) -> p e t", t=NT)
                ends, starts = C[:, :, NT - 1], cum[:, 0:NE * NT].rearrange("p (e t) -> p e t", t=NT)[:, :, 0]
                ch.step(ve.tensor_tensor(cnt[:], ends, starts, ALU.subtract))
                ch.step(ve.tensor_tensor(over[:], cnt[:].unsqueeze(2).to_broadcast([P, NE, NT]),
                                         cst["tilestart"][:].unsqueeze(1).to_broadcast([P, NE, NT]), ALU.is_gt))
                ch.step(ve.tensor_reduce(ntile[:], over[:], AX.X, ALU.add))
                ch.step(ve.memset(tend[:, 0:1], 0.0))
                ch.step(ve.tensor_tensor_scan(tend[:, 1:1 + NE], ntile[:], zero[:, 0:NE], 0.0, ALU.add, ALU.add))
                ch.step(ve.scalar_tensor_tensor(goff[:], tend[:, 0:NE], float(P), starts, ALU.mult, ALU.subtract))
                ch.step(ve.tensor_tensor(base[:], C, tot[:], ALU.subtract))
                ch.step(ve.tensor_tensor(base[:], base[:], goff[:].unsqueeze(2).to_broadcast([P, NE, NT]), ALU.add))
                ch.step(ve.tensor_tensor(slot[:], pRank[:, 0:NT * NE].rearrange("p (t e) -> p t e", e=NE),
                                         base[:].rearrange("p e t -> p t e"), ALU.add))
                ch.step(ve.tensor_tensor(slot[:], slot[:], onehot[:], ALU.mult))
                ch.step(ve.tensor_reduce(posf[:], slot[:], AX.X, ALU.add))
                ve.tensor_copy(pos[:], posf[:]).then_inc(pos_ready, 1)
                ch.step(ve.tensor_tensor(past[:], cst["tileno"][:].unsqueeze(2).to_broadcast([P, MAXT, NE]),
                                         tend[:, 1:1 + NE].unsqueeze(1).to_broadcast([P, MAXT, NE]), ALU.is_ge))
                ch.step(ve.tensor_reduce(eoff[:], past[:], AX.X, ALU.add))
                ch.step(ve.tensor_scalar(eoff[:], eoff[:], float(NE - 1), None, ALU.min))
                ve.tensor_copy(etile[:], eoff[:]).then_inc(etile_ready, 1)

                def stage(t, s, reuse):
                    if reuse:
                        ve.wait_ge(h_psum, t - 1)
                        ve.wait_ge(h_ready, FC * t - FC)
                    e = ve.value_load(etile[0:1, bass.ds(t, 1)], min_val=0, max_val=NE - 1)
                    ve.tensor_copy(b1s[:, s, :], b1T[:, bass.ds(e, 1), :])
                    ve.tensor_copy(w1s[:, s, :], W1[:, bass.ds(e, 1), :]).then_inc(w1_staged, 1)

                def take_y(t, s):
                    ve.wait_ge(y_psum, t + 1)
                    e = ve.value_load(etile[0:1, bass.ds(t, 1)], min_val=0, max_val=NE - 1)
                    ve.tensor_tensor(Y[:, bass.ds(t, 1), :], pY[s][:, 0:D], b2bc[:, bass.ds(e, 1), :], ALU.add).then_inc(y_ready, 1)

                ve.wait_ge(etile_ready, 1)
                ve.wait_ge(weights_in, 48)
                stage(0, 0, False)
                stage(1, 1, False)
                for c, (g, n) in enumerate(groups):
                    ve.wait_ge(xT_psum, c + 1)
                    ve.tensor_copy(xT[:, g:g + n, :], pX[c % 2][:, 0:n * P].rearrange("p (t q) -> p t q", q=P)).then_inc(xT_ready, 1)
                stage(2, 0, True)
                take_y(0, 0)
                with ve.Fori(3, MAXT - 1, 2) as i:
                    for s in (1, 0):
                        stage(i + 1 - s, s, True)
                        take_y(i - 1 - s, s)
                take_y(MAXT - 2, 1)
                take_y(MAXT - 1, 0)
                for t in range(NT):
                    if t % 4 == 0:
                        ve.wait_ge(gathered[t // 4], 64)
                    ve.scalar_tensor_tensor(X[:, t, :], G[:, t, :], wtok[:, t:t + 1], X[:, t, :], ALU.mult, ALU.add)


def layernorm(ve, gp, X, XN, t, ch, var_ready, rstd_ready, xn_ready, neghalf, NT):
    if ve is not None:
        for n in range(NT):
            bs = ve.bn_stats(t["stats"][:, n, :], X[:, n, :])
        ch.step(bs)
        for n in range(NT):
            ag = ve.bn_aggr(t["mv"][:, n, :], t["stats"][:, n, :])
        ch.step(ag)
        ve.tensor_scalar(t["vare"][:], t["mv"][:, :, 1], LN_EPS, None, ALU.add).then_inc(var_ready, 1)
        ve.wait_ge(rstd_ready, 1)
        for n in range(NT):
            ve.tensor_scalar(XN[:, n, :], X[:, n, :], t["mv"][:, n, 0:1], t["rstd"][:, n:n + 1],
                             ALU.subtract, ALU.mult).then_inc(xn_ready, 1)
    if gp is not None:
        gp.wait_ge(var_ready, 1)
        gp.tensor_tensor(t["rstd"][:], t["vare"][:], neghalf[:, 0:1].to_broadcast([P, NT]), ALU.pow)\
          .then_inc(rstd_ready, 1)


def attn_project(nc, cst, mem, banks, B, L, NH):
    NT, NG, TB = B * L // P, B * L // BANK, 4
    DK = P // NH
    X, XN, XNT = mem["X"], mem["XN"], mem["XNT"]
    QT, KT, KBT, K, KB, V, VB, VP = (mem[n] for n in ("QT", "KT", "KBT", "K", "KB", "V", "VB", "VP"))
    ident = cst["ident"]
    TAPS, PAD = cst["convw"].shape[2], VP.shape[2] - L
    with ExitStack() as ctx:
        def sb(name, shape, dt=F32):
            return ctx.enter_context(nc.sbuf_tensor(f"a_{name}", shape, dt))

        def sem(name):
            return ctx.enter_context(nc.semaphore(f"a_{name}"))

        ln = {"stats": sb("stats", [P, NT, 6]), "mv": sb("mv", [P, NT, 2]), "vare": sb("vare", [P, NT]), "rstd": sb("rstd", [P, NT])}
        PRE = [sb(f"PRE{w}", [P, B, TAPS - 1 + L]) for w in range(3)]
        CV = [sb(f"CV{w}", [P, B, L]) for w in range(3)]
        Q = sb("Q", [P, NT, P])
        SQ = [sb("SQ0", [P, NT, P]), XN]
        eb = sb("eb", [P, NT, NH])
        beta = sb("beta", [P, NT, NH])
        ss = sb("ss", [P, 2, NT, NH])
        rn = sb("rn", [P, 2, NT, NH])
        dve_step, var_ready, rstd_ready, xn_ready = sem("dve_step"), sem("var_ready"), sem("rstd_ready"), sem("xn_ready")
        xnT_psum, xnT_ready = sem("xnT_psum"), sem("xnT_ready")
        beta_psum, beta_exp, beta_ready = sem("beta_psum"), sem("beta_exp"), sem("beta_ready")
        proj_psum = sem("proj_psum")
        proj_taken = sem("proj_taken")
        padded = sem("padded")
        conv_ready = sem("conv_ready")
        silu_ready = sem("silu_ready")
        raw_psum, raw_taken = sem("raw_psum"), sem("raw_taken")
        sq_ready = sem("sq_ready")
        ss_ready, rn_ready = sem("ss_ready"), sem("rn_ready")
        norm_ready = sem("norm_ready")
        vb_ready = sem("vb_ready")
        nT_psum, nT_taken = sem("nT_psum"), sem("nT_taken")
        raw_dst = [Q, K, V]
        raw_src = [QT[:], KT[:], None]
        ring = banks[2:6]

        with nc.Block() as block:

            @block.tensor
            def _(pe):
                for t in range(NT):
                    pe.wait_ge(xn_ready, t + 1)
                    if t % TB == 0 and t >= 2 * TB:
                        pe.wait_ge(xnT_ready, t // TB - 1)
                    tr = pe.transpose(banks[t // TB % 2][:, t % TB * P:(t % TB + 1) * P], XN[:, t, :], ident[:])
                    if t % TB == TB - 1:
                        tr.then_inc(xnT_psum, 1)
                for w in range(3):
                    for c in range(NG):
                        i = w * NG + c
                        if w == 0:
                            pe.wait_ge(xnT_ready, c + 1)
                        if i >= 4:
                            pe.wait_ge(proj_taken, i - 3)
                        pe.matmul(ring[i % 4][:], cst["wqkv"][:, w, :], XNT[:, c * BANK:(c + 1) * BANK],
                                  start=True, stop=True).then_inc(proj_psum, 1)
                for t in range(NT):
                    mm = pe.matmul(banks[7][:, t * NH:(t + 1) * NH], XNT[:, t * P:(t + 1) * P], cst["wb"][:], start=True, stop=True)
                mm.then_inc(beta_psum, 1)
                pe.wait_ge(proj_taken, 3 * NG)
                for w in range(3):
                    for g in range(NG):
                        i = w * NG + g
                        pe.wait_ge(silu_ready, w * B + g * BANK // L + 1)
                        if i >= 4:
                            pe.wait_ge(raw_taken, i - 3)
                        for t in range(TB):
                            n = g * TB + t
                            if w < 2:
                                src = raw_src[w][:, n * P:(n + 1) * P]
                            else:
                                b, o = n * P // L, n * P % L
                                src = VP[:, b, PAD + o:PAD + o + P]
                            tr = pe.transpose(ring[i % 4][:, t * P:(t + 1) * P], src, ident[:])
                        tr.then_inc(raw_psum, 1)
                pe.wait_ge(raw_taken, 3 * NG)
                for w, src in enumerate((Q, K, KB)):
                    pe.wait_ge(norm_ready, w + 1)
                    for g in range(NG):
                        i = w * NG + g
                        if i >= 4:
                            pe.wait_ge(nT_taken, i - 3)
                        for t in range(TB):
                            tr = pe.transpose(ring[i % 4][:, t * P:(t + 1) * P], src[:, g * TB + t, :], ident[:])
                        tr.then_inc(nT_psum, 1)

            @block.scalar
            def _(act):
                for c in range(NG):
                    act.wait_ge(xnT_psum, c + 1)
                    act.activation(XNT[:, c * BANK:(c + 1) * BANK], banks[c % 2][:], ACT.Copy).then_inc(xnT_ready, 1)
                for w in range(3):
                    for c in range(NG):
                        i = w * NG + c
                        act.wait_ge(proj_psum, i + 1)
                        b, o = c * BANK // L, c * BANK % L
                        act.activation(PRE[w][:, b, TAPS - 1 + o:TAPS - 1 + o + BANK], ring[i % 4][:], ACT.Copy).then_inc(proj_taken, 1)
                act.wait_ge(beta_psum, 1)
                act.activation(eb[:].rearrange("p t h -> p (t h)"), banks[7][:, 0:NT * NH], ACT.Exp, scale=-1.0).then_inc(beta_exp, 1)
                for w, dst in enumerate((QT[:].rearrange("p (b l) -> p b l", b=B), KT[:].rearrange("p (b l) -> p b l", b=B), VP[:, :, PAD:PAD + L])):
                    for b in range(B):
                        act.wait_ge(conv_ready, w * B + b + 1)
                        act.activation(dst[:, b, :], CV[w][:, b, :], ACT.Silu).then_inc(silu_ready, 1)
                for w in range(3):
                    for g in range(NG):
                        i = w * NG + g
                        act.wait_ge(raw_psum, i + 1)
                        psum = ring[i % 4][:].rearrange("p (t c) -> p t c", c=P)
                        if w < 2:
                            if w == 1 and g == 0:
                                act.wait_ge(xnT_psum, NG)
                            act.activation(SQ[w][:, g * TB:(g + 1) * TB, :], psum, ACT.Square).then_inc(sq_ready, 1)
                        act.activation(raw_dst[w][:, g * TB:(g + 1) * TB, :], psum, ACT.Copy).then_inc(raw_taken, 1)
                act.wait_ge(ss_ready, 2)
                act.activation(rn[:], ss[:], ACT.Sqrt).then_inc(rn_ready, 1)
                for w, dst in enumerate((QT, KT, KBT)):
                    for g in range(NG):
                        act.wait_ge(nT_psum, w * NG + g + 1)
                        act.activation(dst[:, g * BANK:(g + 1) * BANK], ring[(w * NG + g) % 4][:], ACT.Copy).then_inc(nT_taken, 1)

            @block.gpsimd
            def _(gp):
                layernorm(None, gp, X, XN, ln, None, var_ready, rstd_ready, xn_ready, cst["neghalf"], NT)
                gp.wait_ge(beta_ready, 1)
                gp.wait_ge(raw_taken, 3 * NG)
                gp.tensor_tensor(VB[:].rearrange("p t (h d) -> p (t h) d", h=NH), V[:].rearrange("p t (h d) -> p (t h) d", h=NH),
                                 beta[:].rearrange("p t h -> p (t h)").unsqueeze(2).to_broadcast([P, NT * NH, DK]), ALU.mult).then_inc(vb_ready, 1)

            @block.vector
            def _(ve):
                ch = Chain(ve, dve_step)
                for w in range(3):
                    ve.memset(PRE[w][:, :, 0:TAPS - 1], 0.0)
                ve.memset(VP[:, :, 0:PAD], 0.0)
                layernorm(ve, None, X, XN, ln, ch, var_ready, rstd_ready, xn_ready, None, NT)
                for w in range(3):
                    ve.wait_ge(proj_taken, (w + 1) * NG)
                    for k in range(TAPS):
                        for b in range(B):
                            src, cw = PRE[w][:, b, k:k + L], cst["convw"][:, w, k:k + 1]
                            if k == 0:
                                ins = ve.tensor_scalar(CV[w][:, b, :], src, cw, None, ALU.mult)
                            else:
                                ve.wait_ge(dve_step, ch.n - B + 1)
                                ins = ve.scalar_tensor_tensor(CV[w][:, b, :], src, cw, CV[w][:, b, :], ALU.mult, ALU.add)
                            if k == TAPS - 1:
                                ins.then_inc(conv_ready, 1)
                                ch.n += 0
                            else:
                                ch.link(ins)
                        if k == TAPS - 2:
                            ch.wait()
                ve.wait_ge(beta_exp, 1)
                ch.step(ve.tensor_scalar(eb[:], eb[:], 1.0, None, ALU.add))
                ve.reciprocal(beta[:], eb[:]).then_inc(beta_ready, 1)
                for w in range(2):
                    ve.wait_ge(sq_ready, NG * (w + 1))
                    ch.step(ve.tensor_reduce(ss[:, w, :, :], SQ[w][:].rearrange("p t (h d) -> p t h d", h=NH), AX.X, ALU.add))
                    ve.tensor_scalar(ss[:, w, :, :], ss[:, w, :, :], 1e-6, None, ALU.add).then_inc(ss_ready, 1)
                ve.wait_ge(rn_ready, 1)
                ch.step(ve.reciprocal(rn[:], rn[:]))
                ve.wait_ge(raw_taken, 2 * NG)
                ve.wait_ge(beta_ready, 1)

                def bc(ap):
                    return ap.rearrange("p t h -> p (t h)").unsqueeze(2).to_broadcast([P, NT * NH, DK])

                def heads(ap):
                    return ap.rearrange("p t (h d) -> p (t h) d", h=NH)
                ve.tensor_tensor(heads(Q[:]), heads(Q[:]), bc(rn[:, 0, :, :]), ALU.mult).then_inc(norm_ready, 1)
                ve.tensor_tensor(heads(K[:]), heads(K[:]), bc(rn[:, 1, :, :]), ALU.mult).then_inc(norm_ready, 1)
                ve.wait_ge(norm_ready, 2)
                ve.tensor_tensor(heads(KB[:]), heads(K[:]), bc(beta[:]), ALU.mult).then_inc(norm_ready, 1)


def attn_delta(nc, cst, mem, banks, B, L, NH):
    C = 32
    NT, TB, DK = B * L // P, 4, P // NH
    CT = P // C
    TH = NT // B
    NG = NT // TB
    QT, KT, KBT, K, KB, VB, VP = (mem[n] for n in ("QT", "KT", "KBT", "K", "KB", "VB", "VP"))
    FS, FL, DEL = (mem[n] for n in ("FS", "FL", "DEL"))
    PAD = VP.shape[2] - L
    NL = 4
    STEPS = NL * NG
    KL = cst["firl"].shape[1]
    POOL_TAPS = 16
    with ExitStack() as ctx:
        def sb(name, shape, dt=F32):
            return ctx.enter_context(nc.sbuf_tensor(f"d_{name}", shape, dt))

        def sem(name):
            return ctx.enter_context(nc.semaphore(f"d_{name}"))

        ATP = sb("ATP", [P, NG, BANK])
        TP = sb("TP", [P, NG, BANK])
        TMP = sb("TMP", [P, 2, BANK])
        TT = sb("TT", [P, 2, BANK])
        BD = sb("BD", [P, 4, TB * NH, P])
        WT = sb("WT", [P, NT * P])
        UT = sb("UT", [P, 2, BANK])
        U = sb("U", [P, NT, P])
        SB = sb("SB", [P, B, P])
        FLP = mem["XN"][:].rearrange("p (b t) c -> p b (t c)", b=B)
        TAP = sb("TAP", [P, L])
        dve_step = sem("dve_step")
        bd_zero, sb_zero = sem("bd_zero"), sem("sb_zero")
        at_psum, at_ready = sem("at_psum"), sem("at_ready")
        t_ready = sem("t_ready")
        bd_ready = sem("bd_ready")
        tt_psum, tt_ready = sem("tt_psum"), sem("tt_ready")
        z_psum, z_ready = sem("z_psum"), sem("z_ready")
        tz_psum = sem("tz_psum")
        wt_psum, wt_ready = sem("wt_psum"), sem("wt_ready")
        ut_psum, ut_ready = sem("ut_psum"), sem("ut_ready")
        u0_psum, u0_ready = sem("u0_psum"), sem("u0_ready")
        m_psum, m_ready = sem("m_psum"), sem("m_ready")
        ws_psum = sem("ws_psum")
        u_ready = sem("u_ready")
        s_psum, s_ready = sem("s_psum"), sem("s_ready")
        o_psum, o_taken = sem("o_psum"), sem("o_taken")
        fir_step, pool_fir = sem("fir_step"), sem("pool_fir")

        def spread_dst(slot, a):
            return BD[a * C:(a + 1) * C, slot, :, a * C:(a + 1) * C]

        def blocks(ap):
            return ap.rearrange("p (s n) -> p s n", n=C)

        def all_blocks(ap):
            return blocks(ap).unsqueeze(2).to_broadcast([P, TB * NH, CT, C])

        def product(pe, bank, lhs, slot):
            for t in range(TB):
                for a in range(NH):
                    mm = pe.matmul(bank[a * C:(a + 1) * C, t * P:(t + 1) * P], lhs(t, a), BD[:, slot, t * NH + a, :], start=True, stop=True)
            return mm

        def o_bank(b, t):
            return banks[4 + 2 * b + t % 2]

        with nc.Block() as block:

            @block.tensor
            def _(pe):
                for g in range(NG):
                    if g >= 2:
                        pe.wait_ge(at_ready, g - 1)
                    for t in range(TB):
                        for c in range(CT):
                            for h in range(NH):
                                rows, cols = slice(h * DK, (h + 1) * DK), slice((g * TB + t) * P + c * C, (g * TB + t) * P + (c + 1) * C)
                                mm = pe.matmul(banks[6 + g % 2][h * C:(h + 1) * C, t * P + c * C:t * P + (c + 1) * C],
                                               KT[rows, cols], KBT[rows, cols], start=True, stop=True)
                    mm.then_inc(at_psum, 1)

                def transposes(i):
                    pe.wait_ge(t_ready, i + 1)
                    if i >= 2:
                        pe.wait_ge(*((tt_ready, i - 1) if i - 2 < STEPS else (bd_ready, i - 1)))
                    for t in range(TB):
                        tr = pe.transpose(banks[2 + i % 2][:, t * P:(t + 1) * P], TP[:, i % NG, t * P:(t + 1) * P], cst["ident"][:])
                    tr.then_inc(tt_psum, 1)

                def second(i):
                    pe.wait_ge(z_ready, i + 1)
                    pe.wait_ge(tt_ready, i + 1)
                    if i >= 2:
                        pe.wait_ge(t_ready, NG + i - 1)
                    product(pe, banks[4 + i % 2], lambda t, a: TT[:, i % 2, t * P + a * C:t * P + (a + 1) * C], 2 + i % 2).then_inc(tz_psum, 1)

                for i in range(STEPS):
                    transposes(i)
                    pe.wait_ge(bd_ready, i + 1)
                    if i < NG:
                        pe.wait_ge(at_ready, i + 1)
                    if i >= 2:
                        pe.wait_ge(z_ready, i - 1)
                    product(pe, banks[i % 2], lambda t, a: ATP[:, i % NG, t * P + a * C:t * P + (a + 1) * C], i % 2).then_inc(z_psum, 1)
                    if i > 0:
                        second(i - 1)
                second(STEPS - 1)

                def u0(g):
                    pe.wait_ge(ut_ready, g + 1)
                    for t in range(TB):
                        tr = pe.transpose(banks[g % 2][:, t * P:(t + 1) * P], UT[:, g % 2, t * P:(t + 1) * P], cst["ident"][:])
                    tr.then_inc(u0_psum, 1)

                for g in range(NG):
                    i = STEPS + g
                    transposes(i)
                    pe.wait_ge(bd_ready, i + 1)
                    if g >= 1:
                        pe.wait_ge(wt_ready, g)
                        pe.wait_ge(ut_ready, g)
                    if g >= 2:
                        pe.wait_ge(u0_ready, g - 1)
                    product(pe, banks[6], lambda t, a: VB[:, g * TB + t, a * DK:(a + 1) * DK], g % 2).then_inc(ut_psum, 1)
                    product(pe, banks[7], lambda t, a: KB[:, g * TB + t, a * DK:(a + 1) * DK], g % 2).then_inc(wt_psum, 1)
                    if g > 0:
                        u0(g - 1)
                u0(NG - 1)
                pe.wait_ge(u0_ready, NG)
                for g in range(NG):
                    for h in range(NH):
                        rows = slice(h * DK, (h + 1) * DK)
                        if g >= 1:
                            pe.wait_ge(m_ready, (g - 1) * NH + h + 1)
                        for t in range(TB):
                            cols = slice((g * TB + t) * P, (g * TB + t + 1) * P)
                            mm = pe.matmul(banks[h][:, t * P:(t + 1) * P], KT[rows, cols], QT[rows, cols], start=True, stop=True)
                        mm.then_inc(m_psum, 1)
                pe.wait_ge(m_ready, NG * NH)
                pe.wait_ge(wt_ready, NG)
                pe.wait_ge(sb_zero, 1)

                def intra(b, t, h):
                    tile = b * TH + t
                    return pe.matmul(o_bank(b, t)[:, h * DK:(h + 1) * DK], BD[:, tile // TB, tile % TB * NH + h, :],
                                     U[:, tile, h * DK:(h + 1) * DK], start=False, stop=True, skip_group_check=True)

                for n in range(L // C):
                    c, t = n % CT, n // CT
                    rows = slice(c * C, (c + 1) * C)
                    for b in range(B):
                        cols = slice((b * TH + t) * P + c * C, (b * TH + t) * P + (c + 1) * C)
                        i = n * B + b
                        if n > 0:
                            pe.wait_ge(s_ready, i - B + 1)
                        pe.matmul(banks[b][rows, 0:P], WT[:, cols], SB[:, b, :], start=True, stop=True).then_inc(ws_psum, 1)
                        if c == 0 and t >= 2:
                            pe.wait_ge(o_taken, (t - 2) * B + b + 1)
                        pe.matmul(o_bank(b, t)[rows, 0:P], QT[:, cols], SB[:, b, :], start=True, stop=True)
                        if t > 0:
                            mm = intra(b, t - 1, c)
                            if c == CT - 1:
                                mm.then_inc(o_psum, 1)
                    for b in range(B):
                        tile, i = b * TH + t, n * B + b
                        pe.wait_ge(u_ready, i + 1)
                        pe.matmul(banks[2 + b][:, 0:P], K[rows, tile, :], U[rows, tile, :], start=(n == 0),
                                  stop=(n == L // C - 1), skip_group_check=True).then_inc(s_psum, 1)
                for b in range(B):
                    for h in range(NH):
                        mm = intra(b, TH - 1, h)
                    mm.then_inc(o_psum, 1)

            @block.scalar
            def _(act):
                for g in range(NG):
                    act.wait_ge(at_psum, g + 1)
                    act.activation(ATP[:, g, :], banks[6 + g % 2][:], ACT.Copy, scale=-1.0).then_inc(at_ready, 1)
                act.wait_ge(bd_zero, 1)
                for i in range(STEPS):
                    act.wait_ge(t_ready, i + 1)
                    if i >= 2:
                        act.wait_ge(z_psum, i - 1)
                    for a in range(NH):
                        cp = act.activation(spread_dst(i % 2, a), blocks(TP[a * C:(a + 1) * C, i % NG, :]), ACT.Copy)
                    cp.then_inc(bd_ready, 1)
                    act.wait_ge(tt_psum, i + 1)
                    if i >= 2:
                        act.wait_ge(tz_psum, i - 1)
                    act.activation(TT[:, i % 2, :], banks[2 + i % 2][:], ACT.Copy).then_inc(tt_ready, 1)
                for g in range(NG):
                    i = STEPS + g
                    act.wait_ge(tt_psum, i + 1)
                    if g < 2:
                        act.wait_ge(z_psum, i - 1)
                    else:
                        act.wait_ge(wt_psum, g - 1)
                    for a in range(CT):
                        cp = act.activation(spread_dst(g % 2, a), blocks(banks[2 + i % 2][a * C:(a + 1) * C, :]), ACT.Copy)
                    cp.then_inc(bd_ready, 1)
                    act.wait_ge(wt_psum, g + 1)
                    act.activation(WT[:, g * BANK:(g + 1) * BANK], banks[7][:], ACT.Copy).then_inc(wt_ready, 1)
                for t in range(TH):
                    for b in range(B):
                        act.wait_ge(o_psum, t * B + b + 1)
                        act.activation(DEL[:, b * TH + t, :], o_bank(b, t)[:, 0:P], ACT.Copy).then_inc(o_taken, 1)

            @block.gpsimd
            def _(gp):
                gp.memset(BD[:, 0:2, :, :].rearrange("p s m c -> p (s m c)"), 0.0).then_inc(bd_zero, 1)
                gp.memset(SB[:], 0.0).then_inc(sb_zero, 1)
                f = cst["firl"]
                n = 0
                for k in range(POOL_TAPS):
                    for b in range(B):
                        lag = KL - 1 - k
                        src, coef = VP[:, b, PAD - lag:PAD - lag + L], f[:, k:k + 1].to_broadcast([P, L])
                        if n > 0:
                            gp.wait_ge(pool_fir, n)
                        gp.tensor_tensor(FLP[:, b, :] if k == 0 else TAP[:], src, coef, ALU.mult).then_inc(pool_fir, 1)
                        n += 1
                        if k > 0:
                            gp.wait_ge(pool_fir, n)
                            gp.tensor_tensor(FLP[:, b, :], FLP[:, b, :], TAP[:], ALU.add).then_inc(pool_fir, 1)
                            n += 1

            @block.vector
            def _(ve):
                ch = Chain(ve, dve_step)
                taps = [(FS, cst["firs"], 0, k) for k in range(cst["firs"].shape[1])] + \
                       [(FL, cst["firl"], POOL_TAPS, k) for k in range(POOL_TAPS, KL)]
                done = [0]

                def fir(count):
                    for dst, f, first, k in taps[done[0]:done[0] + count]:
                        for b in range(B):
                            lag = f.shape[1] - 1 - k
                            src = VP[:, b, PAD - lag:PAD - lag + L]
                            if k == first:
                                ve.tensor_scalar(dst[:, b, :], src, f[:, k:k + 1], None, ALU.mult).then_inc(fir_step, 1)
                            else:
                                ve.wait_ge(fir_step, B * done[0] + b - B + 1)
                                ve.scalar_tensor_tensor(dst[:, b, :], src, f[:, k:k + 1], dst[:, b, :], ALU.mult, ALU.add).then_inc(fir_step, 1)
                        done[0] += 1

                def stacked(ap):
                    return ap.unsqueeze(1).to_broadcast([P, TB * CT, C])

                for g in range(NG):
                    ve.wait_ge(at_ready, g + 1)
                    tmp = TMP[:, g % 2, :]
                    if g >= 2:
                        ve.wait_ge(t_ready, g - 1)
                    ch.step(ve.tensor_tensor(blocks(tmp), blocks(ATP[:, g, :]), stacked(cst["t2mask"][:]), ALU.mult))
                    ch.step(ve.tensor_tensor(blocks(tmp), blocks(tmp), stacked(cst["istack"][:]), ALU.add))
                    ve.transpose(TP[:, g, :], tmp).then_inc(t_ready, 1)

                def add(i):
                    ve.wait_ge(tz_psum, i + 1)
                    ve.wait_ge(t_ready, i + 1)
                    ve.tensor_tensor(TP[:, i % NG, :], TP[:, i % NG, :], banks[4 + i % 2][:], ALU.add).then_inc(t_ready, 1)

                for i in range(STEPS):
                    ve.wait_ge(z_psum, i + 1)
                    if i >= 2:
                        ve.wait_ge(tz_psum, i - 1)
                    mask = cst["quarter"][:, i // NG, :].rearrange("p (a n) -> p a n", n=C).unsqueeze(1).to_broadcast([P, TB * NH, CT, C])
                    ve.tensor_tensor(BD[:, 2 + i % 2, :, :].rearrange("p s (a n) -> p s a n", n=C), all_blocks(banks[i % 2][:]), mask, ALU.mult).then_inc(z_ready, 1)
                    if i > 0:
                        add(i - 1)
                add(STEPS - 1)

                def take_u0(g):
                    ve.wait_ge(u0_psum, g + 1)
                    ve.tensor_copy(U[:, g * TB:(g + 1) * TB, :], banks[g % 2][:].rearrange("p (t c) -> p t c", c=P)).then_inc(u0_ready, 1)
                for g in range(NG):
                    ve.wait_ge(ut_psum, g + 1)
                    if g >= 2:
                        ve.wait_ge(u0_psum, g - 1)
                    ve.tensor_copy(UT[:, g % 2, :], banks[6][:]).then_inc(ut_ready, 1)
                    if g > 0:
                        take_u0(g - 1)
                take_u0(NG - 1)
                for g in range(NG):
                    for h in range(NH):
                        ve.wait_ge(m_psum, g * NH + h + 1)
                        ve.tensor_tensor(BD[:, g, :, :].rearrange("p (t h) c -> p t h c", h=NH)[:, :, h, :], banks[h][:].rearrange("p (t c) -> p t c", c=P),
                                         cst["mmask"][:].unsqueeze(1).to_broadcast([P, TB, P]), ALU.mult).then_inc(m_ready, 1)
                ve.wait_ge(u0_ready, NG)
                for n in range(L // C):
                    c, t = n % CT, n // CT
                    rows = slice(c * C, (c + 1) * C)
                    for b in range(B):
                        tile, i = b * TH + t, n * B + b
                        ve.wait_ge(ws_psum, i + 1)
                        ve.tensor_tensor(U[rows, tile, :], U[rows, tile, :], banks[b][rows, 0:P], ALU.subtract).then_inc(u_ready, 1)
                    for b in range(B):
                        i = n * B + b
                        ve.wait_ge(s_psum, i + 1)
                        ve.tensor_tensor(SB[:, b, :], banks[2 + b][:, 0:P], cst["blk"][:], ALU.mult).then_inc(s_ready, 1)
                    if n % 2 == 1:
                        fir(1)
                fir(len(taps) - done[0])
                ve.wait_ge(fir_step, B * len(taps))
                ve.wait_ge(pool_fir, B * (2 * POOL_TAPS - 1))
                ve.tensor_tensor(FL[:], FL[:], FLP, ALU.add)


def attn_mix(nc, cst, mem, banks, B, L, NH):
    NT, NG, TB, DK = B * L // P, B * L // BANK, 4, P // NH
    NB, NP = 4, NH // 2
    X, XNT, V, VP, FS, FL, DEL = (mem[n] for n in ("X", "XNT", "V", "VP", "FS", "FL", "DEL"))
    PAD = VP.shape[2] - L
    ident = cst["ident"]
    with ExitStack() as ctx:
        def sb(name, shape, dt=F32):
            return ctx.enter_context(nc.sbuf_tensor(f"m_{name}", shape, dt))

        def sem(name):
            return ctx.enter_context(nc.semaphore(f"m_{name}"))

        FSt, FLt = sb("FSt", [P, NT, P]), sb("FLt", [P, NT, P])
        DELT = sb("DELT", [P, NT * P])
        SQ = sb("SQ", [P, 2, NT, P])
        ms = sb("ms", [P, NT, NB, NH])
        ST = sb("ST", [P, NT, 2, NB, NH])
        STT = sb("STT", [2 * NB * NH, NT * P])
        G = sb("G", [P, NP, NT * P])
        lg = sb("lg", [P, NT, NH, NB])
        mx = sb("mx", [P, NT, NH])
        ex = sb("ex", [P, NT, NH, NB])
        MIX = sb("MIX", [P, NT, P])
        TMP = sb("TMP", [P, 2, NT, P])
        os_ = sb("os", [P, NT, NH])
        ro = sb("ro", [P, NT, NH])
        OT = sb("OT", [P, NT * P])
        dve_step = sem("dve_step")
        tr_psum, tr_taken = sem("tr_psum"), sem("tr_taken")
        sq_ready, sq_read = sem("sq_ready"), sem("sq_read")
        ms_ready, rms_ready, max_ready = sem("ms_ready"), sem("rms_ready"), sem("max_ready")
        st_psum, st_taken = sem("st_psum"), sem("st_taken")
        gate_psum, gelu_ready = sem("gate_psum"), sem("gelu_ready")
        logit_psum, shifted, exp_done = sem("logit_psum"), sem("shifted"), sem("exp_done")
        mix_ready, mixsq_ready, os_ready, ro_ready = sem("mix_ready"), sem("mixsq_ready"), sem("os_ready"), sem("ro_ready")
        o_ready = sem("o_ready")
        oT_psum, oT_taken = sem("oT_psum"), sem("oT_taken")
        out_psum = sem("out_psum")

        tok = [FSt, FLt, DEL, V]

        def by_chan(br, c):
            b, o = c * BANK // L, c * BANK % L
            if br == 2:
                return DELT[:, c * BANK:(c + 1) * BANK]
            if br == 3:
                return VP[:, b, PAD + o:PAD + o + BANK]
            return (FS, FL)[br][:, b, o:o + BANK]

        with nc.Block() as block:

            @block.tensor
            def _(pe):
                for i in range(3 * NG):
                    br, g = i // NG, i % NG
                    if i >= 4:
                        pe.wait_ge(tr_taken, i - 3)
                    for t in range(TB):
                        n = g * TB + t
                        src = DEL[:, n, :] if br == 2 else (FS, FL)[br][:, n * P // L, n * P % L:n * P % L + P]
                        tr = pe.transpose(banks[i % 4][:, t * P:(t + 1) * P], src, ident[:])
                    tr.then_inc(tr_psum, 1)
                pe.wait_ge(rms_ready, 1)
                pe.wait_ge(max_ready, NB)
                pe.wait_ge(tr_taken, 3 * NG)
                R = 2 * NB * NH
                for g in range(NG):
                    for t in range(TB):
                        tr = pe.transpose(banks[g % 4][0:R, t * P:(t + 1) * P],
                                          ST[:, g * TB + t, :, :, :].rearrange("p k b h -> p (k b h)"), ident[:])
                    tr.then_inc(st_psum, 1)
                for c in range(NG):
                    for hp in range(NP):
                        i = c * NP + hp
                        bank = banks[4 + i % 4]
                        cols = slice(c * BANK, (c + 1) * BANK)
                        if i >= 4:
                            pe.wait_ge(gelu_ready, i - 3)
                        pe.matmul(bank[:], cst["w1x"][:], XNT[:, cols], start=True, stop=False)
                        for br in range(NB):
                            pe.matmul(bank[:], cst["wbr"][:, br, hp, :], by_chan(br, c), start=False, stop=False)
                        pe.wait_ge(st_taken, c + 1)
                        pe.matmul(bank[:], cst["wst"][:, hp, :], STT[:, cols], start=False, stop=True).then_inc(gate_psum, 1)
                for t in range(NT):
                    for hp in range(NP):
                        pe.wait_ge(gelu_ready, t // TB * NP + NP)
                        o = t * NH * NB + hp * 2 * NB
                        mm = pe.matmul(banks[0][:, o:o + 2 * NB], G[:, hp, t * P:(t + 1) * P], cst["w2bd"][:], start=True, stop=True)
                mm.then_inc(logit_psum, 1)
                pe.wait_ge(o_ready, 1)
                for g in range(NG):
                    if g >= 2:
                        pe.wait_ge(oT_taken, g - 1)
                    for t in range(TB):
                        tr = pe.transpose(banks[1 + g % 2][:, t * P:(t + 1) * P], MIX[:, g * TB + t, :], ident[:])
                    tr.then_inc(oT_psum, 1)
                    pe.wait_ge(oT_taken, g + 1)
                    for t in range(TB):
                        n = g * TB + t
                        mm = pe.matmul(banks[4 + g][:, t * P:(t + 1) * P], OT[:, n * P:(n + 1) * P], cst["wo"][:], start=True, stop=True)
                    mm.then_inc(out_psum, 1)

            @block.scalar
            def _(act):
                dst = [FSt[:].rearrange("p t c -> p (t c)"), FLt[:].rearrange("p t c -> p (t c)"), DELT[:]]
                for k, br in enumerate((2, 3)):
                    act.activation(SQ[:, k, :, :], tok[br][:], ACT.Square).then_inc(sq_ready, 1)
                for i in range(3 * NG):
                    act.wait_ge(tr_psum, i + 1)
                    act.activation(dst[i // NG][:, i % NG * BANK:(i % NG + 1) * BANK], banks[i % 4][:], ACT.Copy).then_inc(tr_taken, 1)
                    if i in (NG, 2 * NG):
                        br = i // NG - 1
                        act.wait_ge(tr_taken, NG * (br + 1))
                        act.wait_ge(sq_read, br + 1)
                        act.activation(SQ[:, br, :, :], tok[br][:], ACT.Square).then_inc(sq_ready, 1)
                act.wait_ge(ms_ready, 1)
                act.activation(ST[:, :, 0, :, :].rearrange("p t b h -> p t (b h)"), ms[:].rearrange("p t b h -> p t (b h)"), ACT.Sqrt).then_inc(rms_ready, 1)
                for g in range(NG):
                    act.wait_ge(st_psum, g + 1)
                    act.activation(STT[:, g * BANK:(g + 1) * BANK], banks[g % 4][0:2 * NB * NH, :], ACT.Copy).then_inc(st_taken, 1)
                for i in range(NG * NP):
                    act.wait_ge(gate_psum, i + 1)
                    c, hp = i // NP, i % NP
                    act.activation(G[:, hp, c * BANK:(c + 1) * BANK], banks[4 + i % 4][:], ACT.Gelu, bias=cst["gb1"][:, 0:1]).then_inc(gelu_ready, 1)
                act.wait_ge(shifted, 1)
                act.activation(ex[:], lg[:], ACT.Exp).then_inc(exp_done, 1)
                act.wait_ge(mix_ready, 1)
                act.activation(SQ[:, 0, :, :], MIX[:], ACT.Square).then_inc(mixsq_ready, 1)
                act.wait_ge(os_ready, 1)
                act.activation(ro[:], os_[:], ACT.Sqrt).then_inc(ro_ready, 1)
                for g in range(NG):
                    act.wait_ge(oT_psum, g + 1)
                    act.activation(OT[:, g * BANK:(g + 1) * BANK], banks[1 + g % 2][:], ACT.Copy).then_inc(oT_taken, 1)

            @block.gpsimd
            def _(gp):
                pass

            @block.vector
            def _(ve):
                ch = Chain(ve, dve_step)

                def heads(ap):
                    return ap.rearrange("p t (h d) -> p t h d", h=NH)

                for k, br in enumerate((2, 3, 0, 1)):
                    if br < 2:
                        ve.wait_ge(tr_taken, NG * (br + 1))
                    ve.tensor_reduce(ST[:, :, 1, br, :], heads(tok[br][:]), AX.X, ALU.max).then_inc(max_ready, 1)
                    ve.wait_ge(sq_ready, k + 1)
                    ve.tensor_reduce(ms[:, :, br, :], heads(SQ[:, k % 2, :, :]), AX.X, ALU.add).then_inc(sq_read, 1)
                ve.wait_ge(sq_read, NB)
                ch.step(ve.tensor_scalar(ms[:], ms[:], 1.0 / DK, None, ALU.mult))
                ve.tensor_scalar(ms[:], ms[:], 1e-8, None, ALU.max).then_inc(ms_ready, 1)

                def ebc(ap):
                    return ap.unsqueeze(3).to_broadcast([P, NT, NH, NB])
                flat = [P, NT * NH, NB]

                def f3(ap):
                    return ap.rearrange("p t h b -> p (t h) b")

                def e3(ap):
                    return ap.rearrange("p t h -> p (t h)").unsqueeze(2).to_broadcast(flat)
                ve.wait_ge(logit_psum, 1)
                ch.step(ve.tensor_tensor(f3(lg[:]), banks[0][:, 0:NT * NH * NB].rearrange("p (r b) -> p r b", b=NB),
                                         cst["gb2"][:].unsqueeze(1).to_broadcast(flat), ALU.add))
                ch.step(ve.tensor_tensor(lg[:], lg[:], cst["rtemp"][:].unsqueeze(1).unsqueeze(3).to_broadcast([P, NT, NH, NB]), ALU.mult))
                ch.step(ve.tensor_reduce(mx[:], lg[:], AX.X, ALU.max))
                ve.tensor_tensor(f3(lg[:]), f3(lg[:]), e3(mx[:]), ALU.subtract).then_inc(shifted, 1)
                ve.wait_ge(exp_done, 1)
                ch.step(ve.tensor_reduce(mx[:], ex[:], AX.X, ALU.add))
                ch.step(ve.reciprocal(mx[:], mx[:]))
                ch.step(ve.tensor_tensor(f3(ex[:]), f3(ex[:]), e3(mx[:]), ALU.mult))
                ch.step(ve.tensor_tensor(ex[:].rearrange("p t h b -> p t (h b)"), ex[:].rearrange("p t h b -> p t (h b)"),
                                         cst["floor"][:].rearrange("p h b -> p (h b)").unsqueeze(1).to_broadcast([P, NT, NH * NB]), ALU.max))
                ch.step(ve.tensor_reduce(mx[:], ex[:], AX.X, ALU.add))
                ch.step(ve.reciprocal(mx[:], mx[:]))
                ch.step(ve.tensor_tensor(f3(ex[:]), f3(ex[:]), e3(mx[:]), ALU.mult))

                def h3(ap):
                    return ap.rearrange("p t (h d) -> p (t h) d", h=NH)

                def weight(br):
                    return ex[:].rearrange("p t h b -> p (t h) b")[:, :, br:br + 1].to_broadcast([P, NT * NH, DK])

                ch.link(ve.tensor_tensor(h3(MIX[:]), h3(tok[0][:]), weight(0), ALU.mult))
                for br in range(1, NB):
                    ch.step(ve.tensor_tensor(h3(TMP[:, br % 2, :, :]), h3(tok[br][:]), weight(br), ALU.mult))
                    ins = ve.tensor_tensor(MIX[:], MIX[:], TMP[:, br % 2, :, :], ALU.add)
                    if br < NB - 1:
                        ch.link(ins)
                    else:
                        ins.then_inc(mix_ready, 1)
                ve.wait_ge(mixsq_ready, 1)
                ch.step(ve.tensor_reduce(os_[:], heads(SQ[:, 0, :, :]), AX.X, ALU.add))
                ve.tensor_scalar(os_[:], os_[:], 1.0 / DK, 1e-5, ALU.mult, ALU.add).then_inc(os_ready, 1)
                ve.wait_ge(ro_ready, 1)
                ch.step(ve.reciprocal(ro[:], ro[:]))
                ve.tensor_tensor(h3(MIX[:]), h3(MIX[:]), ro[:].rearrange("p t h -> p (t h)").unsqueeze(2).to_broadcast([P, NT * NH, DK]), ALU.mult).then_inc(o_ready, 1)
                for g in range(NG):
                    ve.wait_ge(out_psum, g + 1)
                    ve.tensor_tensor(X[:, g * TB:(g + 1) * TB, :], X[:, g * TB:(g + 1) * TB, :], banks[4 + g][:].rearrange("p (t c) -> p t c", c=P), ALU.add)


def attn_consts(nc, cst, a, banks, NH):
    C, DK, NB, NP = 32, P // NH, 4, NH // 2
    HID = P
    U_ = a["L0_attn_gW1"].shape[1]
    with ExitStack() as ctx:
        def sb(name, shape, dt=F32):
            return ctx.enter_context(nc.sbuf_tensor(f"c_{name}", shape, dt))

        def sem(name):
            return ctx.enter_context(nc.semaphore(f"c_{name}"))
        wm, wr, wx = (sb(n, [P, NB, NP, P]) for n in ("wm", "wr", "wx"))
        sel = sb("sel", [P, 8, 8, NH])
        onrep = sb("onrep", [P, 1])
        full = sb("full", [P, 2, P])
        zeroed, loaded, step, masks, dstep, ps = sem("zeroed"), sem("loaded"), sem("step"), sem("masks"), sem("dstep"), sem("ps")
        wbr = cst["wbr"]
        NLOAD = [0]
        with nc.Block() as block:
            @block.sync
            def _(sp):
                def ld(dst, src):
                    sp.dma_start(dst, src).then_inc(loaded, 16)
                    NLOAD[0] += 16
                for w, n in enumerate(("q", "k", "v")):
                    ld(cst["wqkv"][:, w, :], a[f"L0_attn_W{n}"])
                    ld(cst["convw"][:, w, :], a[f"L0_attn_{n}c_w"])
                ld(cst["wb"][:], a["L0_attn_Wb"])
                ld(cst["firs"][:], a["L0_attn_fir_s"].rearrange("h d k -> (h d) k"))
                ld(cst["firl"][:], a["L0_attn_fir_l"].rearrange("h d k -> (h d) k"))
                gw1 = a["L0_attn_gW1"]
                for i in range(2):
                    ld(cst["w1x"][:, i * U_:(i + 1) * U_], gw1[0:HID, :])
                    ld(cst["gb1"][i * U_:(i + 1) * U_, :], a["L0_attn_gb1"].rearrange("(u o) -> u o", o=1))
                ld(cst["gb2"][:], a["L0_attn_gb2"].partition_broadcast(P))
                ld(cst["rtemp"][:], a["L0_attn_temp"].partition_broadcast(P))
                ld(cst["floor"][:].rearrange("p h b -> p (h b)"), a["L0_attn_eps_floor"].rearrange("h b -> (h b)").partition_broadcast(P))
                ld(cst["wo"][:], a["L0_attn_Wo"])
                for h in range(NH):
                    ld(onrep[h * DK:(h + 1) * DK, :], a["L0_attn_onorm_w"].rearrange("(d o) -> d o", o=1))
                sp.wait_ge(zeroed, 5)
                for i in range(2):
                    ld(cst["w2bd"][i * U_:(i + 1) * U_, i * NB:(i + 1) * NB], a["L0_attn_gW2"])
                stat = gw1[HID:HID + 3 * NB * DK, :].rearrange("(b k d) u -> k d b u", b=NB, k=3)
                for h in range(NH):
                    rows, cols = slice(h * DK, (h + 1) * DK), slice(h % 2 * U_, (h % 2 + 1) * U_)
                    for k, dst in enumerate((wm, wr, wx)):
                        ld(dst[rows, :, h // 2, cols], stat[k])
                    ld(wbr[rows, :, h // 2, cols], gw1[HID + 3 * NB * DK:, :].rearrange("(b d) u -> d b u", b=NB))

            @block.gpsimd
            def _(gp):
                n = [0]

                def sel_(dst, src, op, base, pattern, cm, last=False):
                    gp.wait_ge(step, n[0])
                    gp.affine_select(out=dst, in_=src, compare_op=op, fill=0.0, base=base, pattern=pattern,
                                     channel_multiplier=cm).then_inc(step, 1)
                    n[0] += 1
                gp.memset(cst["blk"][:], 1.0)
                gp.memset(cst["quarter"][:], 0.0)
                gp.memset(full[:], 0.0)
                gp.memset(sel[:], 0.0).then_inc(step, 1)
                n[0] += 1
                gp.wait_ge(step, 1)
                for i in range(8):
                    gp.memset(sel[:, i, i, :], 1.0)
                gp.memset(full[:, 0, :].rearrange("p (b s) -> p b s", s=2)[:, :, 1], 1.0)
                for i in range(4):
                    s = 4 << i
                    ms_ = gp.memset(cst["quarter"][:, i, :].rearrange("p (b s) -> p b s", s=s)[:, :, 0:s // 2], 1.0)
                ms_.then_inc(step, 1)
                n[0] += 1
                v = sel[:].rearrange("p a b h -> p (a b) h")
                sel_(v, v, ALU.is_ge, 0, [[0, 64], [-DK, NH]], 1)
                sel_(v, v, ALU.is_ge, DK - 1, [[0, 64], [DK, NH]], -1)
                v = cst["blk"][:].rearrange("p (b c) -> p b c", c=C)
                sel_(v, v, ALU.is_ge, 0, [[-C, 4], [0, C]], 1)
                sel_(v, v, ALU.is_ge, C - 1, [[C, 4], [0, C]], -1)
                sel_(cst["mmask"][:], cst["blk"][:], ALU.is_ge, 0, [[1, P]], -1)
                v = full[:, 0, :].rearrange("p (b c) -> p b c", c=2)[:, :, 1]
                sel_(v, v, ALU.is_equal, 0, [[-2, P // 2]], 1)
                for i in range(4):
                    s = 4 << i
                    v = cst["quarter"][:, i, :].rearrange("p (b s) -> p b s", s=s)[:, :, 0:s // 2]
                    sel_(v, v, ALU.is_ge, -s // 2, [[-s, P // s], [0, s // 2]], 1)
                    sel_(v, v, ALU.is_ge, s - 1, [[s, P // s], [0, s // 2]], -1)
                gp.wait_ge(step, n[0])
                gp.tensor_copy(full[:, 1, :], cst["ident"][:]).then_inc(masks, 1)

            @block.vector
            def _(ve):
                ch = Chain(ve, dstep)
                for z in (wm, wr, wx, wbr):
                    ve.memset(z[:], 0.0).then_inc(zeroed, 1)
                ve.memset(cst["w2bd"][:], 0.0).then_inc(zeroed, 1)
                ve.wait_ge(masks, 1)
                for i, dst in enumerate((cst["t2mask"], cst["istack"])):
                    ve.tensor_reduce(dst[:], full[:, i, :].rearrange("p (b c) -> p c b", c=C), AX.X, ALU.add)
                ve.wait_ge(loaded, NLOAD[0])
                ch.step(ve.tensor_scalar(cst["rtemp"][:], cst["rtemp"][:], 0.2, 10.0, ALU.max, ALU.min))
                ve.reciprocal(cst["rtemp"][:], cst["rtemp"][:])
                ve.tensor_scalar(cst["floor"][:], cst["floor"][:], 1e-7, 0.1, ALU.max, ALU.min)
                ve.tensor_scalar(cst["wo"][:], cst["wo"][:], onrep[:, 0:1], None, ALU.mult)
                ve.wait_ge(ps, 1)
                for i in range(2):
                    w = wbr[:].rearrange("p b n u -> p (b n u)")[:, i * BANK:(i + 1) * BANK]
                    ve.scalar_tensor_tensor(w, banks[i][:], 1.0 / DK, w, ALU.mult, ALU.add)
                ve.tensor_copy(cst["wst"][:].rearrange("p n u -> p (n u)"), banks[2][0:8 * NH, 0:NP * P])

            @block.tensor
            def _(pe):
                pe.wait_ge(masks, 1)
                pe.wait_ge(loaded, NLOAD[0])
                for i in range(2):
                    pe.matmul(banks[i][:], cst["blk"][:], wm[:].rearrange("p b n u -> p (b n u)")[:, i * BANK:(i + 1) * BANK], start=True, stop=True)
                for i in range(8):
                    w = (wr, wx)[i // NB]
                    mm = pe.matmul(banks[2][0:8 * NH, 0:NP * P], sel[:, i, :, :].rearrange("p b h -> p (b h)"),
                                   w[:, i % NB, :, :].rearrange("p n u -> p (n u)"), start=(i == 0), stop=(i == 7))
                mm.then_inc(ps, 1)


def program(nc, a):
    x, out = a["L0_attn_x"], a["out"]
    B, L, D = x.shape
    NT = B * L // P
    NE, _, F = a["L0_ffn_w1"].shape
    FC = F // P
    MAXT = NT + NE - 1
    NH = a["L0_attn_Wb"].shape[1]
    with ExitStack() as ctx:
        def sb(name, shape, dt=F32):
            return ctx.enter_context(nc.sbuf_tensor(name, shape, dt))

        def sem(name):
            return ctx.enter_context(nc.semaphore(name))

        banks = [ctx.enter_context(nc.psum_tensor(f"bank{i}", [P, BANK], F32)) for i in range(8)]
        X = sb("X", [P, NT, D])
        XN = sb("XN", [P, NT, D])
        XNT = sb("XNT", [P, NT * P])
        b1rows = sb("b1rows", [NE * FC, P])
        b1T = sb("b1T", [P, NE, FC])
        cst = {
            "ident": sb("ident", [P, P]), "before": sb("before", [P, P]), "ones": sb("ones", [P, P]),
            "gw": sb("gw", [P, NE]), "gb": sb("gb", [P, NE]), "neghalf": sb("neghalf", [P, 1]),
            "falling": sb("falling", [P, NE]), "tilestart": sb("tilestart", [P, NT]), "tileno": sb("tileno", [P, MAXT]),
            "blk": sb("blk", [P, P]), "mmask": sb("mmask", [P, P]),
            "quarter": sb("quarter", [P, 4, P]), "t2mask": sb("t2mask", [P, 32]), "istack": sb("istack", [P, 32]),
            "wqkv": sb("wqkv", [P, 3, P]), "convw": sb("convw", [P, 3, 4]), "wb": sb("wb", [P, NH]),
            "firs": sb("firs", [P, a["L0_attn_fir_s"].shape[2]]), "firl": sb("firl", [P, a["L0_attn_fir_l"].shape[2]]),
            "w1x": sb("w1x", [P, P]), "gb1": sb("gb1", [P, 1]), "gb2": sb("gb2", [P, 4]), "rtemp": sb("rtemp", [P, NH]),
            "floor": sb("floor", [P, NH, 4]), "wo": sb("wo", [P, P]), "w2bd": sb("w2bd", [P, 8]),
            "wbr": sb("wbr", [P, 4, 2, P]), "wst": sb("wst", [32, 2, P]),
        }
        zrow = sb("zrow", [P, D])
        xsort = nc.dram_tensor("xsort", (MAXT * P, D), F32, kind="Internal").ap()
        ysort = nc.dram_tensor("ysort", (MAXT * P, D), F32, kind="Internal").ap()
        mem = {"X": X, "XN": XN, "XNT": XNT, "b1T": b1T, "a": a, "xsort": xsort, "ysort": ysort}
        x_in, small_in, pad_zero, pool_step, consts, b1_psum, stored = (sem(n) for n in (
            "x_in", "small_in", "pad_zero", "pool_step", "consts", "b1_psum", "stored"))

        with nc.Block() as block:
            @block.sync
            def _(sp):
                sp.dma_start(X[:], x.rearrange("b (n p) d -> p (b n) d", p=P)).then_inc(x_in, 16)
                sp.wait_ge(x_in, 16)
                sp.wait_ge(pad_zero, 16)

            @block.scalar
            def _(act):
                act.dma_start(b1rows[:], a["L0_ffn_b1"].rearrange("e (j f) -> (e j) f", f=P)).then_inc(small_in, 16)
                act.dma_start(cst["gw"][:], a["L0_ffn_gate_w"]).then_inc(small_in, 16)
                act.dma_start(cst["gb"][:], a["L0_ffn_gate_b"].partition_broadcast(P)).then_inc(small_in, 16)
                act.wait_ge(pool_step, 2)
                act.dma_start(xsort.rearrange("(t p) d -> p t d", p=P),
                              zrow[:].unsqueeze(1).to_broadcast([P, MAXT, D])).then_inc(pad_zero, 16)
                act.wait_ge(b1_psum, 1)
                act.activation(b1T[:].rearrange("p e j -> p (e j)"), banks[7][:, 0:NE * FC], ACT.Copy)

            @block.gpsimd
            def _(gp):
                gp.memset(cst["ident"][:], 0.0).then_inc(pool_step, 1)
                gp.memset(zrow[:], 0.0).then_inc(pool_step, 1)
                gp.memset(cst["ones"][:], 1.0).then_inc(pool_step, 1)
                gp.memset(cst["neghalf"][:], -0.5)
                gp.iota(cst["falling"][:], [[-1, NE]], base=NE, channel_multiplier=0, allow_small_or_imprecise_dtypes=True)
                gp.iota(cst["tilestart"][:], [[P, NT]], base=0, channel_multiplier=0, allow_small_or_imprecise_dtypes=True)
                gp.iota(cst["tileno"][:], [[1, MAXT]], base=0, channel_multiplier=0, allow_small_or_imprecise_dtypes=True)
                gp.wait_ge(pool_step, 3)
                gp.affine_select(out=cst["ident"][:], in_=cst["ident"][:], compare_op=ALU.not_equal, fill=1.0,
                                 base=0, pattern=[[-1, P]], channel_multiplier=1).then_inc(consts, 1)
                gp.affine_select(out=cst["before"][:], in_=cst["ones"][:], compare_op=ALU.is_gt, fill=0.0,
                                 base=0, pattern=[[1, P]], channel_multiplier=-1).then_inc(consts, 1)

            @block.tensor
            def _(pe):
                pe.wait_ge(small_in, 48)
                pe.wait_ge(consts, 2)
                pe.transpose(banks[7][:, 0:NE * FC], b1rows[:], cst["ident"][0:NE * FC, 0:NE * FC]).then_inc(b1_psum, 1)

        attn_consts(nc, cst, a, banks, NH)
        moe_ffn(nc, 0, cst, mem, banks, NT, NE, F)
        with ExitStack() as attn:
            PAD = a["L0_attn_fir_l"].shape[2] - 1

            def ab(name, shape):
                mem[name] = attn.enter_context(nc.sbuf_tensor(name, shape, F32))
            ab("VP", [P, B, PAD + L])
            for name in ("FS", "FL"):
                ab(name, [P, B, L])
            for name in ("V", "DEL"):
                ab(name, [P, NT, P])
            with ExitStack() as delta:
                def db(name, shape):
                    mem[name] = delta.enter_context(nc.sbuf_tensor(name, shape, F32))
                for name in ("QT", "KT", "KBT"):
                    db(name, [P, NT * P])
                for name in ("K", "KB", "VB"):
                    db(name, [P, NT, P])
                attn_project(nc, cst, mem, banks, B, L, NH)
                attn_delta(nc, cst, mem, banks, B, L, NH)
            attn_mix(nc, cst, mem, banks, B, L, NH)
        moe_ffn(nc, 1, cst, mem, banks, NT, NE, F)

        with nc.Block() as block:
            @block.sync
            def _(sp):
                sp.dma_start(out.rearrange("b (n p) d -> p (b n) d", p=P), X[:]).then_inc(stored, 16)
                sp.wait_ge(stored, 16)


_INS = ['L0_attn_x', 'L0_attn_Wq', 'L0_attn_Wk', 'L0_attn_Wv', 'L0_attn_Wb', 'L0_attn_qc_w', 'L0_attn_kc_w',
        'L0_attn_vc_w', 'L0_attn_fir_s', 'L0_attn_fir_l', 'L0_attn_gW1', 'L0_attn_gb1', 'L0_attn_gW2', 'L0_attn_gb2',
        'L0_attn_temp', 'L0_attn_eps_floor', 'L0_attn_onorm_w', 'L0_attn_Wo', 'L0_ffn_gate_w', 'L0_ffn_gate_b',
        'L0_ffn_w1', 'L0_ffn_b1', 'L0_ffn_w2', 'L0_ffn_b2']


def kernel(**inputs):
    import numpy as np
    import concourse.bacc as bacc
    from concourse.bass_utils import run_bass_kernel_spmd as run

    nc = bacc.Bacc("TRN2", target_bir_lowering=False, num_devices=1)
    arrays, aps = {}, {}
    for name in _INS:
        v = np.ascontiguousarray(inputs[name])
        arrays["in_" + name] = v
        aps[name] = nc.dram_tensor("in_" + name, v.shape, mybir.dt.from_np(v.dtype), kind="ExternalInput").ap()
    aps["out"] = nc.dram_tensor("out_0", inputs['L0_attn_x'].shape, F32, kind="ExternalOutput").ap()
    program(nc, aps)
    r = run(nc, [arrays], core_ids=[0])
    return r.results[0]["out_0"]
```

```python
from contextlib import ExitStack

import concourse.bass as bass
from concourse import mybir

F32 = mybir.dt.float32
I32 = mybir.dt.int32
ALU = mybir.AluOpType
ACT = mybir.ActivationFunctionType
AX = mybir.AxisListType

P = 128
BANK = 512
LN_EPS = 1e-5


class Steps:

    def __init__(self, sem):
        self.sem, self.n = sem, 0


class Chain:

    def __init__(self, eng, steps):
        self.eng, self.steps, self.sem = eng, steps, steps.sem

    @property
    def n(self):
        return self.steps.n

    def link(self, ins):
        self.steps.n += 1
        ins.then_inc(self.sem, 1)
        return ins

    def wait(self):
        self.eng.wait_ge(self.sem, self.n)

    def step(self, ins):
        self.link(ins)
        self.wait()


def moe_ffn(nc, rep, cst, mem, banks, NT, NE, F, load=None, make_masks=None, products=None, finish=None):
    D = P
    FC = F // P
    MAXT = NT + NE - 1
    groups = [(g, min(4, MAXT - g)) for g in range(0, MAXT, 4)]
    X, b1T, a = mem["X"], mem["b1T"], mem["a"]
    XN, XNT = mem["XN"], mem["XNT"]
    xsort, ysort = mem["xsort"][rep], mem["ysort"]
    NB = 4
    FIRST = 2
    HEAD = MAXT % NB + NB
    ident, before, ones, gw, gb = cst["ident"], cst["before"], cst["ones"], cst["gw"], cst["gb"]
    with ExitStack() as ctx:
        def sb(name, shape, dt=F32):
            return ctx.enter_context(nc.sbuf_tensor(f"{name}_{rep}", shape, dt))

        def sem(name):
            return ctx.enter_context(nc.semaphore(f"{name}_{rep}"))

        W1 = sb("W1", [P, NE, F])
        W2 = sb("W2", [P, NE, FC, D])
        b2bc = sb("b2bc", [P, NE, D])
        weights_in = sem("weights_in")
        stats, mv = mem["stats"], mem["mv"]
        vare = sb("vare", [P, NT])
        rstd = sb("rstd", [P, NT])
        lg = sb("lg", [P, NT, NE])
        ex = sb("ex", [P, NT, NE])
        pb = sb("pb", [P, NT, NE])
        onehot = sb("onehot", [P, NT, NE])
        mx = sb("mx", [P, NT])
        den = sb("den", [P, NT])
        rden = sb("rden", [P, NT])
        pmax = sb("pmax", [P, NT])
        first = sb("first", [P, NT])
        wtok = sb("wtok", [P, NT])
        tot = sb("tot", [P, NE, NT])
        cum = sb("cum", [P, 1 + NE * NT])
        zero = sb("zero", [P, NE * NT])
        base = sb("base", [P, NE, NT])
        cnt = sb("cnt", [P, NE])
        over = sb("over", [P, NE, NT])
        ntile = sb("ntile", [P, NE])
        tend = sb("tend", [P, 1 + NE])
        goff = sb("goff", [P, NE])
        slot = sb("slot", [P, NT, NE])
        posf = sb("posf", [P, NT])
        pos = sb("pos", [P, NT], I32)
        past = sb("past", [P, MAXT, NE])
        eoff = sb("eoff", [P, MAXT])
        etile = sb("etile", [P, MAXT], I32)
        xr = sb("xr", [P, NT, D + 1])
        xs = sb("xs", [P, MAXT, D + 1])
        row = sb("row", [P, MAXT], I32)
        xT = sb("xT", [P, MAXT, P])
        w1s = sb("w1s", [P, NB, F])
        b1s = sb("b1s", [P, NB, FC])
        b2t = sb("b2t", [P, MAXT, D])
        hT = sb("hT", [P, 2, FC, P])
        Y = sb("Y", [P, MAXT, D])
        G = sb("G", [P, NT, D])

        var_ready = sem("var_ready")
        std_ready = sem("std_ready")
        numbered = sem("numbered")
        xn_ready = sem("xn_ready")
        xnT_psum = sem("xnT_psum")
        xnT_ready = sem("xnT_ready")
        gate_done = sem("gate_done")
        shifted = sem("shifted")
        exp_done = sem("exp_done")
        onehot_ready = sem("onehot_ready")
        ranks_done = sem("ranks_done")
        pos_ready = sem("pos_ready")
        etile_ready = sem("etile_ready")
        scattered = sem("scattered")
        x_loaded = [sem(f"x_loaded{c}") for c in range(len(groups))]
        xT_psum = sem("xT_psum")
        xT_ready = sem("xT_ready")
        w1_staged = sem("w1_staged")
        h_psum = sem("h_psum")
        h_ready = sem("h_ready")
        y_psum = sem("y_psum")
        y_ready = sem("y_ready")
        y_stored = sem("y_stored")
        x_done = sem("x_done")

        pT, pR, pRank, pTot = banks[0:2], banks[2], banks[3], banks[4]
        pX, pH, pY = banks[0:2], banks[2:4], banks[4:6]
        NC = NT // 4

        def each_tile(eng, body):
            for t in range(HEAD):
                body(t, t % NB)
            with eng.Fori(HEAD, MAXT - 2 * NB + 1, NB) as i:
                for k in range(NB):
                    body(i + k, (HEAD + k) % NB)
            for t in range(MAXT - NB, MAXT):
                body(t, t % NB)

        def before_tile(t, n):
            return isinstance(t, int) and t < n

        def exists(t):
            return not isinstance(t, int) or t < MAXT

        with nc.Block() as block:

            @block.sync
            def _(sp):
                sp.dma_start(W1[:], a["L0_ffn_w1"].rearrange("e d f -> d e f")).then_inc(weights_in, 16)
                sp.dma_start(W2[:], a["L0_ffn_w2"].rearrange("e (j f) d -> f e j d", f=P)).then_inc(weights_in, 16)
                sp.dma_start(b2bc[:], a["L0_ffn_b2"].partition_broadcast(P)).then_inc(weights_in, 16)
                if rep == 0:
                    load(sp)
                sp.wait_ge(scattered, 16 * NT)
                for c, (g, n) in enumerate(groups):
                    sp.dma_start(xs[:, g:g + n, :], xsort[g * P:(g + n) * P, :].rearrange("(t p) d -> p t d", p=P))\
                      .then_inc(x_loaded[c], 16)
                sp.wait_ge(y_stored, 16 * MAXT)
                for c in range(NC):
                    sp.dma_start(G[:, c * 4:(c + 1) * 4, :], ysort[c * 4 * P:(c + 1) * 4 * P, :].rearrange("(t p) d -> p t d", p=P))\
                      .then_inc(x_loaded[c], 16)
                if rep == 1:
                    for c in range(NC):
                        sp.wait_ge(x_done, c + 1)
                        sp.dma_start(mem["out"][:, c * 4:(c + 1) * 4, :], X[:, c * 4:(c + 1) * 4, :]).then_inc(mem["stored"], 16)
                    sp.wait_ge(mem["stored"], 16 * NC)

            @block.gpsimd
            def _(gp):
                gp.iota(xr[:, :, D], [[P, NT]], base=0, channel_multiplier=1, allow_small_or_imprecise_dtypes=True).then_inc(numbered, 1)
                if rep == 0:
                    make_masks(gp)
                    gp.wait_ge(mem["pad_zero"], 32)
                gp.wait_ge(numbered, 1)
                gp.wait_ge(pos_ready, 1)
                for t in range(NT):
                    gp.indirect_dma_start(xsort, bass.IndirectOffsetOnAxis(pos[:, t:t + 1], 0),
                                          xr[:, t, :], None).then_inc(scattered, 16)
                for t in range(MAXT):
                    if t % 4 == 0:
                        gp.wait_ge(xT_ready, t // 4 + 1)
                    gp.wait_ge(y_ready, t + 1)
                    gp.indirect_dma_start(ysort, bass.IndirectOffsetOnAxis(row[:, t:t + 1], 0),
                                          Y[:, t, :], None).then_inc(y_stored, 16)

            @block.tensor
            def _(pe):
                def logits(c):
                    pe.wait_ge(xnT_ready, c + 1)
                    for t in range(4 * c, 4 * c + 4):
                        mm = pe.matmul(pR[:, t * NE:(t + 1) * NE], XNT[:, t * P:(t + 1) * P], gw[:], start=True, stop=True)
                    return mm

                for t in range(NT):
                    pe.wait_ge(xn_ready, t + 1)
                    if t % 4 == 0 and t >= 8:
                        pe.wait_ge(xnT_ready, t // 4 - 1)
                    tr = pe.transpose(pT[t // 4 % 2][:, t % 4 * P:(t % 4 + 1) * P], xr[:, t, 0:D], ident[:])
                    if t % 4 == 3:
                        tr.then_inc(xnT_psum, 1)
                        if t > 4:
                            logits(t // 4 - 1)
                logits(NC - 1).then_inc(gate_done, 1)
                pe.wait_ge(onehot_ready, 1)
                pe.matmul(pRank[:, 0:NT * NE], before[:], onehot[:], start=True, stop=True)
                pe.matmul(pTot[:, 0:NT * NE], ones[:], onehot[:], start=True, stop=True).then_inc(ranks_done, 1)
                if rep == 0:
                    products(pe)
                pe.wait_ge(etile_ready, 1)
                pe.wait_ge(weights_in, 48)

                def sorted_group(c):
                    g, n = groups[c]
                    pe.wait_ge(x_loaded[c], 16)
                    if c >= 2:
                        pe.wait_ge(xT_ready, c - 1)
                    for t in range(n):
                        tr = pe.transpose(pX[c % 2][:, t * P:(t + 1) * P], xs[:, g + t, 0:D], ident[:])
                    tr.then_inc(xT_psum, 1)

                def up(t, s):
                    if isinstance(t, int):
                        pe.wait_ge(xT_ready, min(t // 4 + 1, len(groups)) if t < HEAD else len(groups))
                    pe.wait_ge(w1_staged, t + 1)
                    if not before_tile(t, 2):
                        pe.wait_ge(h_ready, FC * t - FC)
                    for j in range(FC):
                        mm = pe.matmul(pH[s % 2][:, j * P:(j + 1) * P], w1s[:, s, j * P:(j + 1) * P],
                                       xT[:, bass.ds(t, 1), :], start=True, stop=True)
                    mm.then_inc(h_psum, 1)

                def tile_products(t, s):
                    if isinstance(t, int) and FIRST + t < len(groups):
                        sorted_group(FIRST + t)
                    if exists(t + 1):
                        up(t + 1, (s + 1) % NB)
                    e = pe.value_load(etile[0:1, bass.ds(t, 1)], min_val=0, max_val=NE - 1)
                    pe.wait_ge(h_ready, FC * t + FC)
                    if not before_tile(t, 2):
                        pe.wait_ge(y_ready, t - 1)
                    for j in range(FC):
                        mm = pe.matmul(pY[s % 2][:, 0:D], hT[:, s % 2, j, :], W2[:, bass.ds(e, 1), j, :],
                                       start=(j == 0), stop=(j == FC - 1))
                    mm.then_inc(y_psum, 1)

                for c in range(FIRST):
                    sorted_group(c)
                up(0, 0)
                each_tile(pe, tile_products)

            @block.scalar
            def _(act):
                act.wait_ge(var_ready, 1)
                act.activation(rstd[:], vare[:], ACT.Sqrt).then_inc(std_ready, 1)
                for c in range(NC):
                    act.wait_ge(xnT_psum, c + 1)
                    act.activation(XNT[:, c * BANK:(c + 1) * BANK], pT[c % 2][:], ACT.Copy).then_inc(xnT_ready, 1)
                act.wait_ge(shifted, 1)
                act.activation(ex[:], lg[:], ACT.Exp).then_inc(exp_done, 1)

                def gelu(t, s):
                    act.wait_ge(h_psum, t + 1)
                    if not before_tile(t, 2):
                        act.wait_ge(y_psum, t - 1)
                    for j in range(FC):
                        act.activation(hT[:, s % 2, j, :], pH[s % 2][:, j * P:(j + 1) * P], ACT.Gelu,
                                       bias=b1s[:, s, j:j + 1]).then_inc(h_ready, 1)

                each_tile(act, gelu)

            @block.vector
            def _(ve):
                ch = Chain(ve, cst["dve_steps"])
                moments(ve, X, mem, ch, 0 if rep == 0 else NT - 4, NT)
                ve.tensor_scalar(vare[:], mv[:, :, 1], LN_EPS, None, ALU.add).then_inc(var_ready, 1)
                ve.wait_ge(std_ready, 1)
                ch.step(ve.reciprocal(rstd[:], rstd[:]))
                for t in range(NT):
                    ve.tensor_scalar(xr[:, t, 0:D], X[:, t, :], mv[:, t, 0:1], rstd[:, t:t + 1],
                                     ALU.subtract, ALU.mult).then_inc(xn_ready, 1)

                def ebc(ap):
                    return ap.unsqueeze(2).to_broadcast([P, NT, NE])

                ve.memset(cum[:, 0:1], 0.0)
                ve.memset(tend[:, 0:1], 0.0)
                ch.step(ve.memset(zero[:], 0.0))
                ve.wait_ge(gate_done, 1)
                ch.step(ve.tensor_tensor(lg[:], pR[:, 0:NT * NE].rearrange("p (t e) -> p t e", e=NE),
                                         gb[:].unsqueeze(1).to_broadcast([P, NT, NE]), ALU.add))
                ch.step(ve.tensor_reduce(mx[:], lg[:], AX.X, ALU.max))
                ve.tensor_tensor(lg[:], lg[:], ebc(mx[:]), ALU.subtract).then_inc(shifted, 1)
                ve.wait_ge(exp_done, 1)
                ch.step(ve.tensor_reduce(den[:], ex[:], AX.X, ALU.add))
                ch.step(ve.reciprocal(rden[:], den[:]))
                ch.step(ve.tensor_tensor(pb[:], ex[:], ebc(rden[:]), ALU.mult))
                ch.step(ve.tensor_reduce(pmax[:], pb[:], AX.X, ALU.max))
                ve.tensor_scalar(wtok[:], pmax[:], 0.5, None, ALU.mult)
                ch.step(ve.tensor_tensor(pb[:], pb[:], ebc(pmax[:]), ALU.is_ge))
                ch.step(ve.tensor_tensor(pb[:], pb[:], cst["falling"][:].unsqueeze(1).to_broadcast([P, NT, NE]), ALU.mult))
                ch.step(ve.tensor_reduce(first[:], pb[:], AX.X, ALU.max))
                ve.tensor_tensor(onehot[:], pb[:], ebc(first[:]), ALU.is_equal).then_inc(onehot_ready, 1)
                ve.wait_ge(ranks_done, 1)
                ch.step(ve.tensor_copy(tot[:].rearrange("p e t -> p t e"), pTot[:, 0:NT * NE].rearrange("p (t e) -> p t e", e=NE)))
                ch.step(ve.tensor_tensor_scan(cum[:, 1:1 + NE * NT], tot[:].rearrange("p e t -> p (e t)"), zero[:], 0.0, ALU.add, ALU.add))
                C = cum[:, 1:1 + NE * NT].rearrange("p (e t) -> p e t", t=NT)
                ends, starts = C[:, :, NT - 1], cum[:, 0:NE * NT].rearrange("p (e t) -> p e t", t=NT)[:, :, 0]
                ch.step(ve.tensor_tensor(cnt[:], ends, starts, ALU.subtract))
                ch.step(ve.tensor_tensor(over[:], cnt[:].unsqueeze(2).to_broadcast([P, NE, NT]),
                                         cst["tilestart"][:].unsqueeze(1).to_broadcast([P, NE, NT]), ALU.is_gt))
                ch.step(ve.tensor_reduce(ntile[:], over[:], AX.X, ALU.add))
                ch.step(ve.tensor_tensor_scan(tend[:, 1:1 + NE], ntile[:], zero[:, 0:NE], 0.0, ALU.add, ALU.add))
                ch.step(ve.scalar_tensor_tensor(goff[:], tend[:, 0:NE], float(P), starts, ALU.mult, ALU.subtract))
                ch.step(ve.tensor_tensor(base[:], C, tot[:], ALU.subtract))
                ch.step(ve.tensor_tensor(base[:], base[:], goff[:].unsqueeze(2).to_broadcast([P, NE, NT]), ALU.add))
                ch.step(ve.tensor_tensor(slot[:], pRank[:, 0:NT * NE].rearrange("p (t e) -> p t e", e=NE),
                                         base[:].rearrange("p e t -> p t e"), ALU.add))
                ch.step(ve.tensor_tensor(slot[:], slot[:], onehot[:], ALU.mult))
                ch.step(ve.tensor_reduce(posf[:], slot[:], AX.X, ALU.add))
                ve.tensor_copy(pos[:], posf[:]).then_inc(pos_ready, 1)
                ch.step(ve.tensor_tensor(past[:], cst["tileno"][:].unsqueeze(2).to_broadcast([P, MAXT, NE]),
                                         tend[:, 1:1 + NE].unsqueeze(1).to_broadcast([P, MAXT, NE]), ALU.is_ge))
                ch.step(ve.tensor_reduce(eoff[:], past[:], AX.X, ALU.add))
                ch.step(ve.tensor_scalar(eoff[:], eoff[:], float(NE - 1), None, ALU.min))
                ve.tensor_copy(etile[:], eoff[:]).then_inc(etile_ready, 1)

                def stage(t, s):
                    e = ve.value_load(etile[0:1, bass.ds(t, 1)], min_val=0, max_val=NE - 1)
                    if not before_tile(t, NB):
                        ve.wait_ge(h_psum, t - NB + 1)
                        ve.wait_ge(h_ready, FC * t - FC * (NB - 1))
                    ve.tensor_copy(b1s[:, s, :], b1T[:, bass.ds(e, 1), :])
                    ve.tensor_copy(b2t[:, bass.ds(t, 1), :], b2bc[:, bass.ds(e, 1), :])
                    ve.tensor_copy(w1s[:, s, :], W1[:, bass.ds(e, 1), :]).then_inc(w1_staged, 1)

                def take_y(t, s):
                    ve.wait_ge(y_psum, t + 1)
                    ve.tensor_tensor(Y[:, bass.ds(t, 1), :], pY[s % 2][:, 0:D], b2t[:, bass.ds(t, 1), :], ALU.add).then_inc(y_ready, 1)

                def around(t, s):
                    if isinstance(t, int) and FIRST + t < len(groups):
                        take_group(FIRST + t)
                    if exists(t + NB - 1):
                        stage(t + NB - 1, (s + NB - 1) % NB)
                    if not before_tile(t, 1):
                        take_y(t - 1, (s + NB - 1) % NB)

                ve.wait_ge(etile_ready, 1)
                ve.wait_ge(weights_in, 48)
                if rep == 0:
                    finish(ve)
                for t in range(NB - 1):
                    stage(t, t)
                def take_group(c):
                    g, n = groups[c]
                    ve.wait_ge(xT_psum, c + 1)
                    ve.tensor_copy(row[:, g:g + n], xs[:, g:g + n, D])
                    ve.tensor_copy(xT[:, g:g + n, :], pX[c % 2][:, 0:n * P].rearrange("p (t q) -> p t q", q=P)).then_inc(xT_ready, 1)

                for c in range(FIRST):
                    take_group(c)
                each_tile(ve, around)
                take_y(MAXT - 1, (MAXT - 1) % NB)
                for t in range(NT):
                    if t % 4 == 0:
                        ve.wait_ge(x_loaded[t // 4], 32)
                    up_x = ve.scalar_tensor_tensor(X[:, t, :], G[:, t, :], wtok[:, t:t + 1], X[:, t, :], ALU.mult, ALU.add)
                    if t % 4 == 3:
                        up_x.then_inc(x_done, 1)


def moments(ve, X, mem, ch, first, end):
    stats, mv = mem["stats"], mem["mv"]
    for n in range(first, end):
        bs = ve.bn_stats(stats[:, n, :], X[:, n, :])
    ch.step(bs)
    for n in range(first, end):
        ag = ve.bn_aggr(mv[:, n, :], stats[:, n, :])
    ch.step(ag)


def attn_project(nc, cst, mem, banks, B, L, NH):
    NT, NG, TB = B * L // P, B * L // BANK, 4
    DK = P // NH
    X, XN, XNT = mem["X"], mem["XN"], mem["XNT"]
    QT, KT, KBT, K, KB, V, VB, VP = (mem[n] for n in ("QT", "KT", "KBT", "K", "KB", "V", "VB", "VP"))
    ident = cst["ident"]
    TAPS, PAD = cst["convw"].shape[2], VP.shape[2] - L
    with ExitStack() as ctx:
        def sb(name, shape, dt=F32):
            return ctx.enter_context(nc.sbuf_tensor(f"a_{name}", shape, dt))

        def sem(name):
            return ctx.enter_context(nc.semaphore(f"a_{name}"))

        vare, rstd = sb("vare", [P, NT]), sb("rstd", [P, NT])
        PRE = [sb(f"PRE{w}", [P, B, TAPS - 1 + L]) for w in range(2)]
        CV = [sb(f"CV{w}", [P, B, L]) for w in range(2)]
        Q = sb("Q", [P, NT, P])
        KR = sb("KR", [P, NT, P])
        SQ = [sb("SQ0", [P, NT, P]), XN]
        eb = sb("eb", [P, NT, NH])
        beta = sb("beta", [P, NT, NH])
        rb = sb("rb", [P, NT, NH])
        ss = sb("ss", [P, 2, NT, NH])
        rn = sb("rn", [P, 2, NT, NH])
        var_ready, std_ready, xn_ready = sem("var_ready"), sem("std_ready"), sem("xn_ready")
        xnT_psum, xnT_ready = sem("xnT_psum"), sem("xnT_ready")
        beta_psum, beta_exp, beta_ready = sem("beta_psum"), sem("beta_exp"), sem("beta_ready")
        proj_psum = sem("proj_psum")
        proj_taken = sem("proj_taken")
        padded = sem("padded")
        conv_ready = sem("conv_ready")
        q_ready, k_ready, v_ready = sem("q_ready"), sem("k_ready"), sem("v_ready")
        raw_psum, raw_taken = sem("raw_psum"), sem("raw_taken")
        ss_ready, rn_ready = sem("ss_ready"), sem("rn_ready")
        norm_ready = sem("norm_ready")
        vb_ready = sem("vb_ready")
        rb_ready, kb_ready = sem("rb_ready"), sem("kb_ready")
        nT_psum, nT_taken = sem("nT_psum"), sem("nT_taken")
        raw_dst = [Q, KR, V]
        raw_src = [QT[:], KT[:], None]
        ring = banks[2:6]
        raw_ring = [banks[i] for i in (0, 1, 6, 7)]

        with nc.Block() as block:

            @block.tensor
            def _(pe):
                for t in range(NT):
                    pe.wait_ge(xn_ready, t + 1)
                    if t % TB == 0 and t >= 2 * TB:
                        pe.wait_ge(xnT_ready, t // TB - 1)
                    tr = pe.transpose(banks[t // TB % 2][:, t % TB * P:(t % TB + 1) * P], XN[:, t, :], ident[:])
                    if t % TB == TB - 1:
                        tr.then_inc(xnT_psum, 1)
                for w in range(2):
                    for c in range(NG):
                        i = w * NG + c
                        if w == 0:
                            pe.wait_ge(xnT_ready, c + 1)
                        if i >= 4:
                            pe.wait_ge(proj_taken, i - 3)
                        pe.matmul(ring[i % 4][:], cst["wqkv"][:, w, :], XNT[:, c * BANK:(c + 1) * BANK],
                                  start=True, stop=True).then_inc(proj_psum, 1)
                for t in range(NT):
                    mm = pe.matmul(banks[7][:, t * NH:(t + 1) * NH], XNT[:, t * P:(t + 1) * P], cst["wb"][:], start=True, stop=True)
                mm.then_inc(beta_psum, 1)
                def raw(w):
                    for g in range(NG):
                        i = w * NG + g
                        if w == 2:
                            pe.wait_ge(v_ready, g + 1)
                        else:
                            pe.wait_ge((q_ready, k_ready)[w], g * BANK // L + 1)
                        if i >= 4:
                            pe.wait_ge(raw_taken, i - 3)
                        for t in range(TB):
                            n = g * TB + t
                            if w < 2:
                                src = raw_src[w][:, n * P:(n + 1) * P]
                            else:
                                b, o = n * P // L, n * P % L
                                src = VP[:, b, PAD + o:PAD + o + P]
                            tr = pe.transpose(raw_ring[i % 4][:, t * P:(t + 1) * P], src, ident[:])
                        tr.then_inc(raw_psum, 1)

                for c in range(NG):
                    pe.wait_ge(proj_taken, NG + c + 1)
                    for k in range(TAPS - 1, -1, -1):
                        back = TAPS - 1 - k
                        skip = back if c * BANK % L == 0 else 0
                        mm = pe.matmul(ring[c][:, skip:], cst["wvk"][:, k, :], XNT[:, c * BANK + skip - back:(c + 1) * BANK - back],
                                       start=(back == 0), stop=(k == 0), skip_group_check=True)
                    mm.then_inc(proj_psum, 1)
                    if c == 1:
                        pe.wait_ge(xnT_ready, NG)
                        pe.wait_ge(beta_exp, 1)
                        raw(0)
                raw(1)
                raw(2)
                pe.wait_ge(raw_taken, 3 * NG)
                for w, src in enumerate((Q, K, KB)):
                    pe.wait_ge(*((norm_ready, w + 1) if w < 2 else (kb_ready, 1)))
                    for g in range(NG):
                        i = w * NG + g
                        if i >= 4:
                            pe.wait_ge(nT_taken, i - 3)
                        for t in range(TB):
                            tr = pe.transpose(ring[i % 4][:, t * P:(t + 1) * P], src[:, g * TB + t, :], ident[:])
                        tr.then_inc(nT_psum, 1)

            @block.scalar
            def _(act):
                act.wait_ge(var_ready, 1)
                act.activation(rstd[:], vare[:], ACT.Sqrt).then_inc(std_ready, 1)
                for c in range(NG):
                    act.wait_ge(xnT_psum, c + 1)
                    act.activation(XNT[:, c * BANK:(c + 1) * BANK], banks[c % 2][:], ACT.Copy).then_inc(xnT_ready, 1)
                for w in range(2):
                    for c in range(NG):
                        i = w * NG + c
                        act.wait_ge(proj_psum, i + 1)
                        b, o = c * BANK // L, c * BANK % L
                        act.activation(PRE[w][:, b, TAPS - 1 + o:TAPS - 1 + o + BANK], ring[i % 4][:], ACT.Copy).then_inc(proj_taken, 1)
                act.wait_ge(beta_psum, 1)
                act.activation(eb[:].rearrange("p t h -> p (t h)"), banks[7][:, 0:NT * NH], ACT.Exp, scale=-1.0).then_inc(beta_exp, 1)

                def silu(w, dst):
                    for b in range(B):
                        act.wait_ge(conv_ready, w * B + b + 1)
                        act.activation(dst[:, b * L:(b + 1) * L], CV[w][:, b, :], ACT.Silu).then_inc((q_ready, k_ready)[w], 1)

                def raw(w):
                    for g in range(NG):
                        i = w * NG + g
                        act.wait_ge(raw_psum, i + 1)
                        psum = raw_ring[i % 4][:].rearrange("p (t c) -> p t c", c=P)
                        act.activation(raw_dst[w][:, g * TB:(g + 1) * TB, :], psum, ACT.Copy).then_inc(raw_taken, 1)
                silu(0, QT)
                for c in range(NG):
                    act.wait_ge(proj_psum, 2 * NG + c + 1)
                    b, o = c * BANK // L, c * BANK % L
                    act.activation(VP[:, b, PAD + o:PAD + o + BANK], ring[c][:], ACT.Silu).then_inc(v_ready, 1)
                    if c == 1:
                        raw(0)
                silu(1, KT)

                def root(w):
                    act.wait_ge(ss_ready, w + 1)
                    act.activation(rn[:, w, :, :], ss[:, w, :, :], ACT.Sqrt).then_inc(rn_ready, 1)
                root(0)
                raw(1)
                raw(2)
                root(1)
                for w, dst in enumerate((QT, KT, KBT)):
                    for g in range(NG):
                        act.wait_ge(nT_psum, w * NG + g + 1)
                        act.activation(dst[:, g * BANK:(g + 1) * BANK], ring[(w * NG + g) % 4][:], ACT.Copy).then_inc(nT_taken, 1)

            @block.gpsimd
            def _(gp):
                gp.wait_ge(beta_ready, 1)
                gp.wait_ge(raw_taken, 3 * NG)
                gp.tensor_tensor(VB[:].rearrange("p t (h d) -> p (t h) d", h=NH), V[:].rearrange("p t (h d) -> p (t h) d", h=NH),
                                 beta[:].rearrange("p t h -> p (t h)").unsqueeze(2).to_broadcast([P, NT * NH, DK]), ALU.mult).then_inc(vb_ready, 1)
                gp.wait_ge(rb_ready, 1)
                gp.tensor_tensor(KB[:].rearrange("p t (h d) -> p (t h) d", h=NH), KR[:].rearrange("p t (h d) -> p (t h) d", h=NH),
                                 rb[:].rearrange("p t h -> p (t h)").unsqueeze(2).to_broadcast([P, NT * NH, DK]), ALU.mult).then_inc(kb_ready, 1)

            @block.vector
            def _(ve):
                ch = Chain(ve, cst["dve_steps"])
                for w in range(2):
                    ve.memset(PRE[w][:, :, 0:TAPS - 1], 0.0)
                ve.memset(VP[:, :, 0:PAD], 0.0)
                moments(ve, X, mem, ch, 0, NT)
                ve.tensor_scalar(vare[:], mem["mv"][:, :, 1], LN_EPS, None, ALU.add).then_inc(var_ready, 1)
                ve.wait_ge(std_ready, 1)
                ch.step(ve.reciprocal(rstd[:], rstd[:]))
                for n in range(NT):
                    ve.tensor_scalar(XN[:, n, :], X[:, n, :], mem["mv"][:, n, 0:1], rstd[:, n:n + 1],
                                     ALU.subtract, ALU.mult).then_inc(xn_ready, 1)
                for w in range(2):
                    ve.wait_ge(proj_taken, (w + 1) * NG)
                    for k in range(TAPS):
                        for b in range(B):
                            src, cw = PRE[w][:, b, k:k + L], cst["convw"][:, w, k:k + 1]
                            if k == 0:
                                ins = ve.tensor_scalar(CV[w][:, b, :], src, cw, None, ALU.mult)
                            else:
                                ve.wait_ge(ch.sem, ch.n - B + 1)
                                ins = ve.scalar_tensor_tensor(CV[w][:, b, :], src, cw, CV[w][:, b, :], ALU.mult, ALU.add)
                            if k == TAPS - 1:
                                ins.then_inc(conv_ready, 1)
                            else:
                                ch.link(ins)
                        if k == TAPS - 2:
                            ch.wait()
                ve.wait_ge(beta_exp, 1)
                ch.step(ve.tensor_scalar(eb[:], eb[:], 1.0, None, ALU.add))
                ve.reciprocal(beta[:], eb[:]).then_inc(beta_ready, 1)

                def bc(ap):
                    return ap.rearrange("p t h -> p (t h)").unsqueeze(2).to_broadcast([P, NT * NH, DK])

                def heads(ap):
                    return ap.rearrange("p t (h d) -> p (t h) d", h=NH)

                def normalise(w):
                    src, dst = (Q, KR)[w], (Q, K)[w]
                    ve.wait_ge(raw_taken, (w + 1) * NG)
                    if w == 1:
                        ve.wait_ge(xnT_psum, NG)
                    ch.step(ve.tensor_tensor(SQ[w][:], src[:], src[:], ALU.mult))
                    ch.step(ve.tensor_reduce(ss[:, w, :, :], SQ[w][:].rearrange("p t (h d) -> p t h d", h=NH), AX.X, ALU.add))
                    ve.tensor_scalar(ss[:, w, :, :], ss[:, w, :, :], 1e-6, None, ALU.add).then_inc(ss_ready, 1)
                    ve.wait_ge(rn_ready, w + 1)
                    ch.step(ve.reciprocal(rn[:, w, :, :], rn[:, w, :, :]))
                    if w == 1:
                        ve.wait_ge(beta_ready, 1)
                        ve.tensor_tensor(rb[:], rn[:, 1, :, :], beta[:], ALU.mult).then_inc(rb_ready, 1)
                    ve.tensor_tensor(heads(dst[:]), heads(src[:]), bc(rn[:, w, :, :]), ALU.mult).then_inc(norm_ready, 1)

                normalise(0)
                normalise(1)


def attn_delta(nc, cst, mem, banks, B, L, NH):
    C = 32
    NT, TB, DK = B * L // P, 4, P // NH
    CT = P // C
    TH = NT // B
    NG = NT // TB
    QT, KT, KBT, K, KB, V, VB, VP = (mem[n] for n in ("QT", "KT", "KBT", "K", "KB", "V", "VB", "VP"))
    FS, FL, DEL = (mem[n] for n in ("FS", "FL", "DEL"))
    PAD = VP.shape[2] - L
    NL = 4
    STEPS = NL * NG
    KL = cst["firl"].shape[1]
    STEPS_S = L // C
    POOL_TAPS = 20
    with ExitStack() as ctx:
        def sb(name, shape, dt=F32):
            return ctx.enter_context(nc.sbuf_tensor(f"d_{name}", shape, dt))

        def sem(name):
            return ctx.enter_context(nc.semaphore(f"d_{name}"))

        ATP = sb("ATP", [P, NG, BANK])
        TP = sb("TP", [P, NG, BANK])
        TMP = sb("TMP", [P, 2, BANK])
        TT = sb("TT", [P, 2, BANK])
        BD = sb("BD", [P, 4, TB * NH, P])
        OI = TMP
        WT = sb("WT", [P, NT * P])
        UT = TMP
        VSQ = BD[:, 0, :, :]
        U = sb("U", [P, NT, P])
        SB = sb("SB", [P, B, P])
        FLP = mem["XN"][:].rearrange("p (b t) c -> p b (t c)", b=B)
        TAP = sb("TAP", [P, L])
        bd_zero, sb_zero = sem("bd_zero"), sem("sb_zero")
        at_psum, at_ready = sem("at_psum"), sem("at_ready")
        t_ready = sem("t_ready")
        bd_ready = sem("bd_ready")
        tt_psum, tt_ready = sem("tt_psum"), sem("tt_ready")
        z_psum, z_ready = sem("z_psum"), sem("z_ready")
        tz_psum = sem("tz_psum")
        wt_psum, wt_ready = sem("wt_psum"), sem("wt_ready")
        ut_psum, ut_ready = sem("ut_psum"), sem("ut_ready")
        u0_psum, u0_ready = sem("u0_psum"), sem("u0_ready")
        m_psum, m_ready = sem("m_psum"), sem("m_ready")
        ws_psum = sem("ws_psum")
        u_ready = sem("u_ready")
        s_psum, s_ready = sem("s_psum"), sem("s_ready")
        oi_psum, oi_taken = sem("oi_psum"), sem("oi_taken")
        o_psum = sem("o_psum")
        fir_step, pool_fir = sem("fir_step"), sem("pool_fir")
        vsq_ready = sem("vsq_ready")

        def spread_dst(slot, a):
            return BD[a * C:(a + 1) * C, slot, :, a * C:(a + 1) * C]

        M = [BD[:, 2, :, :], BD[:, 3, :, :]] + [m[:].rearrange("p g (s c) -> p (g s) c", c=P) for m in (ATP, TP)]

        def blocks(ap):
            return ap.rearrange("p (s n) -> p s n", n=C)

        def all_blocks(ap):
            return blocks(ap).unsqueeze(2).to_broadcast([P, TB * NH, CT, C])

        def product(pe, bank, lhs, slot):
            for t in range(TB):
                for a in range(NH):
                    mm = pe.matmul(bank[a * C:(a + 1) * C, t * P:(t + 1) * P], lhs(t, a), BD[:, slot, t * NH + a, :], start=True, stop=True)
            return mm

        def o_place(tile):
            return banks[4 + tile // TB][:, tile % TB * P:(tile % TB + 1) * P]

        with nc.Block() as block:

            @block.tensor
            def _(pe):
                for g in range(NG):
                    if g >= 2:
                        pe.wait_ge(at_ready, g - 1)
                    for t in range(TB):
                        for c in range(CT):
                            for h in range(NH):
                                rows, cols = slice(h * DK, (h + 1) * DK), slice((g * TB + t) * P + c * C, (g * TB + t) * P + (c + 1) * C)
                                mm = pe.matmul(banks[6 + g % 2][h * C:(h + 1) * C, t * P + c * C:t * P + (c + 1) * C],
                                               KT[rows, cols], KBT[rows, cols], start=True, stop=True)
                    mm.then_inc(at_psum, 1)

                def transposes(i):
                    pe.wait_ge(t_ready, i + 1)
                    if i >= 2:
                        pe.wait_ge(*((tt_ready, i - 1) if i - 2 < STEPS else (bd_ready, i - 1)))
                    for t in range(TB):
                        tr = pe.transpose(banks[2 + i % 2][:, t * P:(t + 1) * P], TP[:, i % NG, t * P:(t + 1) * P], cst["ident"][:])
                    tr.then_inc(tt_psum, 1)

                def second(i):
                    pe.wait_ge(z_ready, i + 1)
                    pe.wait_ge(tt_ready, i + 1)
                    if i >= 2:
                        pe.wait_ge(t_ready, NG + i - 1)
                    product(pe, banks[4 + i % 2], lambda t, a: TT[:, i % 2, t * P + a * C:t * P + (a + 1) * C], 2 + i % 2).then_inc(tz_psum, 1)

                for i in range(STEPS):
                    transposes(i)
                    pe.wait_ge(bd_ready, i + 1)
                    if i < NG:
                        pe.wait_ge(at_ready, i + 1)
                    if i >= 2:
                        pe.wait_ge(z_ready, i - 1)
                    product(pe, banks[i % 2], lambda t, a: ATP[:, i % NG, t * P + a * C:t * P + (a + 1) * C], i % 2).then_inc(z_psum, 1)
                    if i > 0:
                        second(i - 1)
                second(STEPS - 1)

                def u0(g):
                    pe.wait_ge(ut_ready, g + 1)
                    for t in range(TB):
                        tr = pe.transpose(banks[g % 2][:, t * P:(t + 1) * P], UT[:, g % 2, t * P:(t + 1) * P], cst["ident"][:])
                    tr.then_inc(u0_psum, 1)

                def scores(g):
                    for h in range(NH):
                        n = g * NH + h
                        rows = slice(h * DK, (h + 1) * DK)
                        if n >= 2:
                            pe.wait_ge(m_ready, n - 1)
                        for t in range(TB):
                            cols = slice((g * TB + t) * P, (g * TB + t + 1) * P)
                            mm = pe.matmul(banks[4 + n % 2][:, t * P:(t + 1) * P], KT[rows, cols], QT[rows, cols], start=True, stop=True)
                        mm.then_inc(m_psum, 1)

                transposes(STEPS)
                pe.wait_ge(t_ready, NG + STEPS)
                for g in range(NG):
                    i = STEPS + g
                    scores(g)
                    if g + 1 < NG:
                        transposes(i + 1)
                    pe.wait_ge(bd_ready, i + 1)
                    if g >= 1:
                        pe.wait_ge(wt_ready, g)
                        pe.wait_ge(ut_ready, g)
                    if g >= 2:
                        pe.wait_ge(u0_ready, g - 1)
                    product(pe, banks[6], lambda t, a: VB[:, g * TB + t, a * DK:(a + 1) * DK], g % 2).then_inc(ut_psum, 1)
                    product(pe, banks[7], lambda t, a: KB[:, g * TB + t, a * DK:(a + 1) * DK], g % 2).then_inc(wt_psum, 1)
                    if g > 0:
                        u0(g - 1)
                u0(NG - 1)
                pe.wait_ge(u0_ready, NG)
                pe.wait_ge(m_ready, NG * NH)
                pe.wait_ge(wt_ready, NG)
                pe.wait_ge(sb_zero, 1)

                def w_state(b, n):
                    c, t = n % CT, n // CT
                    cols = slice((b * TH + t) * P + c * C, (b * TH + t) * P + (c + 1) * C)
                    if n > 0:
                        pe.wait_ge(s_ready, n * B + b - B + 1)
                    pe.matmul(banks[b][c * C:(c + 1) * C, 0:P], WT[:, cols], SB[:, b, :], start=True, stop=True).then_inc(ws_psum, 1)

                def q_state(b, n):
                    c, tile = n % CT, b * TH + n // CT
                    cols = slice(tile * P + c * C, tile * P + (c + 1) * C)
                    pe.matmul(o_place(tile)[c * C:(c + 1) * C, :], QT[:, cols], SB[:, b, :], start=(tile % TB == 0), stop=True,
                              skip_group_check=True)

                def add_state(b, n):
                    c, t = n % CT, n // CT
                    rows, tile = slice(c * C, (c + 1) * C), b * TH + t
                    pe.wait_ge(u_ready, n * B + b + 1)
                    pe.matmul(banks[2 + b][:, 0:P], K[rows, tile, :], U[rows, tile, :], start=(n == 0),
                              stop=(n == STEPS_S - 1), skip_group_check=True).then_inc(s_psum, 1)

                for n in range(STEPS_S):
                    w_state(0, n)
                    if n > 0:
                        add_state(1, n - 1)
                    q_state(0, n)
                    add_state(0, n)
                    w_state(1, n)
                    q_state(1, n)
                add_state(1, STEPS_S - 1)
                pe.wait_ge(u_ready, B * STEPS_S)
                pe.wait_ge(s_ready, B * STEPS_S)

                def intra(g):
                    for t in range(TB):
                        for h in range(NH):
                            mm = pe.matmul(banks[g][h * DK:(h + 1) * DK, t * P:(t + 1) * P], U[:, g * TB + t, h * DK:(h + 1) * DK],
                                           M[g][:, t * NH + h, :], start=True, stop=True)
                    mm.then_inc(oi_psum, 1)

                def add_intra(g):
                    pe.wait_ge(oi_taken, g + 1)
                    for t in range(TB):
                        mm = pe.matmul(o_place(g * TB + t), OI[:, g % 2, t * P:(t + 1) * P], cst["ident"][:], start=False, stop=True, skip_group_check=True)
                    mm.then_inc(o_psum, 1)

                for g in range(NG + 1):
                    if g < NG:
                        intra(g)
                    if g > 0:
                        add_intra(g - 1)

            @block.scalar
            def _(act):
                for g in range(NG):
                    act.wait_ge(at_psum, g + 1)
                    act.activation(ATP[:, g, :], banks[6 + g % 2][:], ACT.Copy, scale=-1.0).then_inc(at_ready, 1)
                act.wait_ge(bd_zero, 1)
                for i in range(STEPS):
                    act.wait_ge(t_ready, i + 1)
                    if i >= 2:
                        act.wait_ge(z_psum, i - 1)
                    for a in range(NH):
                        cp = act.activation(spread_dst(i % 2, a), blocks(TP[a * C:(a + 1) * C, i % NG, :]), ACT.Copy)
                    cp.then_inc(bd_ready, 1)
                    act.wait_ge(tt_psum, i + 1)
                    if i >= 2:
                        act.wait_ge(tz_psum, i - 1)
                    act.activation(TT[:, i % 2, :], banks[2 + i % 2][:], ACT.Copy).then_inc(tt_ready, 1)
                for g in range(NG):
                    i = STEPS + g
                    act.wait_ge(tt_psum, i + 1)
                    if g < 2:
                        act.wait_ge(z_psum, i - 1)
                    else:
                        act.wait_ge(wt_psum, g - 1)
                    for a in range(CT):
                        cp = act.activation(spread_dst(g % 2, a), blocks(banks[2 + i % 2][a * C:(a + 1) * C, :]), ACT.Copy)
                    cp.then_inc(bd_ready, 1)
                    act.wait_ge(wt_psum, g + 1)
                    act.activation(WT[:, g * BANK:(g + 1) * BANK], banks[7][:], ACT.Copy).then_inc(wt_ready, 1)
                act.wait_ge(ut_psum, NG)
                act.activation(VSQ, V[:], ACT.Square).then_inc(vsq_ready, 1)
                for g in range(NG + 1):
                    if g < NG:
                        act.wait_ge(oi_psum, g + 1)
                        if g >= 2:
                            act.wait_ge(o_psum, g - 1)
                        act.activation(OI[:, g % 2, :], banks[g][:], ACT.Copy).then_inc(oi_taken, 1)
                    if g > 0:
                        act.wait_ge(o_psum, g)
                        act.activation(DEL[:, (g - 1) * TB:g * TB, :], banks[3 + g][:].rearrange("p (t c) -> p t c", c=P), ACT.Copy)

            @block.gpsimd
            def _(gp):
                gp.memset(BD[:, 0:2, :, :].rearrange("p s m c -> p (s m c)"), 0.0).then_inc(bd_zero, 1)
                gp.memset(SB[:], 0.0).then_inc(sb_zero, 1)
                f = cst["firl"]
                n = 0
                for k in range(POOL_TAPS):
                    for b in range(B):
                        lag = KL - 1 - k
                        src, coef = VP[:, b, PAD - lag:PAD - lag + L], f[:, k:k + 1].to_broadcast([P, L])
                        if n > 0:
                            gp.wait_ge(pool_fir, n)
                        gp.tensor_tensor(FLP[:, b, :] if k == 0 else TAP[:], src, coef, ALU.mult).then_inc(pool_fir, 1)
                        n += 1
                        if k > 0:
                            gp.wait_ge(pool_fir, n)
                            gp.tensor_tensor(FLP[:, b, :], FLP[:, b, :], TAP[:], ALU.add).then_inc(pool_fir, 1)
                            n += 1

            @block.vector
            def _(ve):
                ch = Chain(ve, cst["dve_steps"])
                H = L // 4
                pieces = [(b, slice(o, o + H)) for b in range(B) for o in range(0, L, H)]
                taps = [(FS, cst["firs"], 0, k) for k in range(cst["firs"].shape[1])] + \
                       [(FL, cst["firl"], POOL_TAPS, k) for k in range(POOL_TAPS, KL)]
                steps = [(tap, piece) for tap in taps for piece in pieces]
                done = [0]

                def fir(count):
                    for (dst, f, first, k), (b, part) in steps[done[0]:done[0] + count]:
                        start = PAD - (f.shape[1] - 1 - k) + part.start
                        src = VP[:, b, start:start + H]
                        if k == first:
                            ve.tensor_scalar(dst[:, b, part], src, f[:, k:k + 1], None, ALU.mult).then_inc(fir_step, 1)
                        else:
                            ve.wait_ge(fir_step, done[0] - len(pieces) + 1)
                            ve.scalar_tensor_tensor(dst[:, b, part], src, f[:, k:k + 1], dst[:, b, part], ALU.mult, ALU.add).then_inc(fir_step, 1)
                        done[0] += 1

                def stacked(ap):
                    return ap.unsqueeze(1).to_broadcast([P, TB * CT, C])

                for g in range(NG):
                    ve.wait_ge(at_ready, g + 1)
                    tmp = TMP[:, g % 2, :]
                    if g >= 2:
                        ve.wait_ge(t_ready, g - 1)
                    ch.step(ve.tensor_tensor(blocks(tmp), blocks(ATP[:, g, :]), stacked(cst["t2mask"][:]), ALU.mult))
                    ch.step(ve.tensor_tensor(blocks(tmp), blocks(tmp), stacked(cst["istack"][:]), ALU.add))
                    ve.transpose(TP[:, g, :], tmp).then_inc(t_ready, 1)

                def add(i):
                    ve.wait_ge(tz_psum, i + 1)
                    ve.wait_ge(t_ready, i + 1)
                    ve.tensor_tensor(TP[:, i % NG, :], TP[:, i % NG, :], banks[4 + i % 2][:], ALU.add).then_inc(t_ready, 1)

                for i in range(STEPS):
                    ve.wait_ge(z_psum, i + 1)
                    if i >= 2:
                        ve.wait_ge(tz_psum, i - 1)
                    mask = cst["quarter"][:, i // NG, :].rearrange("p (a n) -> p a n", n=C).unsqueeze(1).to_broadcast([P, TB * NH, CT, C])
                    ve.tensor_tensor(BD[:, 2 + i % 2, :, :].rearrange("p s (a n) -> p s a n", n=C), all_blocks(banks[i % 2][:]), mask, ALU.mult).then_inc(z_ready, 1)
                    if i > 0:
                        add(i - 1)
                add(STEPS - 1)

                def take_u0(g):
                    ve.wait_ge(u0_psum, g + 1)
                    ve.tensor_copy(U[:, g * TB:(g + 1) * TB, :], banks[g % 2][:].rearrange("p (t c) -> p t c", c=P)).then_inc(u0_ready, 1)

                def mask_scores(g):
                    if g == NG - 1:
                        ve.wait_ge(tt_psum, STEPS + NG)
                    for h in range(NH):
                        n = g * NH + h
                        ve.wait_ge(m_psum, n + 1)
                        ve.tensor_tensor(M[g].rearrange("p (t h) c -> p t h c", h=NH)[:, :, h, :], banks[4 + n % 2][:].rearrange("p (t c) -> p t c", c=P),
                                         cst["mmask"][:].unsqueeze(1).to_broadcast([P, TB, P]), ALU.mult).then_inc(m_ready, 1)
                        fir(2)

                ve.wait_ge(tz_psum, STEPS)
                for g in range(NG):
                    mask_scores(g)
                    ve.wait_ge(ut_psum, g + 1)
                    if g >= 2:
                        ve.wait_ge(u0_psum, g - 1)
                    ve.tensor_copy(UT[:, g % 2, :], banks[6][:]).then_inc(ut_ready, 1)
                    if g > 0:
                        take_u0(g - 1)
                take_u0(NG - 1)
                ve.wait_ge(u0_ready, NG)
                def subtract(b, n):
                    c, tile = n % CT, b * TH + n // CT
                    rows = slice(c * C, (c + 1) * C)
                    ve.wait_ge(ws_psum, n * B + b + 1)
                    ve.tensor_tensor(U[rows, tile, :], U[rows, tile, :], banks[b][rows, 0:P], ALU.subtract).then_inc(u_ready, 1)

                def state(b, n):
                    ve.wait_ge(s_psum, n * B + b + 1)
                    ve.tensor_tensor(SB[:, b, :], banks[2 + b][:, 0:P], cst["blk"][:], ALU.mult).then_inc(s_ready, 1)

                for n in range(STEPS_S):
                    subtract(0, n)
                    if n > 0:
                        state(1, n - 1)
                    fir(1)
                    state(0, n)
                    subtract(1, n)
                    fir(1)
                state(1, STEPS_S - 1)
                fir(len(steps) - done[0])
                ve.wait_ge(vsq_ready, 1)
                ve.tensor_reduce(mem["ST"][:, :, 1, 3, :], V[:].rearrange("p t (h d) -> p t h d", h=NH), AX.X, ALU.max)
                ve.tensor_reduce(mem["ms"][:, :, 3, :], VSQ.rearrange("p t (h d) -> p t h d", h=NH), AX.X, ALU.add)
                ve.wait_ge(fir_step, len(steps))
                ve.wait_ge(pool_fir, B * (2 * POOL_TAPS - 1))
                ve.tensor_tensor(FL[:], FL[:], FLP, ALU.add)


def attn_mix(nc, cst, mem, banks, B, L, NH):
    NT, NG, TB, DK = B * L // P, B * L // BANK, 4, P // NH
    NB, NP = 4, NH // 2
    X, XNT, V, VP, FS, FL, DEL = (mem[n] for n in ("X", "XNT", "V", "VP", "FS", "FL", "DEL"))
    PAD = VP.shape[2] - L
    R = 2 * NB * NH
    ident = cst["ident"]
    with ExitStack() as ctx:
        def sb(name, shape, dt=F32):
            return ctx.enter_context(nc.sbuf_tensor(f"m_{name}", shape, dt))

        def sem(name):
            return ctx.enter_context(nc.semaphore(f"m_{name}"))

        FSt, FLt = sb("FSt", [P, NT, P]), sb("FLt", [P, NT, P])
        pairs = sb("pairs", [P, 2, NP, NT * P])
        wpair = sb("wpair", [P, 2, NP, P])
        SQ = sb("SQ", [P, 2, 2, TB, P])
        DSQ = sb("DSQ", [P, 2, TB, P])
        SQM = sb("SQM", [P, TB, P])
        ST, ms = mem["ST"], mem["ms"]
        STT = sb("STT", [R, NT * P])
        G = sb("G", [P, 2, NP, BANK])
        lg = sb("lg", [P, NT, NH, NB])
        mx = sb("mx", [P, NT, NH])
        ex = sb("ex", [P, NT, NH, NB])
        MIX = sb("MIX", [P, NT, P])
        TMP = sb("TMP", [P, TB, P])
        PM, PV = sb("PM", [P, 2, TB, P]), sb("PV", [P, 2, TB, P])
        os_ = sb("os", [P, NT, NH])
        ro = sb("ro", [P, NT, NH])
        OT = sb("OT", [P, 2, BANK])
        pairs_in = [sem(f"pairs_in{b}") for b in range(B)]
        tr_psum, tr_taken = sem("tr_psum"), sem("tr_taken")
        sq_ready, sq_read = sem("sq_ready"), sem("sq_read")
        dsq_ready, dsq_read = sem("dsq_ready"), sem("dsq_read")
        ms_ready, rms_ready = sem("ms_ready"), sem("rms_ready")
        st_psum, st_taken = sem("st_psum"), sem("st_taken")
        gate_psum, gelu_ready = sem("gate_psum"), sem("gelu_ready")
        logit_psum, logit_read = sem("logit_psum"), sem("logit_read")
        shifted, exp_done = sem("shifted"), sem("exp_done")
        weights_ready, pool_mix = sem("weights_ready"), sem("pool_mix")
        mix_ready, mixsq_ready, os_ready, ro_ready = sem("mix_ready"), sem("mixsq_ready"), sem("os_ready"), sem("ro_ready")
        o_ready = sem("o_ready")
        oT_psum, oT_taken = sem("oT_psum"), sem("oT_taken")
        out_psum, x_added = sem("out_psum"), sem("x_added")

        tok = [FSt, FLt, DEL, V]

        def half(hp):
            return slice(hp * P // NP, (hp + 1) * P // NP)

        def tiles(c):
            return slice(c * TB, (c + 1) * TB)

        with nc.Block() as block:

            @block.sync
            def _(sp):
                wbr = cst["wbr"][:].rearrange("p (m k) n u -> p m k n u", k=2)
                for hp in range(NP):
                    for k in range(2):
                        sp.dma_start(wpair[half((hp + k) % NP), :, hp, :], wbr[half(hp), :, k, hp, :]).then_inc(pairs_in[0], 16)
                for b in range(B):
                    cols = slice(b * L, (b + 1) * L)
                    for hp in range(NP):
                        sp.dma_start(pairs[half(hp), 0, hp, cols], FS[half(hp), b, 0:L]).then_inc(pairs_in[b], 16)
                        sp.dma_start(pairs[half(1 - hp), 0, hp, cols], FL[half(hp), b, 0:L]).then_inc(pairs_in[b], 16)
                        sp.dma_start(pairs[half(1 - hp), 1, hp, cols], VP[half(hp), b, PAD:PAD + L]).then_inc(pairs_in[b], 16)

            @block.tensor
            def _(pe):
                def branches(c):
                    for br in range(3):
                        i = c * 3 + br
                        if i >= 2:
                            pe.wait_ge(tr_taken, i - 1)
                        for t in range(TB):
                            n = c * TB + t
                            src = DEL[:, n, :] if br == 2 else (FS, FL)[br][:, n * P // L, n * P % L:n * P % L + P]
                            tr = pe.transpose(banks[i % 2][:, t * P:(t + 1) * P], src, ident[:])
                        tr.then_inc(tr_psum, 1)

                def stats(c):
                    pe.wait_ge(rms_ready, c + 1)
                    if c > 0:
                        pe.wait_ge(st_taken, c)
                    for t in range(TB):
                        tr = pe.transpose(banks[2][0:R, t * P:(t + 1) * P], ST[:, c * TB + t, :, :, :].rearrange("p k b h -> p (k b h)"), ident[:])
                    tr.then_inc(st_psum, 1)

                def gate(c):
                    cols = slice(c * BANK, (c + 1) * BANK)
                    pe.wait_ge(tr_taken, 3 * c + 3)
                    b = c * BANK // L
                    pe.wait_ge(pairs_in[b], 16 * 3 * NP + (16 * 2 * NP if b == 0 else 0))
                    for hp in range(NP):
                        if hp == 1 and c == 0:
                            branches(NG - 1)
                        if hp == 1 and c + 1 < NG:
                            stats(c + 1)
                        if hp == 1 and c > 0:
                            logits(c - 1)
                        if c == NG - 1:
                            turn(0) if hp == 0 else project(0)
                        i = c * NP + hp
                        bank = banks[4 + i % 4]
                        if i >= 4:
                            pe.wait_ge(gelu_ready, i - 3)
                        pe.matmul(bank[:], cst["w1x"][:], XNT[:, cols], start=True, stop=False)
                        for m in range(2):
                            pe.matmul(bank[:], wpair[:, m, hp, :], pairs[:, m, hp, cols], start=False, stop=False)
                        pe.wait_ge(st_taken, c + 1)
                        pe.matmul(bank[:], cst["wst"][:, hp, :], STT[:, cols], start=False, stop=True).then_inc(gate_psum, 1)

                def logits(c):
                    pe.wait_ge(gelu_ready, (c + 1) * NP)
                    if c >= 1:
                        pe.wait_ge(logit_read, c)
                    for t in range(TB):
                        for hp in range(NP):
                            o = t * NH * NB + hp * 2 * NB
                            mm = pe.matmul(banks[3][:, o:o + 2 * NB], G[:, c % 2, hp, t * P:(t + 1) * P], cst["w2bd"][:], start=True, stop=True)
                    mm.then_inc(logit_psum, 1)

                def turn(c):
                    pe.wait_ge(o_ready, c + 1)
                    pe.wait_ge(tr_taken, 3 * NG)
                    if c > 0:
                        pe.wait_ge(oT_taken, c)
                    for t in range(TB):
                        tr = pe.transpose(banks[1][:, t * P:(t + 1) * P], MIX[:, c * TB + t, :], ident[:])
                    tr.then_inc(oT_psum, 1)

                def project(c):
                    pe.wait_ge(oT_taken, c + 1)
                    if c > 0:
                        pe.wait_ge(x_added, c)
                    for t in range(TB):
                        mm = pe.matmul(banks[0][:, t * P:(t + 1) * P], OT[:, c % 2, t * P:(t + 1) * P], cst["wo"][:], start=True, stop=True)
                    mm.then_inc(out_psum, 1)

                branches(0)
                branches(1)
                stats(0)
                for c in range(2, NG - 1):
                    branches(c)
                for c in range(NG):
                    gate(c)
                turn(1)
                logits(NG - 1)
                project(1)
                for c in range(2, NG):
                    turn(c)
                    project(c)

            @block.scalar
            def _(act):
                dst = [FSt[:].rearrange("p t c -> p (t c)"), FLt[:].rearrange("p t c -> p (t c)")]

                def branches(c):
                    for br in range(2):
                        i = c * 3 + br
                        act.wait_ge(tr_psum, i + 1)
                        act.activation(dst[br][:, c * BANK:(c + 1) * BANK], banks[i % 2][:], ACT.Copy).then_inc(tr_taken, 1)
                        act.wait_ge(tr_taken, i + 1)
                        if c >= 2:
                            act.wait_ge(sq_read, (c - 2) * 2 + br + 1)
                        act.activation(SQ[:, c % 2, br, :, :], tok[br][:, tiles(c), :], ACT.Square).then_inc(sq_ready, 1)
                    i = c * 3 + 2
                    act.wait_ge(tr_psum, i + 1)
                    for hp in range(NP):
                        cp = act.activation(pairs[half(hp), 1, hp, c * BANK:(c + 1) * BANK], banks[i % 2][half(hp), :], ACT.Copy)
                    cp.then_inc(tr_taken, 1)

                def roots(c):
                    act.wait_ge(ms_ready, c + 1)
                    act.activation(ST[:, tiles(c), 0, :, :].rearrange("p t b h -> p t (b h)"), ms[:, tiles(c), :, :].rearrange("p t b h -> p t (b h)"),
                                   ACT.Sqrt).then_inc(rms_ready, 1)

                def rows(c):
                    act.wait_ge(st_psum, c + 1)
                    act.activation(STT[:, c * BANK:(c + 1) * BANK], banks[2][0:R, :], ACT.Copy).then_inc(st_taken, 1)

                def gelu(c):
                    if c >= 2:
                        act.wait_ge(logit_psum, c - 1)
                    for hp in range(NP):
                        i = c * NP + hp
                        act.wait_ge(gate_psum, i + 1)
                        act.activation(G[:, c % 2, hp, :], banks[4 + i % 4][:], ACT.Gelu, bias=cst["gb1"][:, 0:1]).then_inc(gelu_ready, 1)

                def exp(c):
                    act.wait_ge(shifted, c + 1)
                    act.activation(ex[:, tiles(c), :, :], lg[:, tiles(c), :, :], ACT.Exp).then_inc(exp_done, 1)

                def mix_square(c):
                    act.wait_ge(mix_ready, c + 1)
                    if c > 0:
                        act.wait_ge(os_ready, c)
                    act.activation(SQM[:], MIX[:, tiles(c), :], ACT.Square).then_inc(mixsq_ready, 1)

                def root(c):
                    act.wait_ge(os_ready, c + 1)
                    act.activation(ro[:, tiles(c), :], os_[:, tiles(c), :], ACT.Sqrt).then_inc(ro_ready, 1)

                def output(c):
                    act.wait_ge(oT_psum, c + 1)
                    if c >= 2:
                        act.wait_ge(out_psum, c - 1)
                    act.activation(OT[:, c % 2, :], banks[1][:], ACT.Copy).then_inc(oT_taken, 1)

                branches(0)
                roots(0)
                branches(1)
                rows(0)
                branches(2)
                roots(1)
                branches(3)
                roots(2)
                roots(3)
                rows(1)
                gelu(0)
                rows(2)
                exp(0)
                gelu(1)
                mix_square(0)
                rows(3)
                root(0)
                exp(1)
                gelu(2)
                output(0)
                mix_square(1)
                root(1)
                exp(2)
                gelu(3)
                output(1)
                mix_square(2)
                root(2)
                exp(3)
                output(2)
                mix_square(3)
                root(3)
                output(3)

            def h3(ap):
                return ap.rearrange("p t (h d) -> p (t h) d", h=NH)

            def weight(c, br):
                return ex[:, tiles(c), :, :].rearrange("p t h b -> p (t h) b")[:, :, br:br + 1].to_broadcast([P, TB * NH, DK])

            @block.gpsimd
            def _(gp):
                for c in range(NG):
                    if c >= 2:
                        gp.wait_ge(dsq_read, c - 1)
                    gp.tensor_tensor(DSQ[:, c % 2, :, :], DEL[:, tiles(c), :], DEL[:, tiles(c), :], ALU.mult).then_inc(dsq_ready, 1)
                for c in range(NG):
                    gp.wait_ge(weights_ready, c + 1)
                    pm, pv = PM[:, c % 2, :, :], PV[:, c % 2, :, :]
                    if c >= 2:
                        gp.wait_ge(mix_ready, c - 1)
                    gp.tensor_tensor(h3(pm), h3(DEL[:, tiles(c), :]), weight(c, 2), ALU.mult).then_inc(pool_mix, 1)
                    gp.tensor_tensor(h3(pv), h3(V[:, tiles(c), :]), weight(c, 3), ALU.mult).then_inc(pool_mix, 1)

            @block.vector
            def _(ve):
                ch = Chain(ve, cst["dve_steps"])

                def stats(c):
                    ve.tensor_reduce(ST[:, tiles(c), 1, 2, :], DEL[:, tiles(c), :].rearrange("p t (h d) -> p t h d", h=NH), AX.X, ALU.max)
                    ve.wait_ge(dsq_ready, c + 1)
                    ve.tensor_reduce(ms[:, tiles(c), 2, :], DSQ[:, c % 2, :, :].rearrange("p t (h d) -> p t h d", h=NH), AX.X, ALU.add).then_inc(dsq_read, 1)
                    for br in range(2):
                        ve.wait_ge(tr_taken, c * 3 + br + 1)
                        ve.tensor_reduce(ST[:, tiles(c), 1, br, :], tok[br][:, tiles(c), :].rearrange("p t (h d) -> p t h d", h=NH), AX.X, ALU.max)
                        ve.wait_ge(sq_ready, c * 2 + br + 1)
                        ve.tensor_reduce(ms[:, tiles(c), br, :], SQ[:, c % 2, br, :, :].rearrange("p t (h d) -> p t h d", h=NH), AX.X, ALU.add).then_inc(sq_read, 1)
                    ve.wait_ge(dsq_read, c + 1)
                    ve.wait_ge(sq_read, (c + 1) * 2)
                    m = ms[:, tiles(c), :, :].rearrange("p t b h -> p (t b h)")
                    ve.tensor_scalar(m, m, 1.0 / DK, 1e-8, ALU.mult, ALU.max).then_inc(ms_ready, 1)

                flat = [P, TB * NH, NB]

                def by_row(ap):
                    return ap.unsqueeze(2).to_broadcast(flat)

                def logits(c):
                    l = lg[:, tiles(c), :, :].rearrange("p t h b -> p (t h) b")
                    m = mx[:, tiles(c), :].rearrange("p t h -> p (t h)")
                    ve.wait_ge(logit_psum, c + 1)
                    ve.tensor_tensor(l, banks[3][:, 0:TB * NH * NB].rearrange("p (r b) -> p r b", b=NB),
                                     cst["gb2"][:].unsqueeze(1).to_broadcast(flat), ALU.add).then_inc(logit_read, 1)
                    ve.wait_ge(logit_read, c + 1)
                    ch.step(ve.tensor_tensor(lg[:, tiles(c), :, :], lg[:, tiles(c), :, :],
                                             cst["rtemp"][:].unsqueeze(1).unsqueeze(3).to_broadcast([P, TB, NH, NB]), ALU.mult))
                    ch.step(ve.tensor_reduce(m, l, AX.X, ALU.max))
                    ve.tensor_tensor(l, l, by_row(m), ALU.subtract).then_inc(shifted, 1)

                def weights(c):
                    e = ex[:, tiles(c), :, :].rearrange("p t h b -> p (t h) b")
                    m = mx[:, tiles(c), :].rearrange("p t h -> p (t h)")
                    ve.wait_ge(exp_done, c + 1)
                    ch.step(ve.tensor_reduce(m, e, AX.X, ALU.add))
                    fl = lg[:, tiles(c), :, :]
                    ch.step(ve.tensor_tensor(fl, cst["floor"][:].unsqueeze(1).to_broadcast([P, TB, NH, NB]),
                                             mx[:, tiles(c), :].unsqueeze(3).to_broadcast([P, TB, NH, NB]), ALU.mult))
                    ch.step(ve.tensor_tensor(e, e, fl.rearrange("p t h b -> p (t h) b"), ALU.max))
                    ch.step(ve.tensor_reduce(m, e, AX.X, ALU.add))
                    ch.step(ve.reciprocal(m, m))
                    ve.tensor_tensor(e, e, by_row(m), ALU.mult).then_inc(weights_ready, 1)

                def mix(c):
                    ve.wait_ge(weights_ready, c + 1)
                    M = MIX[:, tiles(c), :]
                    ve.tensor_tensor(h3(M), h3(FSt[:, tiles(c), :]), weight(c, 0), ALU.mult)
                    ch.step(ve.tensor_tensor(h3(TMP[:]), h3(FLt[:, tiles(c), :]), weight(c, 1), ALU.mult))
                    ch.step(ve.tensor_tensor(M, M, TMP[:], ALU.add))
                    ve.wait_ge(pool_mix, 2 * c + 1)
                    ch.step(ve.tensor_tensor(M, M, PM[:, c % 2, :, :], ALU.add))
                    ve.wait_ge(pool_mix, 2 * c + 2)
                    ve.tensor_tensor(M, M, PV[:, c % 2, :, :], ALU.add).then_inc(mix_ready, 1)

                def mean_square(c):
                    ve.wait_ge(mixsq_ready, c + 1)
                    o = os_[:, tiles(c), :].rearrange("p t h -> p (t h)")
                    ch.step(ve.tensor_reduce(o, h3(SQM[:]), AX.X, ALU.add))
                    ve.tensor_scalar(o, o, 1.0 / DK, 1e-5, ALU.mult, ALU.add).then_inc(os_ready, 1)

                def normalise(c):
                    ve.wait_ge(ro_ready, c + 1)
                    ve.wait_ge(mix_ready, c + 1)
                    o = ro[:, tiles(c), :].rearrange("p t h -> p (t h)")
                    ch.step(ve.reciprocal(o, o))
                    M = MIX[:, tiles(c), :]
                    ve.tensor_tensor(h3(M), h3(M), ro[:, tiles(c), :].rearrange("p t h -> p (t h)").unsqueeze(2).to_broadcast([P, TB * NH, DK]), ALU.mult).then_inc(o_ready, 1)

                def add_x(c):
                    ve.wait_ge(out_psum, c + 1)
                    ve.tensor_tensor(X[:, tiles(c), :], X[:, tiles(c), :], banks[0][:].rearrange("p (t c) -> p t c", c=P), ALU.add).then_inc(x_added, 1)

                for c in range(NG):
                    stats(c)
                for c in range(NG):
                    if c == NG - 1:
                        add_x(0)
                    logits(c)
                    if c > 0:
                        normalise(c - 1)
                    if c == NG - 1:
                        add_x(1)
                    weights(c)
                    mix(c)
                    mean_square(c)
                add_x(2)
                normalise(NG - 1)
                ve.wait_ge(x_added, NG - 1)
                moments(ve, X, mem, ch, 0, NT - TB)
                add_x(NG - 1)


def attn_consts(nc, stack, cst, a, banks, NH):
    C, DK, NB, NP = 32, P // NH, 4, NH // 2
    HID = P
    U_ = a["L0_attn_gW1"].shape[1]
    def sb(name, shape, dt=F32):
        return stack.enter_context(nc.sbuf_tensor(f"c_{name}", shape, dt))

    def sem(name):
        return stack.enter_context(nc.semaphore(f"c_{name}"))
    wm, wr, wx = (sb(n, [P, NB, NP, P]) for n in ("wm", "wr", "wx"))
    sel = sb("sel", [P, 8, 8, NH])
    onrep = sb("onrep", [P, 1])
    full = sb("full", [P, 2, P])
    wvs = sb("wvs", [P, 4, P])
    wv_scaled = sem("wv_scaled")
    zeroed, loaded, step, masks, ps = sem("zeroed"), sem("loaded"), sem("step"), sem("masks"), sem("ps")
    wbr = cst["wbr"]
    NLOAD = [0]
    def load(sp):
        def ld(dst, src):
            sp.dma_start(dst, src).then_inc(loaded, 16)
            NLOAD[0] += 16
        for w, n in enumerate(("q", "k", "v")):
            ld(cst["wqkv"][:, w, :], a[f"L0_attn_W{n}"])
            ld(cst["convw"][:, w, :], a[f"L0_attn_{n}c_w"])
        ld(cst["wb"][:], a["L0_attn_Wb"])
        ld(cst["firs"][:], a["L0_attn_fir_s"].rearrange("h d k -> (h d) k"))
        ld(cst["firl"][:], a["L0_attn_fir_l"].rearrange("h d k -> (h d) k"))
        gw1 = a["L0_attn_gW1"]
        for i in range(2):
            ld(cst["w1x"][:, i * U_:(i + 1) * U_], gw1[0:HID, :])
            ld(cst["gb1"][i * U_:(i + 1) * U_, :], a["L0_attn_gb1"].rearrange("(u o) -> u o", o=1))
        ld(cst["gb2"][:], a["L0_attn_gb2"].partition_broadcast(P))
        ld(cst["rtemp"][:], a["L0_attn_temp"].partition_broadcast(P))
        ld(cst["floor"][:].rearrange("p h b -> p (h b)"), a["L0_attn_eps_floor"].rearrange("h b -> (h b)").partition_broadcast(P))
        ld(cst["wo"][:], a["L0_attn_Wo"])
        for h in range(NH):
            ld(onrep[h * DK:(h + 1) * DK, :], a["L0_attn_onorm_w"].rearrange("(d o) -> d o", o=1))
        sp.wait_ge(zeroed, 5)
        for i in range(2):
            ld(cst["w2bd"][i * U_:(i + 1) * U_, i * NB:(i + 1) * NB], a["L0_attn_gW2"])
        stat = gw1[HID:HID + 3 * NB * DK, :].rearrange("(b k d) u -> k d b u", b=NB, k=3)
        for h in range(NH):
            rows, cols = slice(h * DK, (h + 1) * DK), slice(h % 2 * U_, (h % 2 + 1) * U_)
            for k, dst in enumerate((wm, wr, wx)):
                ld(dst[rows, :, h // 2, cols], stat[k])
            ld(wbr[rows, :, h // 2, cols], gw1[HID + 3 * NB * DK:, :].rearrange("(b d) u -> d b u", b=NB))

    def make_masks(gp):
        n = [0]

        def sel_(dst, src, op, base, pattern, cm, last=False):
            gp.wait_ge(step, n[0])
            gp.affine_select(out=dst, in_=src, compare_op=op, fill=0.0, base=base, pattern=pattern,
                             channel_multiplier=cm).then_inc(step, 1)
            n[0] += 1
        gp.memset(cst["blk"][:], 1.0)
        gp.memset(cst["quarter"][:], 0.0)
        gp.memset(full[:], 0.0)
        gp.memset(sel[:], 0.0).then_inc(step, 1)
        n[0] += 1
        gp.wait_ge(step, 1)
        for i in range(8):
            gp.memset(sel[:, i, i, :], 1.0)
        gp.memset(full[:, 0, :].rearrange("p (b s) -> p b s", s=2)[:, :, 1], 1.0)
        for i in range(4):
            s = 4 << i
            ms_ = gp.memset(cst["quarter"][:, i, :].rearrange("p (b s) -> p b s", s=s)[:, :, 0:s // 2], 1.0)
        ms_.then_inc(step, 1)
        n[0] += 1
        v = sel[:].rearrange("p a b h -> p (a b) h")
        sel_(v, v, ALU.is_ge, 0, [[0, 64], [-DK, NH]], 1)
        sel_(v, v, ALU.is_ge, DK - 1, [[0, 64], [DK, NH]], -1)
        v = cst["blk"][:].rearrange("p (b c) -> p b c", c=C)
        sel_(v, v, ALU.is_ge, 0, [[-C, 4], [0, C]], 1)
        sel_(v, v, ALU.is_ge, C - 1, [[C, 4], [0, C]], -1)
        sel_(cst["mmask"][:], cst["blk"][:], ALU.is_ge, 0, [[1, P]], -1)
        v = full[:, 0, :].rearrange("p (b c) -> p b c", c=2)[:, :, 1]
        sel_(v, v, ALU.is_equal, 0, [[-2, P // 2]], 1)
        for i in range(4):
            s = 4 << i
            v = cst["quarter"][:, i, :].rearrange("p (b s) -> p b s", s=s)[:, :, 0:s // 2]
            sel_(v, v, ALU.is_ge, -s // 2, [[-s, P // s], [0, s // 2]], 1)
            sel_(v, v, ALU.is_ge, s - 1, [[s, P // s], [0, s // 2]], -1)
        gp.wait_ge(step, n[0])
        gp.tensor_copy(full[:, 1, :], cst["ident"][:]).then_inc(masks, 1)

    def zero(ve):
        for z in (wm, wr, wx, wbr, cst["w2bd"]):
            ve.memset(z[:], 0.0).then_inc(zeroed, 1)

    def finish(ve):
        ch = Chain(ve, cst["dve_steps"])
        ve.wait_ge(masks, 1)
        for i, dst in enumerate((cst["t2mask"], cst["istack"])):
            ve.tensor_reduce(dst[:], full[:, i, :].rearrange("p (b c) -> p c b", c=C), AX.X, ALU.add)
        ve.wait_ge(loaded, NLOAD[0])
        ch.step(ve.tensor_scalar(cst["rtemp"][:], cst["rtemp"][:], 0.2, 10.0, ALU.max, ALU.min))
        ve.reciprocal(cst["rtemp"][:], cst["rtemp"][:])
        ve.tensor_scalar(cst["floor"][:], cst["floor"][:], 1e-7, 0.1, ALU.max, ALU.min)
        ve.tensor_scalar(cst["wo"][:], cst["wo"][:], onrep[:, 0:1], None, ALU.mult)
        ve.wait_ge(ps, 1)
        for i in range(2):
            w = wbr[:].rearrange("p b n u -> p (b n u)")[:, i * BANK:(i + 1) * BANK]
            ve.scalar_tensor_tensor(w, banks[6 + i][:], 1.0 / DK, w, ALU.mult, ALU.add)
        ve.tensor_copy(cst["wst"][:].rearrange("p n u -> p (n u)"), banks[5][0:8 * NH, 0:NP * P])
        for k in range(4):
            ins = ve.tensor_scalar(wvs[:, k, :], banks[2][:, 0:P], cst["convw"][:, 2, k:k + 1], None, ALU.mult)
        ins.then_inc(wv_scaled, 1)
        ve.wait_ge(ps, 2)
        ve.tensor_copy(cst["wvk"][:].rearrange("p k c -> p (k c)"), banks[2][:])

    def products(pe):
        pe.wait_ge(masks, 1)
        pe.wait_ge(loaded, NLOAD[0])
        for i in range(2):
            pe.matmul(banks[6 + i][:], cst["blk"][:], wm[:].rearrange("p b n u -> p (b n u)")[:, i * BANK:(i + 1) * BANK], start=True, stop=True)
        for i in range(8):
            w = (wr, wx)[i // NB]
            mm = pe.matmul(banks[5][0:8 * NH, 0:NP * P], sel[:, i, :, :].rearrange("p b h -> p (b h)"),
                           w[:, i % NB, :, :].rearrange("p n u -> p (n u)"), start=(i == 0), stop=(i == 7))
        pe.transpose(banks[2][:, 0:P], cst["wqkv"][:, 2, :], cst["ident"][:]).then_inc(ps, 1)
        pe.wait_ge(wv_scaled, 1)
        for k in range(4):
            tr = pe.transpose(banks[2][:, k * P:(k + 1) * P], wvs[:, k, :], cst["ident"][:])
        tr.then_inc(ps, 1)

    return load, zero, make_masks, products, finish


def program(nc, a):
    x, out = a["L0_attn_x"], a["out"]
    B, L, D = x.shape
    NT = B * L // P
    NE, _, F = a["L0_ffn_w1"].shape
    FC = F // P
    MAXT = NT + NE - 1
    NH = a["L0_attn_Wb"].shape[1]
    with ExitStack() as ctx:
        def sb(name, shape, dt=F32):
            return ctx.enter_context(nc.sbuf_tensor(name, shape, dt))

        def sem(name):
            return ctx.enter_context(nc.semaphore(name))

        banks = [ctx.enter_context(nc.psum_tensor(f"bank{i}", [P, BANK], F32)) for i in range(8)]
        X = sb("X", [P, NT, D])
        XN = sb("XN", [P, NT, D])
        XNT = sb("XNT", [P, NT * P])
        b1T = sb("b1T", [P, NE, FC])
        cst = {
            "dve_steps": Steps(sem("dve_step")),
            "ident": sb("ident", [P, P]), "before": sb("before", [P, P]), "ones": sb("ones", [P, P]),
            "gw": sb("gw", [P, NE]), "gb": sb("gb", [P, NE]),
            "falling": sb("falling", [P, NE]), "tilestart": sb("tilestart", [P, NT]), "tileno": sb("tileno", [P, MAXT]),
            "blk": sb("blk", [P, P]), "mmask": sb("mmask", [P, P]),
            "quarter": sb("quarter", [P, 4, P]), "t2mask": sb("t2mask", [P, 32]), "istack": sb("istack", [P, 32]),
            "wqkv": sb("wqkv", [P, 3, P]), "wvk": sb("wvk", [P, 4, P]), "convw": sb("convw", [P, 3, 4]), "wb": sb("wb", [P, NH]),
            "firs": sb("firs", [P, a["L0_attn_fir_s"].shape[2]]), "firl": sb("firl", [P, a["L0_attn_fir_l"].shape[2]]),
            "w1x": sb("w1x", [P, P]), "gb1": sb("gb1", [P, 1]), "gb2": sb("gb2", [P, 4]), "rtemp": sb("rtemp", [P, NH]),
            "floor": sb("floor", [P, NH, 4]), "wo": sb("wo", [P, P]), "w2bd": sb("w2bd", [P, 8]),
            "wbr": sb("wbr", [P, 4, 2, P]), "wst": sb("wst", [32, 2, P]),
        }
        xsort = [nc.dram_tensor(f"xsort{i}", (MAXT * P, D + 1), F32, kind="Internal").ap() for i in range(2)]
        ysort = nc.dram_tensor("ysort", ((NT + MAXT) * P, D), F32, kind="Internal").ap()
        ST, ms = sb("ST", [P, NT, 2, 4, NH]), sb("ms", [P, NT, 4, NH])
        mem = {"ST": ST, "ms": ms, "stats": sb("stats", [P, NT, 6]), "mv": sb("mv", [P, NT, 2]), "X": X, "XN": XN, "XNT": XNT, "b1T": b1T, "a": a, "xsort": xsort, "ysort": ysort}
        x_in, small_in, pad_zero, pool_step, consts, b1_psum, stored = (sem(n) for n in (
            "x_in", "small_in", "pad_zero", "pool_step", "consts", "b1_psum", "stored"))

        start = ctx.enter_context(ExitStack())
        pad = start.enter_context(nc.sbuf_tensor("pad", [P, MAXT, D + 1], F32))
        b1rows = start.enter_context(nc.sbuf_tensor("b1rows", [NE * FC, P], F32))
        load, zero, make_masks, products, finish = attn_consts(nc, start, cst, a, banks, NH)
        mem["pad_zero"] = pad_zero
        mem["stored"], mem["out"] = stored, out.rearrange("b (n p) d -> p (b n) d", p=P)
        with nc.Block() as block:
            @block.vector
            def _(ve):
                zero(ve)

            @block.sync
            def _(sp):
                sp.dma_start(X[:], x.rearrange("b (n p) d -> p (b n) d", p=P)).then_inc(x_in, 16)
                sp.wait_ge(x_in, 16)

            @block.scalar
            def _(act):
                act.dma_start(b1rows[:], a["L0_ffn_b1"].rearrange("e (j f) -> (e j) f", f=P)).then_inc(small_in, 16)
                act.dma_start(cst["gw"][:], a["L0_ffn_gate_w"]).then_inc(small_in, 16)
                act.dma_start(cst["gb"][:], a["L0_ffn_gate_b"].partition_broadcast(P)).then_inc(small_in, 16)
                act.wait_ge(consts, 3)
                for i in range(2):
                    act.dma_start(xsort[i].rearrange("(t p) d -> p t d", p=P), pad[:]).then_inc(pad_zero, 16)
                act.wait_ge(b1_psum, 1)
                act.activation(b1T[:].rearrange("p e j -> p (e j)"), banks[7][:, 0:NE * FC], ACT.Copy)

            @block.gpsimd
            def _(gp):
                gp.memset(cst["ident"][:], 0.0).then_inc(pool_step, 1)
                gp.memset(pad[:], 0.0).then_inc(pool_step, 1)
                gp.memset(cst["ones"][:], 1.0).then_inc(pool_step, 1)
                gp.iota(cst["falling"][:], [[-1, NE]], base=NE, channel_multiplier=0, allow_small_or_imprecise_dtypes=True)
                gp.iota(cst["tilestart"][:], [[P, NT]], base=0, channel_multiplier=0, allow_small_or_imprecise_dtypes=True)
                gp.iota(cst["tileno"][:], [[1, MAXT]], base=0, channel_multiplier=0, allow_small_or_imprecise_dtypes=True)
                gp.wait_ge(pool_step, 3)
                gp.affine_select(out=cst["ident"][:], in_=cst["ident"][:], compare_op=ALU.not_equal, fill=1.0,
                                 base=0, pattern=[[-1, P]], channel_multiplier=1).then_inc(consts, 1)
                gp.iota(pad[:, :, D], [[P, MAXT]], base=NT * P, channel_multiplier=1, allow_small_or_imprecise_dtypes=True).then_inc(consts, 1)
                gp.affine_select(out=cst["before"][:], in_=cst["ones"][:], compare_op=ALU.is_gt, fill=0.0,
                                 base=0, pattern=[[1, P]], channel_multiplier=-1).then_inc(consts, 1)

            @block.tensor
            def _(pe):
                pe.wait_ge(small_in, 48)
                pe.wait_ge(consts, 3)
                pe.transpose(banks[7][:, 0:NE * FC], b1rows[:], cst["ident"][0:NE * FC, 0:NE * FC]).then_inc(b1_psum, 1)

        moe_ffn(nc, 0, cst, mem, banks, NT, NE, F, load, make_masks, products, finish)
        start.close()
        with ExitStack() as attn:
            PAD = a["L0_attn_fir_l"].shape[2] - 1

            def ab(name, shape):
                mem[name] = attn.enter_context(nc.sbuf_tensor(name, shape, F32))
            ab("VP", [P, B, PAD + L])
            for name in ("FS", "FL"):
                ab(name, [P, B, L])
            for name in ("V", "DEL"):
                ab(name, [P, NT, P])
            with ExitStack() as delta:
                def db(name, shape):
                    mem[name] = delta.enter_context(nc.sbuf_tensor(name, shape, F32))
                for name in ("QT", "KT", "KBT"):
                    db(name, [P, NT * P])
                for name in ("K", "KB", "VB"):
                    db(name, [P, NT, P])
                attn_project(nc, cst, mem, banks, B, L, NH)
                attn_delta(nc, cst, mem, banks, B, L, NH)
            attn_mix(nc, cst, mem, banks, B, L, NH)
        moe_ffn(nc, 1, cst, mem, banks, NT, NE, F)


_INS = ['L0_attn_x', 'L0_attn_Wq', 'L0_attn_Wk', 'L0_attn_Wv', 'L0_attn_Wb', 'L0_attn_qc_w', 'L0_attn_kc_w',
        'L0_attn_vc_w', 'L0_attn_fir_s', 'L0_attn_fir_l', 'L0_attn_gW1', 'L0_attn_gb1', 'L0_attn_gW2', 'L0_attn_gb2',
        'L0_attn_temp', 'L0_attn_eps_floor', 'L0_attn_onorm_w', 'L0_attn_Wo', 'L0_ffn_gate_w', 'L0_ffn_gate_b',
        'L0_ffn_w1', 'L0_ffn_b1', 'L0_ffn_w2', 'L0_ffn_b2']


def kernel(**inputs):
    import numpy as np
    import concourse.bacc as bacc
    from concourse.bass_utils import run_bass_kernel_spmd as run

    nc = bacc.Bacc("TRN2", target_bir_lowering=False, num_devices=1)
    arrays, aps = {}, {}
    for name in _INS:
        v = np.ascontiguousarray(inputs[name])
        arrays["in_" + name] = v
        aps[name] = nc.dram_tensor("in_" + name, v.shape, mybir.dt.from_np(v.dtype), kind="ExternalInput").ap()
    aps["out"] = nc.dram_tensor("out_0", inputs['L0_attn_x'].shape, F32, kind="ExternalOutput").ap()
    program(nc, aps)
    r = run(nc, [arrays], core_ids=[0])
    return r.results[0]["out_0"]
```
